# Optimizing a Trainium2 kernel written in Bass

```python
import numpy as np
import jax
import jax.numpy as jnp

def _softmax(x, axis=-1):
    return jax.nn.softmax(x, axis=axis)

def _gelu(x):
    return jax.nn.gelu(x, approximate=True)

def _silu(x):
    return jax.nn.silu(x)

def _sigmoid(x):
    return jax.nn.sigmoid(x)

def _layernorm(x, axis=-1, eps=1e-05):
    m = jnp.mean(x, axis=axis, keepdims=True)
    v = jnp.var(x, axis=axis, keepdims=True)
    return (x - m) / jnp.sqrt(v + eps)

def _scatter_add(tgt, idx, src, axis=0):
    return tgt.at[idx].add(src)

def _segment_sum(src, seg, n):
    return jax.ops.segment_sum(src, seg, n)
kernel_name = 'mk_decoder_preln_d1_seqx_r2_6f6434'

def setup_inputs(seed: int=0):
    np.random.seed(seed)
    _w = jnp.asarray

    def _rec_inputs():
        import jax
        import jax.numpy as jnp
        _rk = jax.random.key(seed)
        x = 7.22e-05 + 1 * jax.random.normal(jax.random.fold_in(_rk, 1), (2, 2048, 512), jnp.float32)
        _lenS = 2048 - jax.random.randint(jax.random.fold_in(_rk, 7), (2,), 0, max(1, 2048 // 4) + 1, jnp.int32)
        _lenS2 = 128 - jax.random.randint(jax.random.fold_in(_rk, 8), (2,), 0, max(1, 128 // 4) + 1, jnp.int32)
        _ctx_1024P = jax.random.normal(jax.random.fold_in(_rk, 11), (2, 16, 512), jnp.float32)
        _ctx_1024c = jax.random.dirichlet(jax.random.fold_in(_rk, 511), 0.3 * jnp.ones((16,), jnp.float32), (2, 128))
        _ctx_1024t = jnp.einsum('bsk,bkd->bsd', _ctx_1024c, _ctx_1024P)
        _ctx_1024t = _ctx_1024t * jax.lax.rsqrt(jnp.mean(jnp.square(_ctx_1024t)) + 1e-12) * 0.953939
        ctx_1024 = 4.13588e-05 + 0.999923 * (_ctx_1024t + 0.3 * jax.random.normal(jax.random.fold_in(_rk, 611), (2, 128, 512), jnp.float32))
        return (x, ctx_1024)
    x, ctx_1024 = _rec_inputs()

    def _L0_attn_setup():
        import jax, jax.numpy as jnp
        import numpy as np
        EPS = 1e-12

        def _l2norm(t, axis=-1):
            return t / jnp.maximum(jnp.linalg.norm(t, axis=axis, keepdims=True), EPS)

        def _selective_scan(u, delta, A, Bm, Cm, D):
            uT = u.transpose(2, 0, 1)
            dT = delta.transpose(2, 0, 1)
            BT = Bm.transpose(2, 0, 1)
            CT = Cm.transpose(2, 0, 1)
            h0 = jnp.zeros(u.shape[:2] + (A.shape[1],), u.dtype)

            def step(h, inp):
                u_t, d_t, b_t, c_t = inp
                dA = jnp.exp(d_t[..., None] * A)
                h = dA * h + (d_t * u_t)[..., None] * b_t[:, None, :]
                y = jnp.einsum('bdn,bn->bd', h, c_t)
                return (h, y)
            _, ys = jax.lax.scan(step, h0, (uT, dT, BT, CT))
            y = ys.transpose(1, 2, 0)
            return y + D[None, :, None] * u
        key = jax.random.key(seed)
        ks = jax.random.split(key, 8)
        B, N, d_inner, d_state, dt_rank, K = (8, 1024, 512, 16, 32, 8)
        x = jax.random.normal(ks[0], (B, N, d_inner), jnp.float32)
        means = jax.random.normal(ks[1], (K, d_inner), jnp.float32)
        prompt_weight = jax.random.normal(ks[2], (d_state, d_inner), jnp.float32) * d_inner ** (-0.5)
        x_proj_weight = jax.random.normal(ks[3], (dt_rank + 2 * d_state, d_inner), jnp.float32) * d_inner ** (-0.5)
        dt_init_std = dt_rank ** (-0.5)
        dt_projs_weight = jax.random.uniform(ks[4], (d_inner, dt_rank), jnp.float32, -dt_init_std, dt_init_std)
        dt = jnp.exp(jax.random.uniform(ks[5], (d_inner,), jnp.float32) * (np.log(0.1) - np.log(0.001)) + np.log(0.001))
        dt = jnp.clip(dt, 0.0001, None)
        dt_projs_bias = dt + jnp.log(-jnp.expm1(-dt))
        A_logs = jnp.log(jnp.broadcast_to(jnp.arange(1, d_state + 1, dtype=jnp.float32), (d_inner, d_state)))
        Ds = jnp.ones((d_inner,), jnp.float32)
        return {'x': x, 'means': means, 'prompt_weight': prompt_weight, 'x_proj_weight': x_proj_weight, 'dt_projs_weight': dt_projs_weight, 'dt_projs_bias': dt_projs_bias, 'A_logs': A_logs, 'Ds': Ds}
    _L0_attn_all = _L0_attn_setup()
    _L0_attn_in = {k: v for k, v in _L0_attn_all.items() if k in ('means', 'prompt_weight', 'x_proj_weight', 'dt_projs_weight', 'dt_projs_bias', 'A_logs', 'Ds')}
    del _L0_attn_all

    def _L0_xattn_setup():
        import jax, jax.numpy as jnp
        import numpy as np
        C = 512
        B, SQ, SKV = (4, 1024, 1024)
        key = jax.random.key(seed)
        ks = jax.random.split(key, 10)
        s = 1.0 / np.sqrt(C)
        return {'x': jax.random.normal(ks[0], (B, SQ, C), jnp.float32), 'content_embeddings': jax.random.normal(ks[1], (B, SKV, C), jnp.float32), 'Wq': jax.random.normal(ks[2], (C, C), jnp.float32) * s, 'bq': jnp.zeros((C,), jnp.float32), 'Wk': jax.random.normal(ks[3], (C, C), jnp.float32) * s, 'bk': jnp.zeros((C,), jnp.float32), 'Wv': jax.random.normal(ks[4], (C, C), jnp.float32) * s, 'bv': jnp.zeros((C,), jnp.float32), 'Wo': jax.random.normal(ks[5], (C, C), jnp.float32) * s, 'bo': jnp.zeros((C,), jnp.float32)}
    _L0_xattn_all = _L0_xattn_setup()
    _L0_xattn_in = {k: v for k, v in _L0_xattn_all.items() if k in ('Wq', 'bq', 'Wk', 'bk', 'Wv', 'bv', 'Wo', 'bo')}
    del _L0_xattn_all

    def _L0_ffn_setup():
        import jax, jax.numpy as jnp
        import numpy as np
        D_MODEL = 512
        D_FF = 2048
        NUM_EXPERTS = 8
        B, N = (16, 512)
        key = jax.random.key(seed)
        ks = jax.random.split(key, 7)
        s_in = 1.0 / np.sqrt(D_MODEL)
        s_ff = 1.0 / np.sqrt(D_FF)
        return {'x': jax.random.normal(ks[0], (B, N, D_MODEL), dtype=jnp.float32), 'Wr': jax.random.uniform(ks[1], (D_MODEL, NUM_EXPERTS), jnp.float32, -s_in, s_in), 'br': jax.random.uniform(ks[2], (NUM_EXPERTS,), jnp.float32, -s_in, s_in), 'W1': jax.random.uniform(ks[3], (NUM_EXPERTS, D_MODEL, D_FF), jnp.float32, -s_in, s_in), 'b1': jax.random.uniform(ks[4], (NUM_EXPERTS, D_FF), jnp.float32, -s_in, s_in), 'W2': jax.random.uniform(ks[5], (NUM_EXPERTS, D_FF, D_MODEL), jnp.float32, -s_ff, s_ff), 'b2': jax.random.uniform(ks[6], (NUM_EXPERTS, D_MODEL), jnp.float32, -s_ff, s_ff)}
    _L0_ffn_all = _L0_ffn_setup()
    _L0_ffn_in = {k: v for k, v in _L0_ffn_all.items() if k in ('Wr', 'br', 'W1', 'b1', 'W2', 'b2')}
    del _L0_ffn_all
    return {'x': x, 'ctx_1024': ctx_1024, 'L0_attn_means': _L0_attn_in['means'], 'L0_attn_prompt_weight': _L0_attn_in['prompt_weight'], 'L0_attn_x_proj_weight': _L0_attn_in['x_proj_weight'], 'L0_attn_dt_projs_weight': _L0_attn_in['dt_projs_weight'], 'L0_attn_dt_projs_bias': _L0_attn_in['dt_projs_bias'], 'L0_attn_A_logs': _L0_attn_in['A_logs'], 'L0_attn_Ds': _L0_attn_in['Ds'], 'L0_xattn_Wq': _L0_xattn_in['Wq'], 'L0_xattn_bq': _L0_xattn_in['bq'], 'L0_xattn_Wk': _L0_xattn_in['Wk'], 'L0_xattn_bk': _L0_xattn_in['bk'], 'L0_xattn_Wv': _L0_xattn_in['Wv'], 'L0_xattn_bv': _L0_xattn_in['bv'], 'L0_xattn_Wo': _L0_xattn_in['Wo'], 'L0_xattn_bo': _L0_xattn_in['bo'], 'L0_ffn_Wr': _L0_ffn_in['Wr'], 'L0_ffn_br': _L0_ffn_in['br'], 'L0_ffn_W1': _L0_ffn_in['W1'], 'L0_ffn_b1': _L0_ffn_in['b1'], 'L0_ffn_W2': _L0_ffn_in['W2'], 'L0_ffn_b2': _L0_ffn_in['b2']}

def reference(x, ctx_1024, L0_attn_means, L0_attn_prompt_weight, L0_attn_x_proj_weight, L0_attn_dt_projs_weight, L0_attn_dt_projs_bias, L0_attn_A_logs, L0_attn_Ds, L0_xattn_Wq, L0_xattn_bq, L0_xattn_Wk, L0_xattn_bk, L0_xattn_Wv, L0_xattn_bv, L0_xattn_Wo, L0_xattn_bo, L0_ffn_Wr, L0_ffn_br, L0_ffn_W1, L0_ffn_b1, L0_ffn_W2, L0_ffn_b2):
    import jax
    import jax.numpy as jnp

    def _L0_attn_ref(x, means, prompt_weight, x_proj_weight, dt_projs_weight, dt_projs_bias, A_logs, Ds):
        import jax, jax.numpy as jnp
        import numpy as np
        EPS = 1e-12

        def _l2norm(t, axis=-1):
            return t / jnp.maximum(jnp.linalg.norm(t, axis=axis, keepdims=True), EPS)

        def _selective_scan(u, delta, A, Bm, Cm, D):
            uT = u.transpose(2, 0, 1)
            dT = delta.transpose(2, 0, 1)
            BT = Bm.transpose(2, 0, 1)
            CT = Cm.transpose(2, 0, 1)
            h0 = jnp.zeros(u.shape[:2] + (A.shape[1],), u.dtype)

            def step(h, inp):
                u_t, d_t, b_t, c_t = inp
                dA = jnp.exp(d_t[..., None] * A)
                h = dA * h + (d_t * u_t)[..., None] * b_t[:, None, :]
                y = jnp.einsum('bdn,bn->bd', h, c_t)
                return (h, y)
            _, ys = jax.lax.scan(step, h0, (uT, dT, BT, CT))
            y = ys.transpose(1, 2, 0)
            return y + D[None, :, None] * u
        dt_rank = dt_projs_weight.shape[1]
        d_state = A_logs.shape[1]
        scores = jnp.einsum('bnd,kd->bnk', _l2norm(x), _l2norm(means))
        buckets = jnp.argmax(jax.lax.stop_gradient(scores), axis=-1)
        sort_idx = jnp.argsort(buckets, axis=-1, stable=True)
        inv_idx = jnp.argsort(sort_idx, axis=-1)
        xs = jnp.take_along_axis(x, sort_idx[..., None], axis=1)
        b_sorted = jnp.take_along_axis(buckets, sort_idx, axis=1)
        cluster_prompts = means @ prompt_weight.T
        prompt = cluster_prompts[b_sorted]
        u = xs.transpose(0, 2, 1)
        x_dbl = jnp.einsum('bdl,cd->bcl', u, x_proj_weight)
        dts = x_dbl[:, :dt_rank]
        Bm = x_dbl[:, dt_rank:dt_rank + d_state]
        Cm = x_dbl[:, dt_rank + d_state:] + prompt.transpose(0, 2, 1)
        delta = jax.nn.softplus(jnp.einsum('brl,dr->bdl', dts, dt_projs_weight) + dt_projs_bias[None, :, None])
        A = -jnp.exp(A_logs)
        y = _selective_scan(u, delta, A, Bm, Cm, Ds)
        y = y.transpose(0, 2, 1)
        out = jnp.take_along_axis(y, inv_idx[..., None], axis=1)
        return out

    def _L0_xattn_ref(x, content_embeddings, Wq, bq, Wk, bk, Wv, bv, Wo, bo):
        import jax, jax.numpy as jnp
        import numpy as np
        C = 512
        B, SQ, SKV = (4, 1024, 1024)
        queries = x @ Wq.T + bq
        keys = content_embeddings @ Wk.T + bk
        values = content_embeddings @ Wv.T + bv
        scale = 1.0 / jnp.sqrt(jnp.asarray(C, x.dtype))
        scores = jnp.einsum('bqc,bkc->bqk', queries, keys) * scale
        attn = jax.nn.softmax(scores, axis=-1)
        attended = jnp.einsum('bqk,bkc->bqc', attn, values)
        out = x + attended
        return out @ Wo.T + bo

    def _L0_ffn_ref(x, Wr, br, W1, b1, W2, b2):
        import jax, jax.numpy as jnp
        import numpy as np
        D_MODEL = 512
        D_FF = 2048
        NUM_EXPERTS = 8
        B, N = (16, 512)
        scores = jnp.einsum('bh,he->be', x.mean(axis=1), Wr) + br
        top1 = jnp.argmax(scores, axis=-1)
        w1 = W1[top1]
        c1 = b1[top1]
        w2 = W2[top1]
        c2 = b2[top1]
        h = jax.nn.relu(jnp.einsum('bnh,bhf->bnf', x, w1) + c1[:, None, :])
        out = jnp.einsum('bnf,bfh->bnh', h, w2) + c2[:, None, :]
        return out
    x = x + _L0_attn_ref(_layernorm(x, axis=-1), L0_attn_means, L0_attn_prompt_weight, L0_attn_x_proj_weight, L0_attn_dt_projs_weight, L0_attn_dt_projs_bias, L0_attn_A_logs, L0_attn_Ds)
    x = x + _L0_xattn_ref(_layernorm(x, axis=-1), ctx_1024, L0_xattn_Wq, L0_xattn_bq, L0_xattn_Wk, L0_xattn_bk, L0_xattn_Wv, L0_xattn_bv, L0_xattn_Wo, L0_xattn_bo)
    x = x + _L0_ffn_ref(_layernorm(x, axis=-1), L0_ffn_Wr, L0_ffn_br, L0_ffn_W1, L0_ffn_b1, L0_ffn_W2, L0_ffn_b2)
    return x

_drawn_inputs = setup_inputs


def setup_inputs(seed=0):
    import zlib

    import numpy as np

    out = dict(_drawn_inputs(seed))
    spreads = {'L0_attn_Ds': (1.0, 0.2),
     'L0_xattn_bq': (0.0, 0.699),
     'L0_xattn_bk': (0.0, 0.8),
     'L0_xattn_bv': (0.0, 0.1),
     'L0_xattn_bo': (0.0, 0.1)}
    factors = {'L0_ffn_b1': 8.0, 'L0_ffn_b2': 8.0}
    for name, (base, spread) in spreads.items():
        noise = np.random.default_rng([zlib.crc32(name.encode()), seed]).standard_normal(out[name].shape)
        drawn = base * np.exp(spread * noise) if base else spread * noise
        out[name] = jnp.asarray(drawn.astype(out[name].dtype))
    for name, factor in factors.items():
        out[name] = (out[name] * factor).astype(out[name].dtype)
    return out
```

```python
from contextlib import ExitStack

import numpy as np
import concourse.bass as bass
from concourse import mybir

F32 = mybir.dt.float32
I32 = mybir.dt.int32
U32 = mybir.dt.uint32
ALU = mybir.AluOpType
ACT = mybir.ActivationFunctionType
AX = mybir.AxisListType

P = 128
B, S, D = 2, 2048, 512
KT = D // P
NS, R = 16, 32
NB = 8
NE, FF = 8, 2048
FT = FF // P
KEYS = 128
LC = 256
SUB = LC // P
CB = S // LC
NC = B * CB
TB = S // P
ROW = D + 1 + NB
XC0, XB0 = 32, 64
XW = XB0 + NS
BG = 4
NG = NS // BG
EPS = 1e-5
SCALE = D ** -0.5

SETUP_USES = ["mhat", "prompt"] + [f"{n}{b}" for b in range(B) for n in ("keysT", "foldedq", "biasq", "valuesT", "foldedo")]
POST_USES = ["xn2T0", "xn2T1", "scores", "probsT", "out0", "out1", "xn3T0", "xn3T1"]
PREP_USES = ["uT0", "uT1", "onehot", "proj", "C0", "C1", "delta0", "delta1"]
AT = {"xn2T": 2, "scores": 3, "expo": 5, "probsT": 7, "out": 8, "xn3T": 12,
      "uT": 5, "proj": 6, "delta": 7, "soft": 8}
AT_DVE = {"norm2": 0, "max": 4, "normal": 6, "norm3": 10, "norm1": 3, "abs": 8, "softplus": 9, "choose": 14}
AT_POOL = {"x2": 9, "acc": 5, "du": 10}
NORMS = ("norm1", "norm2", "norm3")
STEP_USES = {"xn2T": POST_USES[0:2], "scores": POST_USES[2:3], "probsT": POST_USES[3:4], "out": POST_USES[4:6],
             "xn3T": POST_USES[6:8], "uT": PREP_USES[0:3], "proj": PREP_USES[3:4], "delta": PREP_USES[4:8]}
POST_STEPS, PREP_STEPS = ("xn2T", "scores", "expo", "probsT", "out", "xn3T"), ("uT", "proj", "delta", "soft")


def steps_at(n, prep, post):
    return [s for s in POST_STEPS + PREP_STEPS if AT[s] == n and (post if s in POST_STEPS else prep)]


def uses(prep, post, ffn):
    out = []
    for n in range(NS):
        out += [f"hidden{n}"] if ffn else []
        for s in steps_at(n, prep, post):
            out += STEP_USES.get(s, [])
    return out


def build(nc, t):
    with ExitStack() as ctx:
        def sb(name, shape, dt=F32):
            return ctx.enter_context(nc.sbuf_tensor(name, shape, dt))

        def ps(name, shape):
            return ctx.enter_context(nc.psum_tensor(name, shape, F32))

        def sem(name):
            return ctx.enter_context(nc.semaphore(name))

        def dram(name, shape, dt=F32):
            return nc.dram_tensor(name, shape, dt, kind="Internal").ap()

        xsorted = dram("xsorted", (B * S, ROW))
        b_rows = dram("b_rows", (NC, NS, LC))
        x2_dram = dram("x2_dram", (NC, P, SUB * D))
        x3_dram = dram("x3_dram", (NC, P, KT * LC))

        big = sb("big", [P, B * TB * ROW])
        rows = big[:].rearrange("p (b t r) -> p b t r", b=B, t=TB)
        w1 = big[:, 0:KT * FF].rearrange("p (k f) -> p k f", k=KT)
        w2 = big[:, KT * FF:KT * FF + FT * D].rearrange("p (f d) -> p f d", f=FT)

        ident = sb("ident", [P, P])
        ones = sb("ones", [P, P])
        before = sb("before", [P, P])
        rank8 = sb("rank8", [P, TB, NB])
        means = sb("means", [NB, D])
        meansT = sb("meansT", [P, KT, NB])
        mhat = sb("mhat", [NB, D])
        mhatT = sb("mhatT", [P, KT, NB])
        msq = sb("msq", [NB, 4])
        promptT = sb("promptT", [P, KT, NS])
        prompt = sb("prompt", [NB, XW])
        wx = sb("wx", [P, KT, XW])
        wdt = sb("wdt", [R, D])
        bdt = sb("bdt", [P, KT])
        A = sb("A", [P, KT, NS])
        Dbc = sb("Dbc", [P, D])
        wo = sb("wo", [P, KT, D])
        bqkv = sb("bqkv", [P, 3, KT])
        bo = sb("bo", [1, D])
        wr = sb("wr", [P, KT, NE])
        br = sb("br", [1, NE])
        foldedq = sb("foldedq", [P, B, KT, KEYS])
        biasq = sb("biasq", [1, B, KEYS])
        foldedo = sb("foldedo", [P, B, D])

        xs = sb("xs", [P, SUB, ROW])
        xn = sb("xn", [P, SUB, D])
        half = sb("half", [P, SUB + 1])
        st = sb("st", [P, 3, SUB, 6])
        mv = sb("mv", [P, 3, SUB, 2])
        rstd = sb("rstd", [P, 3, SUB])
        u = sb("u", [P, 2, KT, LC])
        dlt = sb("dlt", [P, 2, KT, LC])
        soft_e = sb("soft_e", [P, KT, LC])
        soft_l = sb("soft_l", [P, KT, LC])
        acc = sb("acc", [P, 4, SUB, D])
        onehot = sb("onehot", [NB, LC])
        proj = sb("proj", [XW, LC])
        Cl = sb("Cl", [P, 2, SUB, NS])
        Bs = sb("Bs", [P, 2, BG, LC])
        dBu = sb("dBu", [P, 2, KT, LC])
        h = sb("h", [P, 2, KT, LC])
        carry = sb("carry", [P, NS, KT])
        ids = sb("ids", [P, NC * SUB], U32)
        ids_now = sb("ids_now", [P, SUB], U32)

        xn23 = sb("xn23", [P, SUB, D])
        xnT = sb("xnT", [P, KT, LC])
        prob = sb("prob", [P, SUB, KEYS])
        pstat = sb("pstat", [P, 4, SUB])
        probT = sb("probT", [P, SUB * P])
        outs = sb("outs", [P, SUB, D])
        msum = sb("msum", [P, NC, KT])

        x3 = sb("x3", [P, 2, KT, LC])
        x2 = sb("x2", [P, SUB, D])
        res = sb("res", [P, SUB, D])
        hid = sb("hid", [P, 3, LC])
        b1 = sb("b1", [P, FT])
        b2 = sb("b2", [P, D])
        mean = sb("mean", [P, KT])
        vote = sb("vote", [1, 4, NE])
        expert = sb("expert", [1, 4], I32)

        wq = acc[:].rearrange("p a s d -> p (a s) d")[:, 0:KT, :]
        wk = acc[:].rearrange("p a s d -> p (a s) d")[:, KT:2 * KT, :]
        wv = u[:].rearrange("p a k l -> p (a k l)").rearrange("p (k d) -> p k d", k=KT)
        ctxT = x3[:].rearrange("p a k l -> p (a k l)").rearrange("p (b k n) -> p b k n", b=2 * B, k=KT)
        keysT = dlt[:, 0].rearrange("p k l -> p (k l)").rearrange("p (b k n) -> p b k n", b=B, k=KT)
        valuesT = dlt[:, 1].rearrange("p k l -> p (k l)").rearrange("p (b k n) -> p b k n", b=B, k=KT)
        rawT = dBu[:].rearrange("p a k l -> p (a k l)").rearrange("p (a k n) -> p a k n", a=4, k=KT)
        rt = [h[:].rearrange("p a k l -> p (a k l)")[:, i * P:(i + 1) * P] for i in range(10)]
        pos = sb("pos", [P, B, TB], U32)

        dA = ps("dA", [P, 2, 2 * LC])
        hT = ps("hT", [P, 2, D])
        work = ps("work", [P, 2, 512])
        fo = ps("fo", [P, 2, D])

        weights_in, x_in = sem("weights_in"), [sem(f"x_in{b}") for b in range(B)]
        consts_ready = sem("consts_ready")
        root_ready = sem("root_ready")
        var_ready = [sem(f"var{i}_ready") for i in (1, 2, 3)]
        rstd_ready = [sem(f"rstd{i}_ready") for i in (1, 2, 3)]
        mhat_link, mhat_ready = sem("mhat_link"), sem("mhat_ready")
        filled, evacuated = sem("filled"), sem("evacuated")
        a_link = sem("a_link")
        scored = sem("scored")
        route_link, onehot_ready, counted = sem("route_link"), sem("onehot_ready"), sem("counted")
        pos_ready, tagged, sorted_out = sem("pos_ready"), sem("tagged"), sem("sorted_out")
        xs_in = sem("xs_in")
        norm_link = [sem(f"norm{i}_link") for i in (1, 2, 3)]
        xn_ready, xn2_ready, xn3_ready = sem("xn_ready"), sem("xn2_ready"), sem("xn3_ready")
        acc_link, acc_ready = sem("acc_link"), sem("acc_ready")
        abs_ready, e_ready, ln_ready = sem("abs_ready"), sem("e_ready"), sem("ln_ready")
        soft_link, dlt_ready, du_ready = sem("soft_link"), sem("dlt_ready"), sem("du_ready")
        b_stored, b_in = sem("b_stored"), [sem(f"b_in{i}") for i in range(2)]
        dA_ready, dBu_ready, scanned = sem("dA_ready"), sem("dBu_ready"), sem("scanned")
        hT_ready, hT_used, carried = sem("hT_ready"), sem("hT_used"), sem("carried")
        carry_zeroed = sem("carry_zeroed")
        smax_ready, expo_ready, soft_sum, probs_ready = sem("smax_ready"), sem("expo_ready"), sem("soft_sum"), sem("probs_ready")
        smax_link = sem("smax_link")
        x2_ready, x2_stored, x3_stored = sem("x2_ready"), sem("x2_stored"), sem("x3_stored")
        mean_link, mean_ready, voted = sem("mean_link"), sem("mean_ready"), sem("voted")
        vote_link, expert_ready = sem("vote_link"), sem("expert_ready")
        w_in = sem("w_in")
        x3_in, x2_in, x2_biased = sem("x3_in"), sem("x2_in"), sem("x2_biased")
        ffn_ready, res_ready = sem("ffn_ready"), sem("res_ready")
        ids_link, ids_ready, out_stored = sem("ids_link"), sem("ids_ready"), sem("out_stored")

        def wait(eng, s, value):
            if not isinstance(value, int) or value > 0:
                eng.wait_ge(s, value)

        def settle(eng, value):
            if not isinstance(value, int):
                eng.nop(nofuse=True)

        order = list(SETUP_USES) + [f"raw{b}_{i}" for b in range(B) for i in range(TB)]
        at_prep0 = len(order)
        at_it0 = at_prep0 + len(PREP_USES)
        assert all(x % 2 == 0 for x in (at_prep0, at_it0, len(POST_USES), FT))

        class Uses:
            def __init__(self, base, names):
                self.base, self.names = base, names

            def bank(self, name):
                return work[:, self.names.index(name) % 2]

            def fill(self, pe, name):
                wait(pe, evacuated, self.base + (self.names.index(name) - 1))
                return self.bank(name)

            def read(self, act, name):
                act.wait_ge(filled, self.base + (self.names.index(name) + 1))
                settle(act, self.base)
                return self.bank(name)

            def done(self, eng, name):
                eng.wait_ge(evacuated, self.base + (self.names.index(name) + 1))

        setup_uses = Uses(0, order)
        prep0_uses = Uses(at_prep0, PREP_USES)
        STRETCH = [((0, 1), True, False, False), ((1, 2), True, True, False), ((2, CB), True, True, False),
                   ((CB, CB + 1), True, True, False), ((CB + 1, CB + 2), True, True, True),
                   ((CB + 2, NC - 1), True, True, True), ((NC - 1, NC), False, True, True)]

        def base_of(c, k):
            at = at_it0
            for (lo, hi), prep, post, ffn in STRETCH[:k]:
                at += (hi - lo) * len(uses(prep, post, ffn))
            (lo, _), prep, post, ffn = STRETCH[k]
            return at + (c - lo) * len(uses(prep, post, ffn))

        def stretches(eng, body):
            for k, ((lo, hi), prep, post, ffn) in enumerate(STRETCH):
                names = uses(prep, post, ffn)
                if hi - lo == 1:
                    body(lo, Uses(base_of(lo, k), names), prep, post, ffn)
                else:
                    with eng.Fori(lo, hi) as c:
                        body(c, Uses(base_of(c, k), names), prep, post, ffn)

        at_tail = base_of(NC, len(STRETCH) - 1)
        tail_uses = Uses(at_tail, uses(False, True, True))
        at_ffn = at_tail + len(tail_uses.names)

        block = ctx.enter_context(nc.Block())

        @block.sync
        def _(sp):
            def load(dst, src, s=weights_in):
                sp.dma_start(dst, src).then_inc(s, 16)

            load(means[:], t["means"])
            load(meansT[:], t["meansT"].rearrange("(k p) n -> p k n", p=P))
            for b in range(B):
                for i in range(4):
                    n = TB // 4
                    sp.dma_start(rows[:, b, i * n:(i + 1) * n, 0:D],
                                 t["x"][b, i * n * P:(i + 1) * n * P, :].rearrange("(t p) d -> p t d", p=P)
                                 ).then_inc(x_in[b], 16)
                if b == 0:
                    load(promptT[:], t["promptT"].rearrange("(k p) n -> p k n", p=P))
                    load(wx[:], t["wx"].rearrange("(k p) n -> p k n", p=P))
                    load(wdt[:], t["wdt"])
                    load(bdt[:], t["bdt"])
                    load(A[:], t["A_logs"].rearrange("(k p) n -> p k n", p=P))
                    load(Dbc[:], t["Ds"].rearrange("(o d) -> o d", o=1).to_broadcast([P, D]))
                    load(wo[:], t["WoT"].rearrange("(k p) n -> p k n", p=P))
                    load(wq, t["Wq"].rearrange("(k p) n -> p k n", p=P))
                    load(wk, t["WkT"].rearrange("(k p) n -> p k n", p=P))
                    load(wv, t["WvT"].rearrange("(k p) n -> p k n", p=P))
                    for i, n in enumerate(("bq", "bk", "bv")):
                        load(bqkv[:, i, :], t[n])
                    load(bo[:], t["bo"].rearrange("(o d) -> o d", o=1))
                    load(wr[:], t["Wr"].rearrange("(k p) n -> p k n", p=P))
                    load(br[:], t["br"].rearrange("(o d) -> o d", o=1))
                    for b2_ in range(B):
                        load(ctxT[:, b2_], t["ctxT"][b2_].rearrange("(k p) n -> p k n", p=P))

            def load_xs(c):
                if not isinstance(c, int) or c > 0:
                    sp.wait_ge(dlt_ready, c)
                    sp.wait_ge(acc_ready, c)
                sp.dma_start(xs[:], xsorted.rearrange("(c s p) r -> c p s r", s=SUB, p=P)[c]).then_inc(xs_in, 16)

            def store_b(c, us):
                us.done(sp, "proj")
                sp.dma_start(b_rows[c], proj[XB0:XB0 + NS, :]).then_inc(b_stored, 16)
                sp.wait_ge(b_stored, 16 * (c + 1))

            def load_b(c, g):
                wait(sp, dBu_ready, NS * c + BG * (g - 1))
                sp.dma_start(Bs[:, g % 2],
                             b_rows[c, g * BG:(g + 1) * BG, :].rearrange("(o n) l -> o n l", o=1).to_broadcast([P, BG, LC])
                             ).then_inc(b_in[g % 2], 16)

            def load_w(b):
                sp.wait_ge(expert_ready, b + 1)
                if b > 0:
                    sp.wait_ge(ffn_ready, b * CB)
                    sp.wait_ge(x2_biased, b * CB)
                e = sp.value_load(expert[0:1, 0:1], min_val=0, max_val=NE - 1)
                for k in range(KT):
                    sp.dma_start(w1[:, k, :], t["W1"][e].rearrange("(k p) f -> k p f", p=P)[k]).then_inc(w_in, 16)
                for k in range(4):
                    n = FT // 4
                    sp.dma_start(w2[:, k * n:(k + 1) * n, :],
                                 t["W2"][e].rearrange("(k n p) f -> k p n f", p=P, n=n)[k]).then_inc(w_in, 16)
                sp.dma_start(b1[:], t["b1"][e]).then_inc(w_in, 16)
                sp.dma_start(b2[:], t["b2"][e].rearrange("(o d) -> o d", o=1).to_broadcast([P, D])).then_inc(w_in, 16)

            def load_x3(q):
                wait(sp, ffn_ready, q - 1)
                wait(sp, x3_in, 16 * q)
                sp.wait_ge(x3_stored, 16 * (q + 1))
                sp.dma_start(x3[:, q % 2], x3_dram[q].rearrange("p (k l) -> p k l", k=KT)).then_inc(x3_in, 16)

            def load_x2(q):
                wait(sp, res_ready, q)
                sp.wait_ge(x2_stored, 16 * (q + 1))
                sp.dma_start(x2[:], x2_dram[q].rearrange("p (s d) -> p s d", s=SUB)).then_inc(x2_in, 16)

            def store_post(c):
                sp.wait_ge(x2_ready, c + 1)
                wait(sp, x2_stored, 16 * c)
                sp.dma_start(x2_dram[c].rearrange("p (s d) -> p s d", s=SUB), acc[:, c % 4]).then_inc(x2_stored, 16)

            def store_x3(c, us):
                us.done(sp, "xn3T1")
                wait(sp, x3_stored, 16 * c)
                sp.dma_start(x3_dram[c].rearrange("p (k l) -> p k l", k=KT), xnT[:]).then_inc(x3_stored, 16)

            sp.wait_ge(sorted_out, 16 * TB * B)
            load_xs(0)
            store_b(0, prep0_uses)
            load_b(0, 0)
            load_b(0, 1)

            def body(c, us, prep, post, ffn):
                if prep:
                    load_xs(c + 1)
                if ffn:
                    load_x2(c - (CB + 1))
                    load_x3(c - CB)
                load_b(c, 2)
                load_b(c, 3)
                if prep:
                    store_b(c + 1, us)
                if post:
                    store_post(c - 1)
                    store_x3(c - 1, us)
                if prep:
                    load_b(c + 1, 0)
                    load_b(c + 1, 1)
                if isinstance(c, int) and c == CB:
                    load_w(0)
                    load_x3(0)
            stretches(sp, body)

            load_x2(CB - 1)
            store_post(NC - 1)
            store_x3(NC - 1, tail_uses)
            load_w(1)
            load_x3(CB)
            with sp.Fori(CB, NC - 1) as q:
                load_x2(q)
                load_x3(q + 1)
            load_x2(NC - 1)
            sp.wait_ge(out_stored, 16 * SUB * NC)

        @block.gpsimd
        def _(pool):
            pool.memset(ident[:], 0.0).then_inc(consts_ready, 1)
            pool.memset(ones[:], 1.0).then_inc(consts_ready, 1)
            pool.memset(before[:], 1.0).then_inc(consts_ready, 1)
            pool.memset(prompt[:], 0.0).then_inc(consts_ready, 1)
            pool.memset(carry[:], 0.0).then_inc(consts_ready, 1)
            pool.memset(half[:, 0:SUB], -0.5).then_inc(consts_ready, 1)
            pool.memset(half[:, SUB:SUB + 1], 0.5).then_inc(consts_ready, 1)
            pool.wait_ge(consts_ready, 7)
            pool.affine_select(out=ident[:], in_=ident[:], compare_op=ALU.not_equal, fill=1.0, base=0,
                               pattern=[[-1, P]], channel_multiplier=1).then_inc(consts_ready, 1)
            pool.affine_select(out=before[:], in_=before[:], compare_op=ALU.is_gt, fill=0.0, base=0,
                               pattern=[[1, P]], channel_multiplier=-1).then_inc(consts_ready, 1)
            pool.iota(rank8[:], pattern=[[0, TB], [-1, NB]], base=NB, channel_multiplier=0,
                      allow_small_or_imprecise_dtypes=True).then_inc(consts_ready, 1)
            for b in range(B):
                tags = rows[:, b, :, D:D + 1].bitcast(I32)
                pool.iota(tags, pattern=[[P, TB], [0, 1]], base=b * S, channel_multiplier=1).then_inc(tagged, 1)
            pool.wait_ge(mhat_link, 2)
            pool.tensor_tensor(msq[:, 1:2], msq[:, 0:1], half[0:NB, SUB:SUB + 1], ALU.pow).then_inc(root_ready, 1)
            for b in range(B):
                pool.wait_ge(pos_ready, b + 1)
                pool.wait_ge(tagged, B)
                pool.wait_ge(x_in[b], 64)
                for i in range(TB):
                    pool.indirect_dma_start(xsorted, bass.IndirectOffsetOnAxis(pos[:, b, i:i + 1], 0),
                                            rows[:, b, i, :], None).then_inc(sorted_out, 16)

            def acc_init(c):
                pool.wait_ge(xn_ready, c + 1)
                pool.wait_ge(xs_in, 16 * (c + 1))
                if not isinstance(c, int) or c > 2:
                    pool.wait_ge(x2_stored, 16 * (c - 2))
                    pool.wait_ge(xn3_ready, c - 2)
                settle(pool, c)
                a = acc[:, c % 4]
                pool.tensor_tensor(a, xn[:], Dbc[:].rearrange("p (o d) -> p o d", o=1).to_broadcast([P, SUB, D]),
                                   ALU.mult).then_inc(acc_link, 1)
                pool.wait_ge(acc_link, c + 1)
                settle(pool, c)
                pool.tensor_copy(ids[:, bass.ds(c * SUB, SUB)], xs[:, :, D:D + 1].bitcast(U32)
                                 .rearrange("p s o -> p (s o)")).then_inc(ids_link, 1)
                pool.tensor_tensor(a, a, xs[:, :, 0:D], ALU.add).then_inc(acc_ready, 1)

            def du(c):
                pool.wait_ge(dlt_ready, c + 1)
                settle(pool, c)
                pool.tensor_tensor(u[:, c % 2], u[:, c % 2], dlt[:, c % 2], ALU.mult).then_inc(du_ready, 1)

            def invert_root(i, c):
                pool.wait_ge(var_ready[i], c + 1)
                pool.tensor_tensor(rstd[:, i, :], rstd[:, i, :], half[:, 0:SUB], ALU.pow).then_inc(rstd_ready[i], 1)

            invert_root(0, 0)
            acc_init(0)
            du(0)

            def bias_x2(q, b):
                pool.wait_ge(w_in, 160 * (b + 1))
                pool.wait_ge(x2_in, 16 * (q + 1))
                pool.tensor_tensor(x2[:], x2[:], b2[:].rearrange("p (o d) -> p o d", o=1).to_broadcast([P, SUB, D]),
                                   ALU.add).then_inc(x2_biased, 1)

            def scatter(q):
                wait(pool, out_stored, 16 * SUB * q)
                pool.wait_ge(ids_link, NC if isinstance(q, int) and q >= CB else q + 1)
                pool.tensor_copy(ids_now[:], ids[:, bass.ds(q * SUB, SUB)]).then_inc(ids_ready, 1)
                pool.wait_ge(ids_ready, q + 1)
                pool.wait_ge(res_ready, q + 1)
                settle(pool, q)
                for s in range(SUB):
                    pool.indirect_dma_start(t["out"].rearrange("b s d -> (b s) d"),
                                            bass.IndirectOffsetOnAxis(ids_now[:, s:s + 1], 0),
                                            res[:, s, :], None).then_inc(out_stored, 16)

            def add_out(c, us):
                us.done(pool, "out1")
                pool.wait_ge(xn2_ready, c + 1)
                settle(pool, c)
                pool.tensor_tensor(acc[:, c % 4], acc[:, c % 4], outs[:], ALU.add).then_inc(x2_ready, 1)

            def body(c, us, prep, post, ffn):
                for n in range(NS):
                    if n % BG == 0:
                        g = n // BG
                        pool.wait_ge(b_in[g % 2], 32 * c + 16 * (g // 2 + 1))
                    if n == 0:
                        pool.wait_ge(du_ready, c + 1)
                    wait(pool, scanned, 2 * NS * c + 2 * (n - 1))
                    settle(pool, c)
                    pool.tensor_tensor(dBu[:, n % 2], u[:, c % 2],
                                       Bs[:, (n // BG) % 2, n % BG, :].rearrange("p (o l) -> p o l", o=1)
                                       .to_broadcast([P, KT, LC]), ALU.mult).then_inc(dBu_ready, 1)
                    for i, name in enumerate(NORMS):
                        if n == AT_DVE[name] and (prep if i == 0 else post):
                            invert_root(i, c + 1 if i == 0 else c - 1)
                    if ffn and n == 2:
                        bias_x2(c - (CB + 1), 0)
                    if post and n == AT_POOL["x2"]:
                        add_out(c - 1, us)
                    if prep and n == AT_POOL["acc"]:
                        acc_init(c + 1)
                    if prep and n == AT_POOL["du"]:
                        du(c + 1)
                if ffn:
                    scatter(c - (CB + 1))
            stretches(pool, body)
            invert_root(1, NC - 1)
            bias_x2(CB - 1, 0)
            add_out(NC - 1, tail_uses)
            invert_root(2, NC - 1)
            scatter(CB - 1)
            with pool.Fori(CB, NC) as q:
                bias_x2(q, 1)
                scatter(q)

        @block.scalar
        def _(act):
            def out_of(us, name, dst, view=lambda a: a, func=ACT.Copy, **kw):
                act.activation(dst, view(us.read(act, name)), func, **kw).then_inc(evacuated, 1)

            us = setup_uses
            act.wait_ge(weights_in, 16 * 20)
            act.activation(A[:], A[:], ACT.Exp).then_inc(a_link, 1)
            act.wait_ge(a_link, 1)
            act.activation(A[:], A[:], ACT.Copy, scale=-1.0).then_inc(a_link, 1)
            act.wait_ge(a_link, 2)
            out_of(us, "mhat", mhatT[:], lambda a: a[:, 0:KT * NB].rearrange("p (k n) -> p k n", k=KT))
            out_of(us, "prompt", prompt[:, XC0:XC0 + NS], lambda a: a[0:NB, 0:NS])

            def fours(a):
                return a.rearrange("p (k n) -> p k n", k=KT)

            def biased(name, dst, which):
                a = fours(us.read(act, name))
                for k in range(KT):
                    i = act.activation(dst[:, k, :], a[:, k, :], ACT.Identity, bias=bqkv[:, which, k:k + 1])
                i.then_inc(evacuated, 1)

            for b in range(B):
                biased(f"keysT{b}", keysT[:, b], 1)
                out_of(us, f"foldedq{b}", foldedq[:, b], fours)
                out_of(us, f"biasq{b}", biasq[:, b, :], lambda a: a[0:1, 0:KEYS])
                biased(f"valuesT{b}", valuesT[:, b], 2)
                out_of(us, f"foldedo{b}", foldedo[:, b, :])
            for b in range(B):
                for i in range(TB):
                    name = f"raw{b}_{i}"
                    out_of(us, name, rawT[:, i % 4], fours)

            def prep_uT(c, us):
                wait(act, dBu_ready, NS * (c - 1))
                for i in range(2):
                    out_of(us, f"uT{i}", u[:, c % 2, 2 * i:2 * i + 2, :], lambda a: a.rearrange("p (k l) -> p k l", k=2))
                out_of(us, "onehot", onehot[:], lambda a: a[0:NB, 0:LC])

            def prep_proj(c, us):
                wait(act, b_stored, 16 * c)
                out_of(us, "proj", proj[:], lambda a: a[0:XW, 0:LC])

            def prep_delta(c, us):
                wait(act, hT_used, 2 * NS * (c - 1))
                for s in range(SUB):
                    out_of(us, f"C{s}", Cl[:, c % 2, s, :], lambda a: a[:, XC0:XC0 + NS])
                for i in range(2):
                    a = us.read(act, f"delta{i}").rearrange("p (k l) -> p k l", k=2)
                    for k in range(2):
                        j = act.activation(dlt[:, c % 2, 2 * i + k, :], a[:, k, :], ACT.Identity,
                                           bias=bdt[:, 2 * i + k:2 * i + k + 1])
                    j.then_inc(evacuated, 1)

            def prep_soft(c, us):
                act.wait_ge(abs_ready, c + 1)
                act.activation(soft_e[:], soft_l[:], ACT.Exp).then_inc(e_ready, 1)
                act.wait_ge(e_ready, c + 1)
                act.activation(soft_l[:], soft_e[:], ACT.Ln, bias=1.0).then_inc(ln_ready, 1)

            def post_xn2T(c, us):
                wait(act, x3_stored, 16 * c)
                for i in range(2):
                    out_of(us, f"xn2T{i}", xnT[:, 2 * i:2 * i + 2, :], lambda a: a.rearrange("p (k l) -> p k l", k=2))

            def post_scores(c, us):
                out_of(us, "scores", prob[:], lambda a: a[:, 0:SUB * KEYS].rearrange("p (s n) -> p s n", s=SUB))

            def post_expo(c, us):
                act.wait_ge(smax_ready, c + 1)
                for s in range(SUB):
                    act.activation(prob[:, s, :], prob[:, s, :], ACT.Exp, bias=pstat[:, 1, s:s + 1], scale=SCALE,
                                   accum_out=pstat[:, 2, s:s + 1]).then_inc(expo_ready, 1)

            def post_probsT(c, us):
                out_of(us, "probsT", probT[:], lambda a: a[:, 0:LC])

            def post_out(c, us):
                wait(act, x2_ready, c)
                for s in range(SUB):
                    out_of(us, f"out{s}", outs[:, s, :])

            def post_xn3T(c, us):
                for i in range(2):
                    a = us.read(act, f"xn3T{i}").rearrange("p (k l) -> p k l", k=2)
                    for k in range(2):
                        m = 2 * i + k
                        j = act.activation(xnT[:, m, :], a[:, k, :], ACT.Copy,
                                           accum_out=msum[:, c, m:m + 1])
                    j.then_inc(evacuated, 1)

            steps = {"uT": prep_uT, "proj": prep_proj, "delta": prep_delta, "soft": prep_soft}
            posts = {"xn2T": post_xn2T, "scores": post_scores, "expo": post_expo, "probsT": post_probsT,
                     "out": post_out, "xn3T": post_xn3T}

            def hidden(q, f, us):
                act.activation(hid[:, f % 3, :], us.read(act, f"hidden{f}")[:, 0:LC], ACT.Relu,
                               bias=b1[:, f:f + 1]).then_inc(evacuated, 1)

            for s in PREP_STEPS:
                steps[s](0, prep0_uses)

            def body(c, us, prep, post, ffn):
                act.wait_ge(dlt_ready, c + 1)
                for n in range(NS):
                    for k in range(KT):
                        if k % 2 == 0:
                            wait(act, scanned, 2 * NS * c + 2 * n + k // 2 - 1)
                            settle(act, c)
                        i = act.activation(dA[:, k // 2, (k % 2) * LC:(k % 2 + 1) * LC], dlt[:, c % 2, k, :],
                                           ACT.Exp, scale=A[:, k, n:n + 1])
                        if k % 2 == 1:
                            i.then_inc(dA_ready, 1)
                    if n > 0:
                        save_carry(c, n - 1)
                    if ffn:
                        if n == 0:
                            act.wait_ge(w_in, 160)
                        hidden(c - (CB + 1), n, us)
                    for s in steps_at(n, prep, post):
                        if s in steps:
                            steps[s](c + 1, us)
                        else:
                            posts[s](c - 1, us)
                save_carry(c, NS - 1)

            def save_carry(c, n):
                act.wait_ge(scanned, 2 * NS * c + 2 * n + 2)
                settle(act, c)
                act.activation(carry[:, n, :], h[:, n % 2, :, LC - 1], ACT.Copy).then_inc(carried, 1)
            stretches(act, body)

            us = tail_uses
            for n in range(NS):
                hidden(CB - 1, n, us)
                for s in steps_at(n, False, True):
                    posts[s](NC - 1, us)
            act.wait_ge(w_in, 320)
            with act.Fori(CB, NC) as q:
                us = Uses(at_ffn + (q - CB) * FT, [f"hidden{f}" for f in range(FT)])
                for f in range(FT):
                    hidden(q, f, us)

        @block.vector
        def _(dve):
            V = dve

            def chain(s, base):
                at = [base]

                def link(ins):
                    at[0] = at[0] + 1
                    ins.then_inc(s, 1)
                    dve.wait_ge(s, at[0])
                return link

            dve.wait_ge(weights_in, 16 * 20)
            link = chain(mhat_link, 0)
            link(V.tensor_tensor(mhat[:], means[:], means[:], ALU.mult))
            link(V.tensor_reduce(msq[:, 0:1], mhat[:], AX.X, ALU.add))
            dve.wait_ge(root_ready, 1)
            link(V.tensor_scalar(msq[:, 1:2], msq[:, 1:2], 1e-12, None, ALU.max))
            link(V.reciprocal(msq[:, 2:3], msq[:, 1:2]))
            link(V.tensor_scalar(mhat[:], means[:], msq[:, 2:3], None, ALU.mult))
            link(V.tensor_reduce(msq[:, 0:1], mhat[:], AX.X, ALU.add))
            link(V.tensor_scalar(msq[:, 3:4], msq[:, 0:1], 1.0 / D, None, ALU.mult))
            V.tensor_scalar(mhat[:], mhat[:], msq[:, 3:4], None, ALU.subtract).then_inc(mhat_ready, 1)

            dve.wait_ge(consts_ready, 10)
            link = chain(route_link, 0)
            for b in range(B):
                sc, eq, oh, tot, inc, tmp = [rt[i].rearrange("p (t k) -> p t k", k=NB) for i in range(6)]
                totk = rt[3].rearrange("p (k t) -> p k t", k=NB)
                inck = rt[4].rearrange("p (k t) -> p k t", k=NB)
                m1 = rt[6][:, 0:TB]
                m2 = rt[6][:, TB:2 * TB]

                def spread(m):
                    return m.rearrange("p (t o) -> p t o", o=1).to_broadcast([P, TB, NB])
                dve.wait_ge(scored, b + 1)
                link(V.tensor_copy(sc, fo[:, b, 0:TB * NB].rearrange("p (t k) -> p t k", k=NB)))
                link(V.tensor_reduce(m1, sc, AX.X, ALU.max))
                link(V.tensor_tensor(eq, sc, spread(m1), ALU.is_equal))
                link(V.tensor_tensor(eq, eq, rank8[:], ALU.mult))
                link(V.tensor_reduce(m2, eq, AX.X, ALU.max))
                link(V.tensor_tensor(oh, rank8[:], spread(m2), ALU.is_equal))
                V.tensor_copy(rows[:, b, :, D + 1:ROW], oh).then_inc(onehot_ready, 1)
                dve.wait_ge(counted, b + 1)
                link(V.tensor_copy(totk, hT[:, 1, 0:P].rearrange("p (t k) -> p k t", k=NB)))
                link(V.tensor_tensor_scan(rt[4], ones[:], rt[3], 0.0, ALU.mult, ALU.add))
                link(V.tensor_tensor(rt[4], rt[4], rt[3], ALU.subtract))
                link(V.tensor_tensor(tmp, hT[:, 0, 0:P].rearrange("p (t k) -> p t k", k=NB),
                                     rt[4].rearrange("p (k t) -> p t k", k=NB), ALU.add))
                link(V.tensor_tensor(tmp, tmp, oh, ALU.mult))
                link(V.tensor_reduce(m1, tmp, AX.X, ALU.add))
                V.tensor_scalar(pos[:, b, :], m1, float(b * S), None, ALU.add).then_inc(pos_ready, 1)

            def stats(src, i, c):
                link = chain(norm_link[i], 2 * c)
                settle(dve, c)
                for s in range(SUB):
                    j = V.bn_stats(st[:, i, s, :], src[:, s, :])
                link(j)
                settle(dve, c)
                for s in range(SUB):
                    j = V.bn_aggr(mv[:, i, s, :], st[:, i, s, :])
                link(j)
                V.tensor_scalar(rstd[:, i, :], mv[:, i, :, 1], EPS, None, ALU.add).then_inc(var_ready[i], 1)

            def normalise(dst, src, i, c, ready):
                dve.wait_ge(rstd_ready[i], c + 1)
                for s in range(SUB):
                    j = V.tensor_scalar(dst[:, s, :], src[:, s, :], mv[:, i, s, 0:1], rstd[:, i, s:s + 1],
                                        ALU.subtract, ALU.mult)
                j.then_inc(ready, 1)

            def norm1_stats(c):
                dve.wait_ge(xs_in, 16 * (c + 1))
                stats(xs[:, :, 0:D], 0, c)

            def norm1(c):
                wait(dve, acc_ready, c)
                normalise(xn, xs[:, :, 0:D], 0, c, xn_ready)

            def absz(c, us):
                us.done(dve, "delta1")
                wait(dve, dlt_ready, c)
                z = dlt[:, c % 2].rearrange("p k l -> p (k l)")
                V.scalar_tensor_tensor(out=soft_l[:].rearrange("p k l -> p (k l)"), in0=z, scalar=-1.0, in1=z,
                                       op0=ALU.mult, op1=ALU.min).then_inc(abs_ready, 1)

            def softplus(c):
                link = chain(soft_link, 3 * c)
                dve.wait_ge(ln_ready, c + 1)
                z = dlt[:, c % 2].rearrange("p k l -> p (k l)")
                e_, l_ = [v[:].rearrange("p k l -> p (k l)") for v in (soft_e, soft_l)]
                link(V.scalar_tensor_tensor(out=z, in0=z, scalar=0.0, in1=l_, op0=ALU.max, op1=ALU.add))
                link(V.tensor_scalar(l_, e_, 1.0, 1.0, ALU.add, ALU.subtract))
                link(V.tensor_tensor(e_, e_, l_, ALU.subtract))
                V.tensor_tensor(z, z, e_, ALU.add).then_inc(dlt_ready, 1)

            def norm2_stats(c):
                dve.wait_ge(hT_used, 2 * NS * (c + 1))
                stats(acc[:, c % 4], 1, c)

            def norm2(c):
                normalise(xn23, acc[:, c % 4], 1, c, xn2_ready)

            def smax(c, us):
                us.done(dve, "scores")
                V.tensor_reduce(pstat[:, 0, :], prob[:], AX.X, ALU.max).then_inc(smax_link, 1)
                dve.wait_ge(smax_link, c + 1)
                V.tensor_scalar(pstat[:, 1, :], pstat[:, 0, :], -SCALE, None, ALU.mult).then_inc(smax_ready, 1)

            def snorm(c):
                dve.wait_ge(expo_ready, SUB * (c + 1))
                V.reciprocal(pstat[:, 3, :], pstat[:, 2, :]).then_inc(soft_sum, 1)
                dve.wait_ge(soft_sum, c + 1)
                V.tensor_tensor(prob[:], prob[:], pstat[:, 3, :].rearrange("p (s o) -> p s o", o=1)
                                .to_broadcast([P, SUB, KEYS]), ALU.mult).then_inc(probs_ready, 1)

            def norm3_stats(c):
                dve.wait_ge(x2_ready, c + 1)
                stats(acc[:, c % 4], 2, c)

            def norm3(c):
                normalise(xn23, acc[:, c % 4], 2, c, xn3_ready)

            def finish(q):
                dve.wait_ge(ffn_ready, q + 1)
                dve.wait_ge(x2_biased, q + 1)
                wait(dve, out_stored, 16 * SUB * q)
                for s in range(SUB):
                    j = V.tensor_tensor(res[:, s, :], fo[:, s, :], x2[:, s, :], ALU.add)
                j.then_inc(res_ready, 1)

            def choose(b, us):
                us.done(dve, "xn3T1")
                V.tensor_reduce(mean[:], msum[:, b * CB:(b + 1) * CB, :].rearrange("p c k -> p k c"), AX.X,
                                ALU.add).then_inc(mean_link, 1)
                dve.wait_ge(mean_link, b + 1)
                V.tensor_scalar(mean[:], mean[:], 1.0 / S, None, ALU.mult).then_inc(mean_ready, 1)
                dve.wait_ge(voted, b + 1)
                link = chain(vote_link, 5 * b)
                link(V.tensor_tensor(vote[:, 0, :], fo[0:1, 0, 0:NE], br[:], ALU.add))
                link(V.tensor_reduce(vote[:, 1, 0:1], vote[:, 0, :], AX.X, ALU.max))
                link(V.tensor_scalar(vote[:, 2, :], vote[:, 0, :], vote[:, 1, 0:1], None, ALU.is_equal))
                link(V.tensor_tensor(vote[:, 2, :], vote[:, 2, :], rank8[0:1, 0, :], ALU.mult))
                link(V.tensor_reduce(vote[:, 3, 0:1], vote[:, 2, :], AX.X, ALU.max))
                V.tensor_scalar(expert[:, 0:1], vote[:, 3, 0:1], -1.0, float(NE), ALU.mult, ALU.add
                                ).then_inc(expert_ready, 1)

            norm1_stats(0)
            norm1(0)
            absz(0, prep0_uses)
            softplus(0)

            def body(c, us, prep, post, ffn):
                def rows_of(n, j):
                    use = 2 * NS * c + 2 * n + j
                    dve.wait_ge(hT_ready, use + 1)
                    if n == 0:
                        dve.wait_ge(acc_ready, c + 1)
                    else:
                        dve.wait_ge(hT_used, use - 1)
                    a = acc[:, c % 4, j, :]
                    V.scalar_tensor_tensor(out=a, in0=hT[:, j, :], scalar=Cl[:, c % 2, j, n:n + 1], in1=a,
                                           op0=ALU.mult, op1=ALU.add).then_inc(hT_used, 1)

                if isinstance(c, int) and c == CB:
                    dve.wait_ge(carried, NS * c)
                    V.memset(carry[:], 0.0).then_inc(carry_zeroed, 1)
                    dve.wait_ge(carry_zeroed, 1)
                for n in range(NS):
                    for k in range(KT):
                        if k % 2 == 0:
                            dve.wait_ge(dA_ready, 2 * NS * c + 2 * n + k // 2 + 1)
                        if k == 0:
                            dve.wait_ge(dBu_ready, NS * c + n + 1)
                            wait(dve, hT_ready, 2 * NS * c + 2 * (n - 1))
                            wait(dve, carried, NS * c + n - 1)
                        j = V.tensor_tensor_scan(h[:, n % 2, k, :], dA[:, k // 2, (k % 2) * LC:(k % 2 + 1) * LC],
                                                 dBu[:, n % 2, k, :], carry[:, n, k:k + 1], ALU.mult, ALU.add)
                        if k % 2 == 1:
                            j.then_inc(scanned, 1)
                            if n > 0:
                                rows_of(n - 1, k // 2)
                    if post and n == AT_DVE["norm2"]:
                        norm2_stats(c - 1)
                    if post and n == AT_DVE["norm2"] + 1:
                        norm2(c - 1)
                    if prep and n == AT_DVE["norm1"]:
                        norm1_stats(c + 1)
                    if prep and n == AT_DVE["norm1"] + 1:
                        norm1(c + 1)
                    if post and n == AT_DVE["max"]:
                        smax(c - 1, us)
                    if post and n == AT_DVE["normal"]:
                        snorm(c - 1)
                    if prep and n == AT_DVE["abs"]:
                        absz(c + 1, us)
                    if prep and n == AT_DVE["softplus"]:
                        softplus(c + 1)
                    if post and n == AT_DVE["norm3"]:
                        norm3_stats(c - 1)
                    if post and n == AT_DVE["norm3"] + 1:
                        norm3(c - 1)
                    if isinstance(c, int) and c == CB and n == AT_DVE["choose"]:
                        choose(0, us)
                for j in range(SUB):
                    rows_of(NS - 1, j)
                if ffn:
                    finish(c - (CB + 1))
            stretches(dve, body)

            us = tail_uses
            norm2_stats(NC - 1)
            norm2(NC - 1)
            smax(NC - 1, us)
            snorm(NC - 1)
            norm3_stats(NC - 1)
            norm3(NC - 1)
            finish(CB - 1)
            choose(1, us)
            with dve.Fori(CB, NC) as q:
                finish(q)

        @block.tensor
        def _(pe):
            us = setup_uses
            pe.wait_ge(weights_in, 16 * 20)
            pe.wait_ge(consts_ready, 10)
            pe.wait_ge(mhat_ready, 1)
            w = us.fill(pe, "mhat")
            for k in range(KT):
                i = pe.transpose(w[:, k * NB:(k + 1) * NB], mhat[:, k * P:(k + 1) * P], ident[0:NB, 0:NB])
            i.then_inc(filled, 1)

            def product(out, lhs, rhs):
                n = len(lhs)
                for i in range(n):
                    j = pe.matmul(out, lhs[i], rhs[i], start=(i == 0), stop=(i == n - 1))
                return j

            w = us.fill(pe, "prompt")
            product(w[0:NB, 0:NS], [meansT[:, k, :] for k in range(KT)], [promptT[:, k, :] for k in range(KT)]
                    ).then_inc(filled, 1)
            for b in range(B):
                ctx_k = [ctxT[:, b, k, :] for k in range(KT)]
                w = us.fill(pe, f"keysT{b}")
                for m in range(KT):
                    i = product(w[:, m * P:(m + 1) * P], [wk[:, k, m * P:(m + 1) * P] for k in range(KT)], ctx_k)
                i.then_inc(filled, 1)
                us.done(pe, f"keysT{b}")
                keys_k = [keysT[:, b, k, :] for k in range(KT)]
                w = us.fill(pe, f"foldedq{b}")
                for m in range(KT):
                    i = product(w[:, m * P:(m + 1) * P], [wq[:, k, m * P:(m + 1) * P] for k in range(KT)], keys_k)
                i.then_inc(filled, 1)
                w = us.fill(pe, f"biasq{b}")
                product(w[0:1, 0:KEYS], [bqkv[:, 0, k:k + 1] for k in range(KT)], keys_k).then_inc(filled, 1)
                w = us.fill(pe, f"valuesT{b}")
                for m in range(KT):
                    i = product(w[:, m * P:(m + 1) * P], [wv[:, k, m * P:(m + 1) * P] for k in range(KT)], ctx_k)
                i.then_inc(filled, 1)
                us.done(pe, f"valuesT{b}")
                w = us.fill(pe, f"foldedo{b}")
                product(w, [valuesT[:, b, k, :] for k in range(KT)] + [ones[0:1, :]],
                        [wo[:, k, :] for k in range(KT)] + [bo[:]]).then_inc(filled, 1)

            for b in range(B):
                def score(i):
                    us.done(pe, f"raw{b}_{i}")
                    return product(fo[:, b, i * NB:(i + 1) * NB], [rawT[:, i % 4, k, :] for k in range(KT)],
                                   [mhatT[:, k, :] for k in range(KT)])
                pe.wait_ge(x_in[b], 64)
                for i in range(TB):
                    w = us.fill(pe, f"raw{b}_{i}")
                    for k in range(KT):
                        j = pe.transpose(w[:, k * P:(k + 1) * P], rows[:, b, i, k * P:(k + 1) * P], ident[:])
                    j.then_inc(filled, 1)
                    if i > 0:
                        score(i - 1)
                score(TB - 1).then_inc(scored, 1)
                pe.wait_ge(onehot_ready, b + 1)
                wait(pe, pos_ready, b)
                pe.matmul(hT[:, 0, 0:P], before[:], rt[2], start=True, stop=True)
                pe.matmul(hT[:, 1, 0:P], ones[:], rt[2], start=True, stop=True).then_inc(counted, 1)

            def prep_uT(c, us):
                pe.wait_ge(xn_ready, c + 1)
                for i in range(2):
                    w = us.fill(pe, f"uT{i}")
                    for k in range(2):
                        for s in range(SUB):
                            m = 2 * i + k
                            j = pe.transpose(w[:, k * LC + s * P:k * LC + (s + 1) * P], xn[:, s, m * P:(m + 1) * P], ident[:])
                    j.then_inc(filled, 1)
                w = us.fill(pe, "onehot")
                for s in range(SUB):
                    j = pe.matmul(w[0:NB, s * P:(s + 1) * P], xs[:, s, D + 1:ROW], ident[:], start=True, stop=True)
                j.then_inc(filled, 1)

            def prep_proj(c, us):
                us.done(pe, "onehot")
                w = us.fill(pe, "proj")
                product(w[0:XW, 0:LC], [wx[:, k, :] for k in range(KT)] + [prompt[:]],
                        [u[:, c % 2, k, :] for k in range(KT)] + [onehot[:]]).then_inc(filled, 1)

            def prep_delta(c, us):
                us.done(pe, "proj")
                for s in range(SUB):
                    w = us.fill(pe, f"C{s}")
                    settle(pe, us.base)
                    pe.transpose(w[:, 0:XB0], proj[0:XB0, s * P:(s + 1) * P], ident[0:XB0, 0:XB0]).then_inc(filled, 1)
                for i in range(2):
                    w = us.fill(pe, f"delta{i}")
                    for k in range(2):
                        m = 2 * i + k
                        j = pe.matmul(w[:, k * LC:(k + 1) * LC], wdt[:, m * P:(m + 1) * P], proj[0:R, :], start=True, stop=True)
                    j.then_inc(filled, 1)

            def turn(us, name, ready, c):
                pe.wait_ge(ready, c + 1)
                for i in range(2):
                    w = us.fill(pe, f"{name}{i}")
                    for k in range(2):
                        for s in range(SUB):
                            m = 2 * i + k
                            j = pe.transpose(w[:, k * LC + s * P:k * LC + (s + 1) * P], xn23[:, s, m * P:(m + 1) * P], ident[:])
                    j.then_inc(filled, 1)

            def post_scores(b, us):
                us.done(pe, "xn2T1")
                w = us.fill(pe, "scores")
                for s in range(SUB):
                    j = product(w[:, s * KEYS:(s + 1) * KEYS],
                                [xnT[:, k, s * P:(s + 1) * P] for k in range(KT)] + [ones[0:1, :]],
                                [foldedq[:, b, k, :] for k in range(KT)] + [biasq[:, b, :]])
                j.then_inc(filled, 1)

            def post_probsT(c, us):
                pe.wait_ge(probs_ready, c + 1)
                w = us.fill(pe, "probsT")
                for s in range(SUB):
                    j = pe.transpose(w[:, s * P:(s + 1) * P], prob[:, s, :], ident[:])
                j.then_inc(filled, 1)

            def post_out(b, us):
                us.done(pe, "probsT")
                for s in range(SUB):
                    w = us.fill(pe, f"out{s}")
                    product(w, [xnT[:, k, s * P:(s + 1) * P] for k in range(KT)] + [probT[:, s * P:(s + 1) * P]],
                            [wo[:, k, :] for k in range(KT)] + [foldedo[:, b, :]]).then_inc(filled, 1)

            def step(s, c, us, b):
                if s == "uT":
                    prep_uT(c + 1, us)
                elif s == "proj":
                    prep_proj(c + 1, us)
                elif s == "delta":
                    prep_delta(c + 1, us)
                elif s == "xn2T":
                    turn(us, "xn2T", xn2_ready, c - 1)
                elif s == "scores":
                    post_scores(b, us)
                elif s == "probsT":
                    post_probsT(c - 1, us)
                elif s == "out":
                    post_out(b, us)
                elif s == "xn3T":
                    turn(us, "xn3T", xn3_ready, c - 1)

            def first_product(q, f, us):
                w = us.fill(pe, f"hidden{f}")
                product(w[:, 0:LC], [w1[:, k, f * P:(f + 1) * P] for k in range(KT)],
                        [x3[:, q % 2, k, :] for k in range(KT)]).then_inc(filled, 1)

            def second_product(q, f, us):
                us.done(pe, f"hidden{f}")
                if f == 0:
                    wait(pe, res_ready, q)
                for s in range(SUB):
                    j = pe.matmul(fo[:, s, :], hid[:, f % 3, s * P:(s + 1) * P], w2[:, f, :],
                                  start=(f == 0), stop=(f == FT - 1))
                if f == FT - 1:
                    j.then_inc(ffn_ready, 1)

            def vote_for(b):
                pe.wait_ge(mean_ready, b + 1)
                product(fo[0:1, 0, 0:NE], [mean[:, k:k + 1] for k in range(KT)], [wr[:, k, :] for k in range(KT)]
                        ).then_inc(voted, 1)

            for s in PREP_STEPS:
                step(s, -1, prep0_uses, 0)

            def body(c, us, prep, post, ffn):
                def turn_h(n, j):
                    use = 2 * NS * c + 2 * n + j
                    if j == 0:
                        pe.wait_ge(scanned, 2 * NS * c + 2 * n + 2)
                    wait(pe, hT_used, use - 1)
                    for k in range(KT):
                        i = pe.transpose(hT[:, j, k * P:(k + 1) * P], h[:, n % 2, k, j * P:(j + 1) * P], ident[:])
                    i.then_inc(hT_ready, 1)

                batch = us.batch
                q = c - (CB + 1)
                for n in range(NS):
                    if n > 0:
                        turn_h(n - 1, 0)
                    if ffn:
                        if n == 0:
                            pe.wait_ge(w_in, 160)
                            pe.wait_ge(x3_in, 16 * (q + 1))
                        first_product(q, n, us)
                    if n > 0:
                        turn_h(n - 1, 1)
                        if ffn:
                            second_product(q, n - 1, us)
                    for s in steps_at(n, prep, post):
                        step(s, c, us, batch)
                    if isinstance(c, int) and c == CB and n == AT_DVE["choose"]:
                        vote_for(0)
                for j in range(SUB):
                    turn_h(NS - 1, j)
                if ffn:
                    second_product(q, FT - 1, us)

            for k, ((lo, hi), prep, post, ffn) in enumerate(STRETCH):
                names = uses(prep, post, ffn)

                def one(c):
                    us = Uses(base_of(c, k), names)
                    us.batch = 0 if lo <= CB else 1
                    body(c, us, prep, post, ffn)
                if hi - lo == 1:
                    one(lo)
                else:
                    with pe.Fori(lo, hi) as c:
                        one(c)

            us = tail_uses
            q = CB - 1
            pe.wait_ge(x3_in, 16 * (q + 1))
            for n in range(NS):
                first_product(q, n, us)
                if n > 0:
                    second_product(q, n - 1, us)
                for s in steps_at(n, False, True):
                    step(s, NC, us, 1)
            second_product(q, FT - 1, us)
            pe.wait_ge(res_ready, CB)
            vote_for(1)
            pe.wait_ge(w_in, 320)
            with pe.Fori(CB, NC) as q:
                us = Uses(at_ffn + (q - CB) * FT, [f"hidden{f}" for f in range(FT)])
                pe.wait_ge(x3_in, 16 * (q + 1))
                for f in range(FT):
                    first_product(q, f, us)
                    if f > 0:
                        second_product(q, f - 1, us)
                second_product(q, FT - 1, us)


def kernel(x, ctx_1024, L0_attn_means, L0_attn_prompt_weight, L0_attn_x_proj_weight, L0_attn_dt_projs_weight,
           L0_attn_dt_projs_bias, L0_attn_A_logs, L0_attn_Ds, L0_xattn_Wq, L0_xattn_bq, L0_xattn_Wk, L0_xattn_bk,
           L0_xattn_Wv, L0_xattn_bv, L0_xattn_Wo, L0_xattn_bo, L0_ffn_Wr, L0_ffn_br, L0_ffn_W1, L0_ffn_b1,
           L0_ffn_W2, L0_ffn_b2):
    import concourse.bacc as bacc
    from concourse.bass_utils import run_bass_kernel_spmd

    def tiles(v):
        return np.ascontiguousarray(np.asarray(v).reshape(-1, P).T)

    def turned(m):
        return np.ascontiguousarray(np.asarray(m).T)

    xp = np.asarray(L0_attn_x_proj_weight)
    wx = np.zeros((D, XW), xp.dtype)
    wx[:, 0:R] = xp[0:R].T
    wx[:, XC0:XC0 + NS] = xp[R + NS:].T
    wx[:, XB0:XB0 + NS] = xp[R:R + NS].T
    arrays = {
        "x": np.ascontiguousarray(x), "ctxT": np.ascontiguousarray(np.asarray(ctx_1024).transpose(0, 2, 1)),
        "means": np.ascontiguousarray(L0_attn_means), "meansT": turned(L0_attn_means),
        "promptT": turned(L0_attn_prompt_weight), "wx": wx, "wdt": turned(L0_attn_dt_projs_weight),
        "bdt": tiles(L0_attn_dt_projs_bias), "A_logs": np.ascontiguousarray(L0_attn_A_logs),
        "Ds": np.ascontiguousarray(L0_attn_Ds),
        "Wq": np.ascontiguousarray(L0_xattn_Wq), "WkT": turned(L0_xattn_Wk), "WvT": turned(L0_xattn_Wv),
        "WoT": turned(L0_xattn_Wo), "bq": tiles(L0_xattn_bq), "bk": tiles(L0_xattn_bk), "bv": tiles(L0_xattn_bv),
        "bo": np.ascontiguousarray(L0_xattn_bo), "Wr": np.ascontiguousarray(L0_ffn_Wr),
        "br": np.ascontiguousarray(L0_ffn_br), "W1": np.ascontiguousarray(L0_ffn_W1),
        "b1": np.ascontiguousarray(np.asarray(L0_ffn_b1).reshape(NE, FT, P).transpose(0, 2, 1)),
        "W2": np.ascontiguousarray(L0_ffn_W2), "b2": np.ascontiguousarray(L0_ffn_b2),
    }
    nc = bacc.Bacc("TRN2", target_bir_lowering=False, num_devices=1)
    t = {n: nc.dram_tensor(f"in_{n}", a.shape, mybir.dt.from_np(a.dtype), kind="ExternalInput").ap()
         for n, a in arrays.items()}
    t["out"] = nc.dram_tensor("out_x", (B, S, D), F32, kind="ExternalOutput").ap()
    build(nc, t)
    r = run_bass_kernel_spmd(nc, [{f"in_{n}": a for n, a in arrays.items()}], core_ids=[0])
    return r.results[0]["out_x"]
```

```python
from contextlib import ExitStack

import numpy as np
import concourse.bass as bass
from concourse import mybir

F32 = mybir.dt.float32
I32 = mybir.dt.int32
U32 = mybir.dt.uint32
ALU = mybir.AluOpType
ACT = mybir.ActivationFunctionType
AX = mybir.AxisListType

P = 128
B, S, D = 2, 2048, 512
KT = D // P
NS, R = 16, 32
NB = 8
NE, FF = 8, 2048
FT = FF // P
KEYS = 128
LC = 256
SUB = LC // P
CB = S // LC
NC = B * CB
TB = S // P
ROW = D + 1 + NB
XC0, XB0 = 32, 64
XW = XB0 + NS
BG = 4
NG = NS // BG
EPS = 1e-5
SCALE = D ** -0.5

RAW_USES = [[f"raw{b}_{i}" for i in range(TB)] for b in range(B)]
SETUP_USES = ["mhat", "prompt"] + RAW_USES[0]
FOLD_USES = [f"{n}{b}" for b in range(B) for n in ("keysT", "foldedq", "biasq", "valuesT", "foldedo")]
SLOTS = {0: ["onehot"], 1: ["uT0"], 2: ["uT1", "xn2T0"], 3: ["xn2T1"], 4: ["scores"], 5: ["proj"], 6: ["delta0"],
         7: ["delta1", "probsT"], 9: ["out0"], 10: ["out1"], 11: ["C0"], 12: ["C1"], 15: ["xn3T0", "xn3T1"]}
OUT_SPREAD = {(8, 0): ("out0", 0, 2), (8, 1): ("out0", 2, 3), (9, 0): ("out0", 3, 5),
              (9, 1): ("out1", 0, 2), (10, 0): ("out1", 2, 3), (10, 1): ("out1", 3, 5)}
OUT_TIGHT = {(9, 0): ("out0", 0, 3), (9, 1): ("out0", 3, 5), (10, 0): ("out1", 0, 3), (10, 1): ("out1", 3, 5)}
AT_ACT = {"expo": 6, "soft_e": 9, "soft_l": 10}
AT_DVE = {"finish": 0, "norm1": 0, "norm2": 1, "max": 4, "normal": 6, "abs": 8, "softplus": 10, "stats3": 12,
          "norm3": 14, "choose": 15, "route": 1, "place": 4}
AT_POOL = {"root12": 2, "scatter": 3, "acc": 4, "bias": 9, "x2": 13, "du": 14, "root3": 15}
H_RING = 4
DBU_SLOT = [n % 3 for n in range(NS - 1)] + [1]
DBU_BACK = [next(i for i in range(1, NS) if DBU_SLOT[n - i] == DBU_SLOT[n]) for n in range(NS)]
PREP_USES = ["onehot", "uT0", "uT1", "proj", "delta0", "delta1", "C0", "C1"]


class Kind:
    def __init__(self, first=False, second=False, prep=True, post=True, ffn=False, finish=False, choose=False):
        self.first, self.second, self.choose = first, second, choose
        self.prep, self.post, self.ffn, self.finish = prep, post, ffn, finish

    def slots(self, n):
        return [u for u in SLOTS.get(n, []) if (self.prep if u in PREP_USES else self.post)]

    def uses_at(self, n):
        return ([f"hidden{n}"] if self.ffn else []) + ([RAW_USES[1][n]] if self.first else []) + self.slots(n) + \
            ([FOLD_USES[n - 1]] if self.first and 1 <= n <= len(FOLD_USES) else [])

    def uses(self):
        return [u for n in range(NS) for u in self.uses_at(n)]


STRETCH = [((0, 1), Kind(first=True, post=False)), ((1, 2), Kind(second=True)), ((2, CB), Kind()),
           ((CB, CB + 1), Kind(choose=True)), ((CB + 1, CB + 2), Kind(ffn=True)),
           ((CB + 2, CB + 3), Kind(ffn=True, finish=True)), ((CB + 3, NC - 1), Kind(ffn=True, finish=True)), ((NC - 1, NC), Kind(prep=False, ffn=True, finish=True))]


def build(nc, t):
    with ExitStack() as ctx:
        def sb(name, shape, dt=F32):
            return ctx.enter_context(nc.sbuf_tensor(name, shape, dt))

        def ps(name, shape):
            return ctx.enter_context(nc.psum_tensor(name, shape, F32))

        def sem(name):
            return ctx.enter_context(nc.semaphore(name))

        def dram(name, shape, dt=F32):
            return nc.dram_tensor(name, shape, dt, kind="Internal").ap()

        xsorted = dram("xsorted", (B * S, ROW))
        b_rows = dram("b_rows", (NC, NS, LC))
        x2_dram = dram("x2_dram", (NC, P, SUB * D))
        x3_dram = dram("x3_dram", (NC, P, KT * LC))

        big = sb("big", [P, B * TB * ROW])
        rows = big[:].rearrange("p (b t r) -> p b t r", b=B, t=TB)
        w1 = big[:, 0:KT * FF].rearrange("p (k f) -> p k f", k=KT)
        w2 = big[:, KT * FF:KT * FF + FT * D].rearrange("p (f d) -> p f d", f=FT)

        ident = sb("ident", [P, P])
        ones = sb("ones", [P, P])
        before = sb("before", [P, P])
        rank8 = sb("rank8", [P, TB, NB])
        means = sb("means", [NB, D])
        meansT = sb("meansT", [P, KT, NB])
        mhat = sb("mhat", [NB, D])
        mhatT = sb("mhatT", [P, KT, NB])
        msq = sb("msq", [NB, 4])
        promptT = sb("promptT", [P, KT, NS])
        prompt = sb("prompt", [NB, XW])
        wx = sb("wx", [P, KT, XW])
        wdt = sb("wdt", [R, D])
        bdt = sb("bdt", [P, KT])
        A = sb("A", [P, KT, NS])
        Dbc = sb("Dbc", [P, D])
        wo = sb("wo", [P, KT, D])
        bqkv = sb("bqkv", [P, 3, KT])
        bo = sb("bo", [1, D])
        wr = sb("wr", [P, KT, NE])
        br = sb("br", [1, NE])
        foldedq = sb("foldedq", [P, B, KT, KEYS])
        biasq = sb("biasq", [1, B, KEYS])
        foldedo = sb("foldedo", [P, B, D])

        xs = sb("xs", [P, SUB, ROW])
        xn = sb("xn", [P, SUB, D])
        soft_e = xn[:].rearrange("p s (a l) -> p (s a) l", l=LC)
        half = sb("half", [P, SUB + 1])
        st = sb("st", [P, 3, SUB, 6])
        mv = sb("mv", [P, 3, SUB, 2])
        rstd = sb("rstd", [P, 3, SUB])
        u = sb("u", [P, 2, KT, LC])
        dlt = sb("dlt", [P, 2, KT, LC])
        soft_l = sb("soft_l", [P, KT, LC])
        acc = sb("acc", [P, 4, SUB, D])
        onehot = sb("onehot", [NB, LC])
        proj = sb("proj", [XW, LC])
        Cl = sb("Cl", [P, 2, SUB, NS])
        Bs = sb("Bs", [P, 2, BG, LC])
        dBu = sb("dBu", [P, 3, KT, LC])
        h = sb("h", [P, H_RING, KT, LC])
        carry = sb("carry", [P, NS, KT])
        ids = sb("ids", [P, NC * SUB], U32)
        ids_now = sb("ids_now", [P, SUB], U32)

        xn23 = sb("xn23", [P, SUB, D])
        xnT = sb("xnT", [P, KT, LC])
        prob = sb("prob", [P, SUB, KEYS])
        pstat = sb("pstat", [P, 4, SUB])
        probT = sb("probT", [P, SUB * P])
        msum = sb("msum", [P, NC, KT])

        x3 = sb("x3", [P, 2, KT, LC])
        x2 = sb("x2", [P, SUB, D])
        hid = sb("hid", [P, 3, LC])
        b1 = sb("b1", [P, FT])
        b2 = sb("b2", [P, D])
        mean = sb("mean", [P, KT])
        vote = sb("vote", [1, 4, NE])
        expert = sb("expert", [1, 4], I32)

        free = big[:, 0:TB * ROW]
        wq, wk, wv = [free[:, i * KT * D:(i + 1) * KT * D].rearrange("p (k d) -> p k d", k=KT) for i in range(3)]
        keysT, valuesT = [free[:, 3 * KT * D + i * B * KT * KEYS:3 * KT * D + (i + 1) * B * KT * KEYS]
                          .rearrange("p (b k n) -> p b k n", b=B, k=KT) for i in range(2)]
        x3flat = x3[:].rearrange("p a k l -> p (a k l)")
        ctxT = x3flat[:, 0:B * KT * KEYS].rearrange("p (b k n) -> p b k n", b=B, k=KT)
        rawT = x3flat[:, B * KT * KEYS:].rearrange("p (a k n) -> p a k n", a=2, k=KT)
        rt = [x2[:].rearrange("p s d -> p (s d)")[:, i * P:(i + 1) * P] for i in range(7)]
        pos = sb("pos", [P, B, TB], U32)

        dA = ps("dA", [P, 2, 2 * LC])
        hT = ps("hT", [P, 2, D])
        work = ps("work", [P, 2, 512])
        fo = ps("fo", [P, 2, D])

        prep_in, fold_in, x_in = sem("prep_in"), sem("fold_in"), [sem(f"x_in{b}") for b in range(B)]
        consts_ready = sem("consts_ready")
        root_ready = sem("root_ready")
        var_ready = [sem(f"var{i}_ready") for i in (1, 2, 3)]
        rstd_ready = [sem(f"rstd{i}_ready") for i in (1, 2, 3)]
        mhat_link, mhat_ready = sem("mhat_link"), sem("mhat_ready")
        filled, evacuated = sem("filled"), sem("evacuated")
        a_link = sem("a_link")
        scored = sem("scored")
        route_link, onehot_ready, counted = sem("route_link"), sem("onehot_ready"), sem("counted")
        pos_ready, tagged, sorted_out = sem("pos_ready"), sem("tagged"), sem("sorted_out")
        xs_in = sem("xs_in")
        norm_link = [sem(f"norm{i}_link") for i in (1, 2, 3)]
        xn_ready, xn2_ready, xn3_ready = sem("xn_ready"), sem("xn2_ready"), sem("xn3_ready")
        acc_link, acc_ready = sem("acc_link"), sem("acc_ready")
        abs_ready, e_ready, ln_ready = sem("abs_ready"), sem("e_ready"), sem("ln_ready")
        soft_link, dlt_ready, du_ready = sem("soft_link"), sem("dlt_ready"), sem("du_ready")
        b_stored, b_in = sem("b_stored"), [sem(f"b_in{i}") for i in range(2)]
        dA_ready, dBu_ready, scanned = sem("dA_ready"), sem("dBu_ready"), sem("scanned")
        hT_ready, hT_used, carried = sem("hT_ready"), sem("hT_used"), sem("carried")
        carry_zeroed = sem("carry_zeroed")
        smax_ready, expo_ready, soft_sum, probs_ready = sem("smax_ready"), sem("expo_ready"), sem("soft_sum"), sem("probs_ready")
        smax_link = sem("smax_link")
        x2_ready, x2_stored, x3_stored = sem("x2_ready"), sem("x2_stored"), sem("x3_stored")
        mean_link, mean_ready, voted = sem("mean_link"), sem("mean_ready"), sem("voted")
        vote_link, expert_ready = sem("vote_link"), sem("expert_ready")
        w_in = sem("w_in")
        x3_in, x2_in, x2_biased = sem("x3_in"), sem("x2_in"), sem("x2_biased")
        ffn_ready, res_ready = sem("ffn_ready"), sem("res_ready")
        ids_link, ids_ready, out_stored = sem("ids_link"), sem("ids_ready"), sem("out_stored")

        def wait(eng, s, value):
            if not isinstance(value, int) or value > 0:
                eng.wait_ge(s, value)

        def settle(eng, value):
            if not isinstance(value, int):
                eng.nop(nofuse=True)

        at_prep0 = len(SETUP_USES)
        at_it0 = at_prep0 + len(PREP_USES)
        assert all(n % 2 == 0 for n in (at_prep0, at_it0, FT, *(len(k.uses()) for _, k in STRETCH)))

        class Uses:
            def __init__(self, base, names):
                self.base, self.names = base, names

            def bank(self, name):
                return work[:, self.names.index(name) % 2]

            def fill(self, pe, name):
                wait(pe, evacuated, self.base + (self.names.index(name) - 1))
                return self.bank(name)

            def read(self, act, name):
                act.wait_ge(filled, self.base + (self.names.index(name) + 1))
                settle(act, self.base)
                return self.bank(name)

            def done(self, eng, name):
                eng.wait_ge(evacuated, self.base + (self.names.index(name) + 1))

        setup_uses = Uses(0, SETUP_USES)
        prep0_uses = Uses(at_prep0, PREP_USES)
        def base_of(c, k):
            at = at_it0
            for (lo, hi), kind in STRETCH[:k]:
                at += (hi - lo) * len(kind.uses())
            (lo, _), kind = STRETCH[k]
            return at + (c - lo) * len(kind.uses())

        def stretches(eng, body):
            for k, ((lo, hi), kind) in enumerate(STRETCH):
                batch = 0 if lo <= CB else 1
                if hi - lo == 1:
                    body(lo, Uses(base_of(lo, k), kind.uses()), kind, batch)
                else:
                    with eng.Fori(lo, hi) as c:
                        body(c, Uses(base_of(c, k), kind.uses()), kind, batch)

        at_tail = base_of(NC, len(STRETCH) - 1)
        tail_kind = Kind(prep=False, ffn=True)
        tail_uses = Uses(at_tail, tail_kind.uses())
        at_ffn = at_tail + len(tail_uses.names)

        block = ctx.enter_context(nc.Block())

        @block.sync
        def _(sp):
            def load(dst, src, s):
                sp.dma_start(dst, src).then_inc(s, 16)

            def row(v):
                return v.rearrange("(o d) -> o d", o=1)

            def by_tile(m):
                return m.rearrange("(k p) n -> p k n", p=P)

            def load_rows(b):
                n = TB // 4
                for i in range(4):
                    load(rows[:, b, i * n:(i + 1) * n, 0:D],
                         t["x"][b, i * n * P:(i + 1) * n * P, :].rearrange("(t p) d -> p t d", p=P), x_in[b])

            load(means[:], t["means"], prep_in)
            load(meansT[:], by_tile(t["meansT"]), prep_in)
            load(promptT[:], by_tile(t["promptT"]), prep_in)
            load_rows(0)
            load(wx[:], by_tile(t["wx"]), prep_in)
            load(wdt[:], t["wdt"], prep_in)
            load(bdt[:], t["bdt"], prep_in)
            load(A[:], by_tile(t["A_logs"]), prep_in)
            load(Dbc[:], row(t["Ds"]).to_broadcast([P, D]), prep_in)
            load_rows(1)
            load(wo[:], by_tile(t["WoT"]), fold_in)
            for i, n in enumerate(("bq", "bk", "bv")):
                load(bqkv[:, i, :], t[n], fold_in)
            load(bo[:], row(t["bo"]), fold_in)
            load(wr[:], by_tile(t["Wr"]), fold_in)
            load(br[:], row(t["br"]), fold_in)
            for b in range(B):
                load(ctxT[:, b], by_tile(t["ctxT"][b]), fold_in)

            def load_xs(c):
                if not isinstance(c, int) or c > 0:
                    sp.wait_ge(dlt_ready, c)
                    sp.wait_ge(acc_ready, c)
                sp.dma_start(xs[:], xsorted.rearrange("(c s p) r -> c p s r", s=SUB, p=P)[c]).then_inc(xs_in, 16)

            def store_b(c, us):
                us.done(sp, "proj")
                sp.dma_start(b_rows[c], proj[XB0:XB0 + NS, :]).then_inc(b_stored, 16)
                sp.wait_ge(b_stored, 16 * (c + 1))

            def load_b(c, g):
                wait(sp, dBu_ready, NS * c + BG * (g - 1))
                sp.dma_start(Bs[:, g % 2],
                             b_rows[c, g * BG:(g + 1) * BG, :].rearrange("(o n) l -> o n l", o=1).to_broadcast([P, BG, LC])
                             ).then_inc(b_in[g % 2], 16)

            def load_w(b):
                sp.wait_ge(expert_ready, b + 1)
                if b > 0:
                    sp.wait_ge(ffn_ready, b * CB)
                    sp.wait_ge(x2_biased, b * CB)
                e = sp.value_load(expert[0:1, 0:1], min_val=0, max_val=NE - 1)
                for k in range(KT):
                    sp.dma_start(w1[:, k, :], t["W1"][e].rearrange("(k p) f -> k p f", p=P)[k]).then_inc(w_in, 16)
                for k in range(4):
                    n = FT // 4
                    sp.dma_start(w2[:, k * n:(k + 1) * n, :],
                                 t["W2"][e].rearrange("(k n p) f -> k p n f", p=P, n=n)[k]).then_inc(w_in, 16)
                sp.dma_start(b1[:], t["b1"][e]).then_inc(w_in, 16)
                sp.dma_start(b2[:], t["b2"][e].rearrange("(o d) -> o d", o=1).to_broadcast([P, D])).then_inc(w_in, 16)

            def load_x3(q):
                wait(sp, ffn_ready, q - 1)
                wait(sp, x3_in, 16 * q)
                sp.wait_ge(x3_stored, 16 * (q + 1))
                sp.dma_start(x3[:, q % 2], x3_dram[q].rearrange("p (k l) -> p k l", k=KT)).then_inc(x3_in, 16)

            def load_x2(q):
                wait(sp, out_stored, 16 * SUB * q)
                sp.wait_ge(x2_stored, 16 * (q + 1))
                sp.dma_start(x2[:], x2_dram[q].rearrange("p (s d) -> p s d", s=SUB)).then_inc(x2_in, 16)

            def store_post(c):
                sp.wait_ge(x2_ready, c + 1)
                wait(sp, x2_stored, 16 * c)
                sp.dma_start(x2_dram[c].rearrange("p (s d) -> p s d", s=SUB), acc[:, c % 4]).then_inc(x2_stored, 16)

            def store_x3(c, uses):
                sp.wait_ge(evacuated, uses)
                wait(sp, x3_stored, 16 * c)
                sp.dma_start(x3_dram[c].rearrange("p (k l) -> p k l", k=KT), xnT[:]).then_inc(x3_stored, 16)

            sp.wait_ge(sorted_out, 16 * TB)
            load_xs(0)
            for w, n in ((wq, "Wq"), (wk, "WkT"), (wv, "WvT")):
                load(w, by_tile(t[n]), fold_in)
            store_b(0, prep0_uses)
            load_b(0, 0)
            load_b(0, 1)

            def body(c, us, kind, batch):
                if kind.prep:
                    load_xs(c + 1)
                if kind.post and not kind.second:
                    store_x3(c - 2, us.base)
                load_b(c, 2)
                if kind.ffn:
                    load_x2(c - (CB + 1))
                    load_x3(c - CB)
                load_b(c, 3)
                if kind.prep:
                    store_b(c + 1, us)
                if kind.post:
                    store_post(c - 1)
                if kind.prep:
                    load_b(c + 1, 0)
                if kind.prep:
                    load_b(c + 1, 1)
                if kind.second:
                    sp.wait_ge(sorted_out, 16 * TB * B)
                if kind.choose:
                    load_w(0)
                    load_x3(0)
            stretches(sp, body)

            store_x3(NC - 2, at_tail)
            load_x2(CB - 1)
            store_post(NC - 1)
            store_x3(NC - 1, at_ffn)
            load_w(1)
            load_x3(CB)
            with sp.Fori(CB, NC - 1) as q:
                load_x2(q)
                load_x3(q + 1)
            load_x2(NC - 1)
            sp.wait_ge(out_stored, 16 * SUB * NC)

        @block.gpsimd
        def _(pool):
            pool.memset(ident[:], 0.0).then_inc(consts_ready, 1)
            pool.memset(ones[:], 1.0).then_inc(consts_ready, 1)
            pool.memset(before[:], 1.0).then_inc(consts_ready, 1)
            pool.memset(prompt[:], 0.0).then_inc(consts_ready, 1)
            pool.memset(carry[:], 0.0).then_inc(consts_ready, 1)
            pool.memset(half[:, 0:SUB], -0.5).then_inc(consts_ready, 1)
            pool.memset(half[:, SUB:SUB + 1], 0.5).then_inc(consts_ready, 1)
            pool.wait_ge(consts_ready, 7)
            pool.affine_select(out=ident[:], in_=ident[:], compare_op=ALU.not_equal, fill=1.0, base=0,
                               pattern=[[-1, P]], channel_multiplier=1).then_inc(consts_ready, 1)
            pool.affine_select(out=before[:], in_=before[:], compare_op=ALU.is_gt, fill=0.0, base=0,
                               pattern=[[1, P]], channel_multiplier=-1).then_inc(consts_ready, 1)
            pool.iota(rank8[:], pattern=[[0, TB], [-1, NB]], base=NB, channel_multiplier=0,
                      allow_small_or_imprecise_dtypes=True).then_inc(consts_ready, 1)
            for b in range(B):
                tags = rows[:, b, :, D:D + 1].bitcast(I32)
                pool.iota(tags, pattern=[[P, TB], [0, 1]], base=b * S, channel_multiplier=1).then_inc(tagged, 1)
            pool.wait_ge(mhat_link, 2)
            pool.tensor_tensor(msq[:, 1:2], msq[:, 0:1], half[0:NB, SUB:SUB + 1], ALU.pow).then_inc(root_ready, 1)

            def sort_tiles(b, lo, hi):
                if lo == 0:
                    pool.wait_ge(pos_ready, b + 1)
                    pool.wait_ge(tagged, B)
                    pool.wait_ge(x_in[b], 64)
                for i in range(lo, hi):
                    pool.indirect_dma_start(xsorted, bass.IndirectOffsetOnAxis(pos[:, b, i:i + 1], 0),
                                            rows[:, b, i, :], None).then_inc(sorted_out, 16)

            sort_tiles(0, 0, TB)

            def acc_init(c):
                pool.wait_ge(xn_ready, c + 1)
                pool.wait_ge(xs_in, 16 * (c + 1))
                if not isinstance(c, int) or c > 2:
                    pool.wait_ge(x2_stored, 16 * (c - 2))
                    pool.wait_ge(xn3_ready, c - 2)
                settle(pool, c)
                a = acc[:, c % 4]
                pool.tensor_tensor(a, xn[:], Dbc[:].rearrange("p (o d) -> p o d", o=1).to_broadcast([P, SUB, D]),
                                   ALU.mult).then_inc(acc_link, 1)
                pool.wait_ge(acc_link, c + 1)
                settle(pool, c)
                pool.tensor_copy(ids[:, bass.ds(c * SUB, SUB)], xs[:, :, D:D + 1].bitcast(U32)
                                 .rearrange("p s o -> p (s o)")).then_inc(ids_link, 1)
                pool.tensor_tensor(a, a, xs[:, :, 0:D], ALU.add).then_inc(acc_ready, 1)

            def du(c):
                pool.wait_ge(dlt_ready, c + 1)
                settle(pool, c)
                pool.tensor_tensor(u[:, c % 2], u[:, c % 2], dlt[:, c % 2], ALU.mult).then_inc(du_ready, 1)

            def invert_root(i, c):
                pool.wait_ge(var_ready[i], c + 1)
                pool.tensor_tensor(rstd[:, i, :], rstd[:, i, :], half[:, 0:SUB], ALU.pow).then_inc(rstd_ready[i], 1)

            invert_root(0, 0)
            acc_init(0)
            du(0)

            def bias_x2(q, b):
                pool.wait_ge(w_in, 160 * (b + 1))
                pool.wait_ge(x2_in, 16 * (q + 1))
                pool.tensor_tensor(x2[:], x2[:], b2[:].rearrange("p (o d) -> p o d", o=1).to_broadcast([P, SUB, D]),
                                   ALU.add).then_inc(x2_biased, 1)

            def scatter(q):
                wait(pool, out_stored, 16 * SUB * q)
                pool.wait_ge(ids_link, NC if isinstance(q, int) and q >= CB else q + 1)
                pool.tensor_copy(ids_now[:], ids[:, bass.ds(q * SUB, SUB)]).then_inc(ids_ready, 1)
                pool.wait_ge(ids_ready, q + 1)
                pool.wait_ge(res_ready, q + 1)
                settle(pool, q)
                for s in range(SUB):
                    pool.indirect_dma_start(t["out"].rearrange("b s d -> (b s) d"),
                                            bass.IndirectOffsetOnAxis(ids_now[:, s:s + 1], 0),
                                            x2[:, s, :], None).then_inc(out_stored, 16)

            def add_out(c, us):
                us.done(pool, "out1")
                pool.wait_ge(xn2_ready, c + 1)
                settle(pool, c)
                pool.tensor_tensor(acc[:, c % 4], acc[:, c % 4], xn23[:], ALU.add).then_inc(x2_ready, 1)

            def body(c, us, kind, batch):
                for n in range(NS):
                    if n % BG == 0:
                        g = n // BG
                        pool.wait_ge(b_in[g % 2], 32 * c + 16 * (g // 2 + 1))
                    if n == 0:
                        pool.wait_ge(du_ready, c + 1)
                    wait(pool, scanned, 2 * NS * c + 2 * (n - DBU_BACK[n] + 1))
                    settle(pool, c)
                    pool.tensor_tensor(dBu[:, DBU_SLOT[n]], u[:, c % 2],
                                       Bs[:, (n // BG) % 2, n % BG, :].rearrange("p (o l) -> p o l", o=1)
                                       .to_broadcast([P, KT, LC]), ALU.mult).then_inc(dBu_ready, 1)
                    if kind.prep and n == AT_POOL["root12"]:
                        invert_root(0, c + 1)
                    if kind.post and n == AT_POOL["root12"]:
                        invert_root(1, c - 1)
                    if kind.post and n == AT_POOL["root3"]:
                        invert_root(2, c - 1)
                    if kind.finish and n == AT_POOL["scatter"]:
                        scatter(c - (CB + 2))
                    if kind.ffn and n == AT_POOL["bias"]:
                        bias_x2(c - (CB + 1), 0)
                    if kind.post and n == AT_POOL["x2"]:
                        add_out(c - 1, us)
                    if kind.prep and n == AT_POOL["acc"]:
                        acc_init(c + 1)
                    if kind.second and 7 <= n < 7 + TB // 2:
                        sort_tiles(1, 2 * (n - 7), 2 * (n - 7) + 2)
                    if kind.prep and n == AT_POOL["du"]:
                        du(c + 1)
            stretches(pool, body)
            invert_root(1, NC - 1)
            scatter(CB - 2)
            bias_x2(CB - 1, 0)
            add_out(NC - 1, tail_uses)
            invert_root(2, NC - 1)
            scatter(CB - 1)
            with pool.Fori(CB, NC) as q:
                bias_x2(q, 1)
                scatter(q)

        @block.scalar
        def _(act):
            def out_of(us, name, dst, view=lambda a: a, func=ACT.Copy, **kw):
                act.activation(dst, view(us.read(act, name)), func, **kw).then_inc(evacuated, 1)

            act.preload_act_table_set("natural_log_exp_and_others")
            us = setup_uses
            act.wait_ge(prep_in, 16 * 8)
            act.activation(A[:], A[:], ACT.Exp).then_inc(a_link, 1)
            act.wait_ge(a_link, 1)
            act.activation(A[:], A[:], ACT.Copy, scale=-1.0).then_inc(a_link, 1)
            act.wait_ge(a_link, 2)
            out_of(us, "mhat", mhatT[:], lambda a: a[:, 0:KT * NB].rearrange("p (k n) -> p k n", k=KT))
            out_of(us, "prompt", prompt[:, XC0:XC0 + NS], lambda a: a[0:NB, 0:NS])

            def fours(a):
                return a.rearrange("p (k n) -> p k n", k=KT)

            def biased(us, name, dst, which):
                a = fours(us.read(act, name))
                for k in range(KT):
                    i = act.activation(dst[:, k, :], a[:, k, :], ACT.Identity, bias=bqkv[:, which, k:k + 1])
                i.then_inc(evacuated, 1)

            def fold(name, us):
                what, b = name[:-1], int(name[-1])
                if name == FOLD_USES[0]:
                    act.wait_ge(fold_in, 16 * 12)
                if what == "keysT":
                    biased(us, name, keysT[:, b], 1)
                elif what == "foldedq":
                    out_of(us, name, foldedq[:, b], fours)
                elif what == "biasq":
                    out_of(us, name, biasq[:, b, :], lambda a: a[0:1, 0:KEYS])
                elif what == "valuesT":
                    biased(us, name, valuesT[:, b], 2)
                else:
                    out_of(us, name, foldedo[:, b, :])

            def raw(b, i, us):
                out_of(us, RAW_USES[b][i], rawT[:, i % 2], fours)

            for i in range(TB):
                raw(0, i, us)

            def read_prep(name, c, us):
                i = int(name[-1]) if name[-1].isdigit() else 0
                if name == "onehot":
                    out_of(us, name, onehot[:], lambda a: a[0:NB, 0:LC])
                elif name in ("uT0", "uT1"):
                    if i == 0:
                        wait(act, dBu_ready, NS * (c - 1))
                    out_of(us, name, u[:, c % 2, 2 * i:2 * i + 2, :], twos)
                elif name == "proj":
                    wait(act, b_stored, 16 * c)
                    out_of(us, name, proj[:], lambda a: a[0:XW, 0:LC])
                elif name in ("delta0", "delta1"):
                    a = twos(us.read(act, name))
                    for k in range(2):
                        j = act.activation(dlt[:, c % 2, 2 * i + k, :], a[:, k, :], ACT.Identity,
                                           bias=bdt[:, 2 * i + k:2 * i + k + 1])
                    j.then_inc(evacuated, 1)
                elif name in ("C0", "C1"):
                    if i == 0:
                        wait(act, hT_used, 2 * NS * (c - 1))
                    out_of(us, name, Cl[:, c % 2, i, :], lambda a: a[:, XC0:XC0 + NS])

            def twos(a):
                return a.rearrange("p (k l) -> p k l", k=2)

            def prep_soft_e(c):
                act.wait_ge(abs_ready, c + 1)
                act.wait_ge(acc_ready, c + 1)
                act.activation(soft_e, soft_l[:], ACT.Exp).then_inc(e_ready, 1)

            def prep_soft_l(c):
                act.wait_ge(e_ready, c + 1)
                act.activation(soft_l[:], soft_e, ACT.Ln, bias=1.0).then_inc(ln_ready, 1)

            def read_post(name, c, us):
                i = int(name[-1]) if name[-1].isdigit() else 0
                if name in ("xn2T0", "xn2T1"):
                    if i == 0:
                        wait(act, x3_stored, 16 * c)
                    out_of(us, name, xnT[:, 2 * i:2 * i + 2, :], twos)
                elif name == "scores":
                    out_of(us, name, prob[:], lambda a: a[:, 0:SUB * KEYS].rearrange("p (s n) -> p s n", s=SUB))
                elif name == "probsT":
                    out_of(us, name, probT[:], lambda a: a[:, 0:LC])
                elif name in ("out0", "out1"):
                    out_of(us, name, xn23[:, i, :])
                elif name in ("xn3T0", "xn3T1"):
                    a = twos(us.read(act, name))
                    for k in range(2):
                        m = 2 * i + k
                        j = act.activation(xnT[:, m, :], a[:, k, :], ACT.Copy, accum_out=msum[:, c, m:m + 1])
                    j.then_inc(evacuated, 1)

            def post_expo(c):
                act.wait_ge(smax_ready, c + 1)
                for s in range(SUB):
                    act.activation(prob[:, s, :], prob[:, s, :], ACT.Exp, bias=pstat[:, 1, s:s + 1], scale=SCALE,
                                   accum_out=pstat[:, 2, s:s + 1]).then_inc(expo_ready, 1)

            def hidden(q, f, us):
                act.activation(hid[:, f % 3, :], us.read(act, f"hidden{f}")[:, 0:LC], ACT.Relu,
                               bias=b1[:, f:f + 1]).then_inc(evacuated, 1)

            for name in PREP_USES:
                read_prep(name, 0, prep0_uses)
            prep_soft_e(0)
            prep_soft_l(0)

            def read_at(n, c, us, kind):
                for name in kind.uses_at(n):
                    if name.startswith("hidden"):
                        if n == 0:
                            act.wait_ge(w_in, 160)
                        hidden(c - (CB + 1), n, us)
                    elif name.startswith("raw"):
                        raw(1, n, us)
                    elif name in FOLD_USES:
                        fold(name, us)
                    elif name in PREP_USES:
                        read_prep(name, c + 1, us)
                    else:
                        read_post(name, c - 1, us)

            def body(c, us, kind, batch):
                act.wait_ge(dlt_ready, c + 1)
                for n in range(NS):
                    for k in range(KT):
                        if k % 2 == 0:
                            wait(act, scanned, 2 * NS * c + 2 * n + k // 2 - 1)
                            settle(act, c)
                        i = act.activation(dA[:, k // 2, (k % 2) * LC:(k % 2 + 1) * LC], dlt[:, c % 2, k, :],
                                           ACT.Exp, scale=A[:, k, n:n + 1])
                        if k % 2 == 1:
                            i.then_inc(dA_ready, 1)
                    if n > 0:
                        save_carry(c, n - 1)
                    if kind.prep and n == AT_ACT["soft_e"]:
                        prep_soft_e(c + 1)
                    if kind.prep and n == AT_ACT["soft_l"]:
                        prep_soft_l(c + 1)
                    if n > 0:
                        read_at(n - 1, c, us, kind)
                    if kind.post and n == AT_ACT["expo"]:
                        post_expo(c - 1)
                save_carry(c, NS - 1)
                read_at(NS - 1, c, us, kind)

            def save_carry(c, n):
                act.wait_ge(scanned, 2 * NS * c + 2 * n + 2)
                settle(act, c)
                act.activation(carry[:, n, :], h[:, n % H_RING, :, LC - 1], ACT.Copy).then_inc(carried, 1)
            stretches(act, body)

            us = tail_uses
            for n in range(NS):
                read_at(n, NC, us, tail_kind)
                if n == AT_ACT["expo"]:
                    post_expo(NC - 1)
            act.wait_ge(w_in, 320)
            with act.Fori(CB, NC) as q:
                us = Uses(at_ffn + (q - CB) * FT, [f"hidden{f}" for f in range(FT)])
                for f in range(FT):
                    hidden(q, f, us)

        @block.vector
        def _(dve):
            V = dve

            def chain(s, base):
                at = [base]

                def link(ins):
                    at[0] = at[0] + 1
                    ins.then_inc(s, 1)
                    dve.wait_ge(s, at[0])
                return link

            dve.wait_ge(prep_in, 16 * 8)
            link = chain(mhat_link, 0)
            link(V.tensor_tensor(mhat[:], means[:], means[:], ALU.mult))
            link(V.tensor_reduce(msq[:, 0:1], mhat[:], AX.X, ALU.add))
            dve.wait_ge(root_ready, 1)
            link(V.tensor_scalar(msq[:, 1:2], msq[:, 1:2], 1e-12, None, ALU.max))
            link(V.reciprocal(msq[:, 2:3], msq[:, 1:2]))
            link(V.tensor_scalar(mhat[:], means[:], msq[:, 2:3], None, ALU.mult))
            link(V.tensor_reduce(msq[:, 0:1], mhat[:], AX.X, ALU.add))
            link(V.tensor_scalar(msq[:, 3:4], msq[:, 0:1], 1.0 / D, None, ALU.mult))
            V.tensor_scalar(mhat[:], mhat[:], msq[:, 3:4], None, ALU.subtract).then_inc(mhat_ready, 1)

            dve.wait_ge(consts_ready, 10)
            sc, eq, oh, tot, inc, tmp = [rt[i].rearrange("p (t k) -> p t k", k=NB) for i in range(6)]
            m1, m2 = rt[6][:, 0:TB], rt[6][:, TB:2 * TB]
            ROUTE_LINKS, PLACE_LINKS = 6, 6

            def spread(m):
                return m.rearrange("p (t o) -> p t o", o=1).to_broadcast([P, TB, NB])

            def route(b):
                link = chain(route_link, b * (ROUTE_LINKS + PLACE_LINKS))
                dve.wait_ge(scored, b + 1)
                link(V.tensor_copy(sc, fo[:, 1, 0:TB * NB].rearrange("p (t k) -> p t k", k=NB)))
                link(V.tensor_reduce(m1, sc, AX.X, ALU.max))
                link(V.tensor_tensor(eq, sc, spread(m1), ALU.is_equal))
                link(V.tensor_tensor(eq, eq, rank8[:], ALU.mult))
                link(V.tensor_reduce(m2, eq, AX.X, ALU.max))
                link(V.tensor_tensor(oh, rank8[:], spread(m2), ALU.is_equal))
                V.tensor_copy(rows[:, b, :, D + 1:ROW], oh).then_inc(onehot_ready, 1)

            def place(b):
                link = chain(route_link, b * (ROUTE_LINKS + PLACE_LINKS) + ROUTE_LINKS)
                dve.wait_ge(counted, b + 1)
                link(V.tensor_copy(rt[3].rearrange("p (k t) -> p k t", k=NB),
                                   fo[:, 0, P:2 * P].rearrange("p (t k) -> p k t", k=NB)))
                link(V.tensor_tensor_scan(rt[4], ones[:], rt[3], 0.0, ALU.mult, ALU.add))
                link(V.tensor_tensor(rt[4], rt[4], rt[3], ALU.subtract))
                link(V.tensor_tensor(tmp, fo[:, 0, 0:P].rearrange("p (t k) -> p t k", k=NB),
                                     rt[4].rearrange("p (k t) -> p t k", k=NB), ALU.add))
                link(V.tensor_tensor(tmp, tmp, oh, ALU.mult))
                link(V.tensor_reduce(m1, tmp, AX.X, ALU.add))
                V.tensor_scalar(pos[:, b, :], m1, float(b * S), None, ALU.add).then_inc(pos_ready, 1)

            route(0)
            place(0)

            def stats(src, i, c):
                link = chain(norm_link[i], 2 * c)
                settle(dve, c)
                for s in range(SUB):
                    j = V.bn_stats(st[:, i, s, :], src[:, s, :])
                link(j)
                settle(dve, c)
                for s in range(SUB):
                    j = V.bn_aggr(mv[:, i, s, :], st[:, i, s, :])
                link(j)
                V.tensor_scalar(rstd[:, i, :], mv[:, i, :, 1], EPS, None, ALU.add).then_inc(var_ready[i], 1)

            def normalise(dst, src, i, c, ready):
                dve.wait_ge(rstd_ready[i], c + 1)
                for s in range(SUB):
                    j = V.tensor_scalar(dst[:, s, :], src[:, s, :], mv[:, i, s, 0:1], rstd[:, i, s:s + 1],
                                        ALU.subtract, ALU.mult)
                j.then_inc(ready, 1)

            def norm1_stats(c):
                dve.wait_ge(xs_in, 16 * (c + 1))
                stats(xs[:, :, 0:D], 0, c)

            def norm1(c):
                wait(dve, acc_ready, c)
                normalise(xn, xs[:, :, 0:D], 0, c, xn_ready)

            def absz(c, us):
                us.done(dve, "delta1")
                wait(dve, dlt_ready, c)
                z = dlt[:, c % 2].rearrange("p k l -> p (k l)")
                V.scalar_tensor_tensor(out=soft_l[:].rearrange("p k l -> p (k l)"), in0=z, scalar=-1.0, in1=z,
                                       op0=ALU.mult, op1=ALU.min).then_inc(abs_ready, 1)

            def softplus(c):
                link = chain(soft_link, 3 * c)
                dve.wait_ge(ln_ready, c + 1)
                z = dlt[:, c % 2].rearrange("p k l -> p (k l)")
                e_, l_ = [v.rearrange("p k l -> p (k l)") for v in (soft_e, soft_l[:])]
                link(V.scalar_tensor_tensor(out=z, in0=z, scalar=0.0, in1=l_, op0=ALU.max, op1=ALU.add))
                link(V.tensor_scalar(l_, e_, 1.0, 1.0, ALU.add, ALU.subtract))
                link(V.tensor_tensor(e_, e_, l_, ALU.subtract))
                V.tensor_tensor(z, z, e_, ALU.add).then_inc(dlt_ready, 1)

            def norm2_stats(c):
                dve.wait_ge(hT_used, 2 * NS * (c + 1))
                stats(acc[:, c % 4], 1, c)

            def norm2(c):
                normalise(xn23, acc[:, c % 4], 1, c, xn2_ready)

            def smax(c, us):
                us.done(dve, "scores")
                V.tensor_reduce(pstat[:, 0, :], prob[:], AX.X, ALU.max).then_inc(smax_link, 1)
                dve.wait_ge(smax_link, c + 1)
                V.tensor_scalar(pstat[:, 1, :], pstat[:, 0, :], -SCALE, None, ALU.mult).then_inc(smax_ready, 1)

            def snorm(c):
                dve.wait_ge(expo_ready, SUB * (c + 1))
                V.reciprocal(pstat[:, 3, :], pstat[:, 2, :]).then_inc(soft_sum, 1)
                dve.wait_ge(soft_sum, c + 1)
                V.tensor_tensor(prob[:], prob[:], pstat[:, 3, :].rearrange("p (s o) -> p s o", o=1)
                                .to_broadcast([P, SUB, KEYS]), ALU.mult).then_inc(probs_ready, 1)

            def norm3_stats(c):
                dve.wait_ge(x2_ready, c + 1)
                stats(acc[:, c % 4], 2, c)

            def norm3(c):
                normalise(xn23, acc[:, c % 4], 2, c, xn3_ready)

            def finish(q):
                dve.wait_ge(ffn_ready, q + 1)
                dve.wait_ge(x2_biased, q + 1)
                for s in range(SUB):
                    j = V.tensor_tensor(x2[:, s, :], fo[:, s, :], x2[:, s, :], ALU.add)
                j.then_inc(res_ready, 1)

            def choose(b, us):
                us.done(dve, "xn3T1")
                V.tensor_reduce(mean[:], msum[:, b * CB:(b + 1) * CB, :].rearrange("p c k -> p k c"), AX.X,
                                ALU.add).then_inc(mean_link, 1)
                dve.wait_ge(mean_link, b + 1)
                V.tensor_scalar(mean[:], mean[:], 1.0 / S, None, ALU.mult).then_inc(mean_ready, 1)
                dve.wait_ge(voted, b + 1)
                link = chain(vote_link, 5 * b)
                link(V.tensor_tensor(vote[:, 0, :], fo[0:1, 0, 0:NE], br[:], ALU.add))
                link(V.tensor_reduce(vote[:, 1, 0:1], vote[:, 0, :], AX.X, ALU.max))
                link(V.tensor_scalar(vote[:, 2, :], vote[:, 0, :], vote[:, 1, 0:1], None, ALU.is_equal))
                link(V.tensor_tensor(vote[:, 2, :], vote[:, 2, :], rank8[0:1, 0, :], ALU.mult))
                link(V.tensor_reduce(vote[:, 3, 0:1], vote[:, 2, :], AX.X, ALU.max))
                V.tensor_scalar(expert[:, 0:1], vote[:, 3, 0:1], -1.0, float(NE), ALU.mult, ALU.add
                                ).then_inc(expert_ready, 1)

            norm1_stats(0)
            norm1(0)
            absz(0, prep0_uses)
            softplus(0)

            def body(c, us, kind, batch):
                def rows_of(n, j):
                    use = 2 * NS * c + 2 * n + j
                    dve.wait_ge(hT_ready, use + 1)
                    if n == 0:
                        dve.wait_ge(acc_ready, c + 1)
                    else:
                        dve.wait_ge(hT_used, use - 1)
                    a = acc[:, c % 4, j, :]
                    V.scalar_tensor_tensor(out=a, in0=hT[:, j, :], scalar=Cl[:, c % 2, j, n:n + 1], in1=a,
                                           op0=ALU.mult, op1=ALU.add).then_inc(hT_used, 1)

                if kind.choose:
                    dve.wait_ge(carried, NS * c)
                    V.memset(carry[:], 0.0).then_inc(carry_zeroed, 1)
                    dve.wait_ge(carry_zeroed, 1)
                if kind.prep:
                    norm1_stats(c + 1)
                if kind.post:
                    norm2_stats(c - 1)
                for n in range(NS):
                    for k in range(KT):
                        if k % 2 == 0:
                            dve.wait_ge(dA_ready, 2 * NS * c + 2 * n + k // 2 + 1)
                        if k == 0:
                            dve.wait_ge(dBu_ready, NS * c + n + 1)
                            wait(dve, hT_ready, 2 * NS * c + 2 * (n - H_RING + 1))
                            wait(dve, carried, NS * c + n - H_RING + 1)
                        j = V.tensor_tensor_scan(h[:, n % H_RING, k, :], dA[:, k // 2, (k % 2) * LC:(k % 2 + 1) * LC],
                                                 dBu[:, DBU_SLOT[n], k, :], carry[:, n, k:k + 1], ALU.mult, ALU.add)
                        if k % 2 == 1:
                            j.then_inc(scanned, 1)
                            if n > 1:
                                rows_of(n - 2, k // 2)
                    if kind.finish and n == AT_DVE["finish"]:
                        finish(c - (CB + 2))
                    if kind.prep and n == AT_DVE["norm1"]:
                        norm1(c + 1)
                    if kind.post and n == AT_DVE["norm2"]:
                        norm2(c - 1)
                    if kind.second and n == AT_DVE["route"]:
                        route(1)
                    if kind.second and n == AT_DVE["place"]:
                        place(1)
                    if kind.post and n == AT_DVE["max"]:
                        smax(c - 1, us)
                    if kind.post and n == AT_DVE["normal"]:
                        snorm(c - 1)
                    if kind.prep and n == AT_DVE["abs"]:
                        absz(c + 1, us)
                    if kind.prep and n == AT_DVE["softplus"]:
                        softplus(c + 1)
                    if kind.post and n == AT_DVE["stats3"]:
                        norm3_stats(c - 1)
                    if kind.post and n == AT_DVE["norm3"]:
                        norm3(c - 1)
                    if kind.choose and n == AT_DVE["choose"]:
                        choose(0, us)
                for n in range(NS - 2, NS):
                    for j in range(SUB):
                        rows_of(n, j)
            stretches(dve, body)

            us = tail_uses
            finish(CB - 2)
            norm2_stats(NC - 1)
            norm2(NC - 1)
            smax(NC - 1, us)
            snorm(NC - 1)
            norm3_stats(NC - 1)
            norm3(NC - 1)
            finish(CB - 1)
            choose(1, us)
            with dve.Fori(CB, NC) as q:
                finish(q)

        @block.tensor
        def _(pe):
            us = setup_uses
            pe.wait_ge(prep_in, 16 * 8)
            pe.wait_ge(consts_ready, 10)
            pe.wait_ge(mhat_ready, 1)
            w = us.fill(pe, "mhat")
            for k in range(KT):
                i = pe.transpose(w[:, k * NB:(k + 1) * NB], mhat[:, k * P:(k + 1) * P], ident[0:NB, 0:NB])
            i.then_inc(filled, 1)

            def product(out, lhs, rhs, lo=0, hi=None):
                n = len(lhs)
                for i in range(lo, n if hi is None else hi):
                    j = pe.matmul(out, lhs[i], rhs[i], start=(i == 0), stop=(i == n - 1))
                return j

            w = us.fill(pe, "prompt")
            product(w[0:NB, 0:NS], [meansT[:, k, :] for k in range(KT)], [promptT[:, k, :] for k in range(KT)]
                    ).then_inc(filled, 1)

            def fold(name, us):
                what, b = name[:-1], int(name[-1])
                if name == FOLD_USES[0]:
                    pe.wait_ge(fold_in, 16 * 12)
                ctx_k = [ctxT[:, b, k, :] for k in range(KT)]
                keys_k = [keysT[:, b, k, :] for k in range(KT)]
                w = us.fill(pe, name)
                if what in ("keysT", "foldedq", "valuesT"):
                    weight, moving = {"keysT": (wk, ctx_k), "foldedq": (wq, keys_k), "valuesT": (wv, ctx_k)}[what]
                    if what == "foldedq":
                        us.done(pe, f"keysT{b}")
                    for m in range(KT):
                        i = product(w[:, m * P:(m + 1) * P], [weight[:, k, m * P:(m + 1) * P] for k in range(KT)], moving)
                elif what == "biasq":
                    i = product(w[0:1, 0:KEYS], [bqkv[:, 0, k:k + 1] for k in range(KT)], keys_k)
                else:
                    us.done(pe, f"valuesT{b}")
                    i = product(w, [valuesT[:, b, k, :] for k in range(KT)] + [ones[0:1, :]],
                                [wo[:, k, :] for k in range(KT)] + [bo[:]])
                i.then_inc(filled, 1)

            def raw(b, i, us):
                w = us.fill(pe, RAW_USES[b][i])
                for k in range(KT):
                    j = pe.transpose(w[:, k * P:(k + 1) * P], rows[:, b, i, k * P:(k + 1) * P], ident[:])
                j.then_inc(filled, 1)

            def score(b, i, number):
                pe.wait_ge(evacuated, number + 1)
                j = product(fo[:, 1, i * NB:(i + 1) * NB], [rawT[:, i % 2, k, :] for k in range(KT)],
                            [mhatT[:, k, :] for k in range(KT)])
                if i == TB - 1:
                    j.then_inc(scored, 1)

            def count(b):
                pe.wait_ge(onehot_ready, b + 1)
                pe.matmul(fo[:, 0, 0:P], before[:], rt[2], start=True, stop=True)
                pe.matmul(fo[:, 0, P:2 * P], ones[:], rt[2], start=True, stop=True).then_inc(counted, 1)

            pe.wait_ge(x_in[0], 64)
            for i in range(TB):
                raw(0, i, us)
                if i > 0:
                    score(0, i - 1, SETUP_USES.index(RAW_USES[0][i - 1]))
            score(0, TB - 1, SETUP_USES.index(RAW_USES[0][TB - 1]))
            count(0)

            def turn(us, name, src):
                w = us.fill(pe, name)
                i = int(name[-1])
                for k in range(2):
                    for s in range(SUB):
                        m = 2 * i + k
                        j = pe.transpose(w[:, k * LC + s * P:k * LC + (s + 1) * P], src[:, s, m * P:(m + 1) * P], ident[:])
                j.then_inc(filled, 1)

            def fill_prep(name, c, us):
                i = int(name[-1]) if name[-1].isdigit() else 0
                if name == "onehot":
                    pe.wait_ge(xs_in, 16 * (c + 1))
                    w = us.fill(pe, name)
                    settle(pe, us.base)
                    for s in range(SUB):
                        j = pe.matmul(w[0:NB, s * P:(s + 1) * P], xs[:, s, D + 1:ROW], ident[:], start=True, stop=True)
                    j.then_inc(filled, 1)
                elif name in ("uT0", "uT1"):
                    pe.wait_ge(xn_ready, c + 1)
                    turn(us, name, xn)
                elif name == "proj":
                    us.done(pe, "uT1")
                    w = us.fill(pe, name)
                    product(w[0:XW, 0:LC], [wx[:, k, :] for k in range(KT)] + [prompt[:]],
                            [u[:, c % 2, k, :] for k in range(KT)] + [onehot[:]]).then_inc(filled, 1)
                elif name in ("delta0", "delta1"):
                    us.done(pe, "proj")
                    w = us.fill(pe, name)
                    for k in range(2):
                        m = 2 * i + k
                        j = pe.matmul(w[:, k * LC:(k + 1) * LC], wdt[:, m * P:(m + 1) * P], proj[0:R, :], start=True, stop=True)
                    j.then_inc(filled, 1)
                elif name in ("C0", "C1"):
                    w = us.fill(pe, name)
                    settle(pe, us.base)
                    pe.transpose(w[:, 0:XB0], proj[0:XB0, i * P:(i + 1) * P], ident[0:XB0, 0:XB0]).then_inc(filled, 1)

            def fill_post(name, c, us, b):
                if name in ("xn2T0", "xn2T1"):
                    pe.wait_ge(xn2_ready, c + 1)
                    turn(us, name, xn23)
                elif name in ("xn3T0", "xn3T1"):
                    pe.wait_ge(xn3_ready, c + 1)
                    turn(us, name, xn23)
                elif name == "scores":
                    us.done(pe, "xn2T1")
                    w = us.fill(pe, name)
                    for s in range(SUB):
                        j = product(w[:, s * KEYS:(s + 1) * KEYS],
                                    [xnT[:, k, s * P:(s + 1) * P] for k in range(KT)] + [ones[0:1, :]],
                                    [foldedq[:, b, k, :] for k in range(KT)] + [biasq[:, b, :]])
                    j.then_inc(filled, 1)
                elif name == "probsT":
                    pe.wait_ge(probs_ready, c + 1)
                    w = us.fill(pe, name)
                    for s in range(SUB):
                        j = pe.transpose(w[:, s * P:(s + 1) * P], prob[:, s, :], ident[:])
                    j.then_inc(filled, 1)
            def out_terms(us, name, b, lo, hi):
                t, n = int(name[-1]), KT + 1
                if lo == 0:
                    us.done(pe, "probsT")
                    us.fill(pe, name)
                j = product(us.bank(name), [xnT[:, k, t * P:(t + 1) * P] for k in range(KT)] + [probT[:, t * P:(t + 1) * P]],
                            [wo[:, k, :] for k in range(KT)] + [foldedo[:, b, :]], lo, hi)
                if hi == n:
                    j.then_inc(filled, 1)

            def first_product(q, f, us):
                w = us.fill(pe, f"hidden{f}")
                product(w[:, 0:LC], [w1[:, k, f * P:(f + 1) * P] for k in range(KT)],
                        [x3[:, q % 2, k, :] for k in range(KT)]).then_inc(filled, 1)

            def second_product(q, f, us):
                us.done(pe, f"hidden{f}")
                if f == 0:
                    wait(pe, res_ready, q)
                for s in range(SUB):
                    j = pe.matmul(fo[:, s, :], hid[:, f % 3, s * P:(s + 1) * P], w2[:, f, :],
                                  start=(f == 0), stop=(f == FT - 1))
                if f == FT - 1:
                    j.then_inc(ffn_ready, 1)

            def vote_for(b):
                pe.wait_ge(mean_ready, b + 1)
                product(fo[0:1, 0, 0:NE], [mean[:, k:k + 1] for k in range(KT)], [wr[:, k, :] for k in range(KT)]
                        ).then_inc(voted, 1)

            for name in PREP_USES:
                fill_prep(name, 0, prep0_uses)

            def fill_at(n, half, c, us, b, kind):
                names = [name for name in kind.slots(n) if name not in ("out0", "out1")]
                for name in names[0:1] if half == 0 else names[1:]:
                    if name in PREP_USES:
                        fill_prep(name, c + 1, us)
                    else:
                        fill_post(name, c - 1, us, b)
                part = (OUT_TIGHT if kind.ffn else OUT_SPREAD).get((n, half))
                if part and kind.post:
                    name, lo, hi = part
                    out_terms(us, name, b, lo, hi)

            def body(c, us, kind, batch):
                def turn_h(n, j):
                    use = 2 * NS * c + 2 * n + j
                    if j == 0:
                        pe.wait_ge(scanned, 2 * NS * c + 2 * n + 2)
                    wait(pe, hT_used, use - 1)
                    for k in range(KT):
                        i = pe.transpose(hT[:, j, k * P:(k + 1) * P], h[:, n % H_RING, k, j * P:(j + 1) * P], ident[:])
                    i.then_inc(hT_ready, 1)

                q = c - (CB + 1)
                for n in range(NS):
                    if n > 0:
                        turn_h(n - 1, 0)
                    if kind.ffn:
                        if n == 0:
                            pe.wait_ge(w_in, 160)
                            pe.wait_ge(x3_in, 16 * (q + 1))
                        first_product(q, n, us)
                    if kind.first:
                        raw(1, n, us)
                    fill_at(n, 0, c, us, batch, kind)
                    if n > 0:
                        turn_h(n - 1, 1)
                        if kind.ffn:
                            second_product(q, n - 1, us)
                    if kind.first and n > 0:
                        score(1, n - 1, us.base + us.names.index(RAW_USES[1][n - 1]))
                    if kind.second and n == 0:
                        score(1, TB - 1, last_raw)
                    if kind.second and n == AT_DVE["route"] + 1:
                        count(1)
                    fill_at(n, 1, c, us, batch, kind)
                    if kind.first and 1 <= n <= len(FOLD_USES):
                        fold(FOLD_USES[n - 1], us)
                    if kind.choose and n == AT_DVE["choose"]:
                        vote_for(0)
                for j in range(SUB):
                    turn_h(NS - 1, j)
                if kind.ffn:
                    second_product(q, FT - 1, us)

            last_raw = at_it0 + STRETCH[0][1].uses().index(RAW_USES[1][TB - 1])
            stretches(pe, body)

            us = tail_uses
            q = CB - 1
            pe.wait_ge(x3_in, 16 * (q + 1))
            for n in range(NS):
                first_product(q, n, us)
                if n > 0:
                    second_product(q, n - 1, us)
                for half in range(2):
                    fill_at(n, half, NC, us, 1, tail_kind)
            second_product(q, FT - 1, us)
            pe.wait_ge(res_ready, CB)
            vote_for(1)
            pe.wait_ge(w_in, 320)
            with pe.Fori(CB, NC) as q:
                us = Uses(at_ffn + (q - CB) * FT, [f"hidden{f}" for f in range(FT)])
                pe.wait_ge(x3_in, 16 * (q + 1))
                for f in range(FT):
                    first_product(q, f, us)
                    if f > 0:
                        second_product(q, f - 1, us)
                second_product(q, FT - 1, us)


def kernel(x, ctx_1024, L0_attn_means, L0_attn_prompt_weight, L0_attn_x_proj_weight, L0_attn_dt_projs_weight,
           L0_attn_dt_projs_bias, L0_attn_A_logs, L0_attn_Ds, L0_xattn_Wq, L0_xattn_bq, L0_xattn_Wk, L0_xattn_bk,
           L0_xattn_Wv, L0_xattn_bv, L0_xattn_Wo, L0_xattn_bo, L0_ffn_Wr, L0_ffn_br, L0_ffn_W1, L0_ffn_b1,
           L0_ffn_W2, L0_ffn_b2):
    import concourse.bacc as bacc
    from concourse.bass_utils import run_bass_kernel_spmd

    def tiles(v):
        return np.ascontiguousarray(np.asarray(v).reshape(-1, P).T)

    def turned(m):
        return np.ascontiguousarray(np.asarray(m).T)

    xp = np.asarray(L0_attn_x_proj_weight)
    wx = np.zeros((D, XW), xp.dtype)
    wx[:, 0:R] = xp[0:R].T
    wx[:, XC0:XC0 + NS] = xp[R + NS:].T
    wx[:, XB0:XB0 + NS] = xp[R:R + NS].T
    arrays = {
        "x": np.ascontiguousarray(x), "ctxT": np.ascontiguousarray(np.asarray(ctx_1024).transpose(0, 2, 1)),
        "means": np.ascontiguousarray(L0_attn_means), "meansT": turned(L0_attn_means),
        "promptT": turned(L0_attn_prompt_weight), "wx": wx, "wdt": turned(L0_attn_dt_projs_weight),
        "bdt": tiles(L0_attn_dt_projs_bias), "A_logs": np.ascontiguousarray(L0_attn_A_logs),
        "Ds": np.ascontiguousarray(L0_attn_Ds),
        "Wq": np.ascontiguousarray(L0_xattn_Wq), "WkT": turned(L0_xattn_Wk), "WvT": turned(L0_xattn_Wv),
        "WoT": turned(L0_xattn_Wo), "bq": tiles(L0_xattn_bq), "bk": tiles(L0_xattn_bk), "bv": tiles(L0_xattn_bv),
        "bo": np.ascontiguousarray(L0_xattn_bo), "Wr": np.ascontiguousarray(L0_ffn_Wr),
        "br": np.ascontiguousarray(L0_ffn_br), "W1": np.ascontiguousarray(L0_ffn_W1),
        "b1": np.ascontiguousarray(np.asarray(L0_ffn_b1).reshape(NE, FT, P).transpose(0, 2, 1)),
        "W2": np.ascontiguousarray(L0_ffn_W2), "b2": np.ascontiguousarray(L0_ffn_b2),
    }
    nc = bacc.Bacc("TRN2", target_bir_lowering=False, num_devices=1)
    t = {n: nc.dram_tensor(f"in_{n}", a.shape, mybir.dt.from_np(a.dtype), kind="ExternalInput").ap()
         for n, a in arrays.items()}
    t["out"] = nc.dram_tensor("out_x", (B, S, D), F32, kind="ExternalOutput").ap()
    build(nc, t)
    r = run_bass_kernel_spmd(nc, [{f"in_{n}": a for n, a in arrays.items()}], core_ids=[0])
    return r.results[0]["out_x"]
```

```python
from contextlib import ExitStack

import numpy as np
import concourse.bass as bass
from concourse import mybir

F32 = mybir.dt.float32
F32R = mybir.dt.float32r
I32 = mybir.dt.int32
U32 = mybir.dt.uint32
ALU = mybir.AluOpType
ACT = mybir.ActivationFunctionType
AX = mybir.AxisListType

P = 128
B, S, D = 2, 2048, 512
KT = D // P
NS, R = 16, 32
NB = 8
NE, FF = 8, 2048
FT = FF // P
KEYS = 128
LC = 256
SUB = LC // P
CB = S // LC
NC = B * CB
TB = S // P
ROW = D + 1 + NB
XC0, XB0 = 32, 64
XW = XB0 + NS
BG = 4
EPS = 1e-5
SCALE = D ** -0.5

RAW_USES = [[f"raw{b}_{i}" for i in range(TB)] for b in range(B)]
SETUP_USES = ["mhat", "prompt"] + RAW_USES[0]
FOLD_USES = [f"{n}{b}" for b in range(B) for n in ("keysT", "foldedq", "biasq", "valuesT", "foldedo")]
SLOTS = {0: ["onehot"], 1: ["uT0"], 2: ["uT1", "xn2T0"], 3: ["xn2T1"], 4: ["scores"], 5: ["proj"], 6: ["delta0"],
         7: ["delta1", "probsT"], 9: ["out0"], 10: ["out1"], 11: ["C0"], 12: ["C1"], 15: ["xn3T0", "xn3T1"]}
AT_ACT = {"norm1": 0, "norm2": 1, "expo": 6, "soft_e": 9, "soft_l": 10, "norm3": 14}
AT_DVE = {"finish": 0, "norm1": 0, "norm2": 1, "norm3": 14, "max": 5, "normal": 6, "abs": 8,
          "softplus": 10, "stats3": 12, "route": 1, "place": 4}
AT_POOL = {"root12": 2, "scatter": 3, "acc": 4, "bias": 9, "x2": 13, "du": 14, "root3": 15}
OUT_SPREAD = {(8, 0): ("out0", 0, 2), (8, 1): ("out0", 2, 3), (9, 0): ("out0", 3, 5),
              (9, 1): ("out1", 0, 2), (10, 0): ("out1", 2, 3), (10, 1): ("out1", 3, 5)}
OUT_TIGHT = {(9, 0): ("out0", 0, 3), (9, 1): ("out0", 3, 5), (10, 0): ("out1", 0, 3), (10, 1): ("out1", 3, 5)}
SLOTS_CHOOSE = {0: ["onehot"], 2: ["xn2T0", "xn2T1"], 3: ["scores"], 4: ["uT0"], 5: ["uT1", "probsT"], 6: ["out0"],
                7: ["proj", "out1"], 9: ["delta0"], 10: ["delta1", "xn3T0"], 11: ["xn3T1"], 12: ["C0"], 13: ["C1"]}
OUT_CHOOSE = {(6, 0): ("out0", 0, 3), (6, 1): ("out0", 3, 5), (7, 0): ("out1", 0, 5)}
CHOOSE_ACT = {"expo": 4, "soft_e": 12, "soft_l": 13}
CHOOSE_DVE = {"max": 3, "normal": 4, "abs": 11, "softplus": 13, "stats3": 8, "norm3": 9, "mean": 12, "choose": 13}
CHOOSE_POOL = {"x2": 9, "root3": 10, "acc": 4, "du": 15}
TAIL_SLOTS = {1: ["xn2T0", "xn2T1"], 2: ["scores"], 3: ["probsT"], 4: ["out0", "out1"], 6: ["xn3T0", "xn3T1"]}
TAIL_OUT = {(4, 0): ("out0", 0, 5), (4, 1): ("out1", 0, 5)}
TAIL_EXPO, TAIL_VOTE = 2, 7
H_RING = 4
DBU_SLOT = [n % 3 for n in range(NS - 1)] + [1]
DBU_BACK = [next(i for i in range(1, NS) if DBU_SLOT[n - i] == DBU_SLOT[n]) for n in range(NS)]
PREP_USES = ["onehot", "uT0", "uT1", "proj", "delta0", "delta1", "C0", "C1"]


class Kind:
    def __init__(self, first=False, second=False, prep=True, post=True, ffn=False, finish=False, choose=False,
                 tail=False, fast=False):
        self.first, self.second, self.choose = first, second, choose
        self.act_norms = not (choose or ffn or tail)
        self.tail, self.fast = tail, fast
        self.places = TAIL_SLOTS if tail else SLOTS_CHOOSE if choose else SLOTS
        self.out = TAIL_OUT if tail else OUT_CHOOSE if choose else OUT_TIGHT if ffn else OUT_SPREAD
        self.act, self.dve, self.pool = (({**a, **b} if choose else a) for a, b in
                                         ((AT_ACT, CHOOSE_ACT), (AT_DVE, CHOOSE_DVE), (AT_POOL, CHOOSE_POOL)))
        self.prep, self.post, self.ffn, self.finish = prep, post, ffn, finish

    def slots(self, n):
        return [u for u in self.places.get(n, []) if (self.prep if u in PREP_USES else self.post)]

    def uses_at(self, n):
        return ([f"hidden{n}"] if self.ffn else []) + ([RAW_USES[1][n]] if self.first else []) + self.slots(n) + \
            ([FOLD_USES[n - 1]] if self.first and 1 <= n <= len(FOLD_USES) else [])

    def uses(self):
        return [u for n in range(NS) for u in self.uses_at(n)]


STRETCH = [((0, 1), Kind(first=True, post=False)), ((1, 2), Kind(second=True)), ((2, CB), Kind(fast=True)),
           ((CB, CB + 1), Kind(choose=True)), ((CB + 1, CB + 2), Kind(ffn=True)),
           ((CB + 2, CB + 3), Kind(ffn=True, finish=True)), ((CB + 3, NC - 1), Kind(ffn=True, finish=True)),
           ((NC - 1, NC), Kind(prep=False, ffn=True, finish=True))]


def build(nc, t):
    with ExitStack() as ctx:
        def sb(name, shape, dt=F32):
            return ctx.enter_context(nc.sbuf_tensor(name, shape, dt))

        def ps(name, shape):
            return ctx.enter_context(nc.psum_tensor(name, shape, F32))

        def sem(name):
            return ctx.enter_context(nc.semaphore(name))

        def dram(name, shape, dt=F32):
            return nc.dram_tensor(name, shape, dt, kind="Internal").ap()

        def aligned():
            return -(-nc.sbuf_base // 32) * 32

        xsorted = dram("xsorted", (B * S, ROW))
        b_rows = dram("b_rows", (NC, NS, LC))
        x2_dram = dram("x2_dram", (NC, P, SUB * D))
        x3_dram = dram("x3_dram", (NC, P, KT * LC))

        big_at = aligned()
        big = sb("big", [P, B * TB * ROW])
        rows = big[:].rearrange("p (b t r) -> p b t r", b=B, t=TB)
        w1 = big[:, 0:KT * FF].rearrange("p (k f) -> p k f", k=KT)
        w2 = big[:, KT * FF:KT * FF + FT * D].rearrange("p (f d) -> p f d", f=FT)

        ident = sb("ident", [P, P])
        ones = sb("ones", [P, P])
        before = sb("before", [P, P])
        rank8 = sb("rank8", [P, TB, NB])
        means = sb("means", [NB, D])
        meansT = sb("meansT", [P, KT, NB])
        mhat = sb("mhat", [NB, D])
        mhatT = sb("mhatT", [P, KT, NB])
        msq = sb("msq", [NB, 4])
        promptT = sb("promptT", [P, KT, NS])
        prompt = sb("prompt", [NB, XW])
        wx = sb("wx", [P, KT, XW])
        wdt = sb("wdt", [R, D])
        bdt = sb("bdt", [P, KT])
        A = sb("A", [P, KT, NS])
        Dbc = sb("Dbc", [P, D])
        wo_at = aligned()
        wo = sb("wo", [P, KT, D])
        bqkv = sb("bqkv", [P, 3, KT])
        bo = sb("bo", [1, D])
        wr = sb("wr", [P, KT, NE])
        br = sb("br", [1, NE])
        foldedq = sb("foldedq", [P, B, KT, KEYS])
        biasq = sb("biasq", [1, B, KEYS])
        foldedo_at = aligned()
        foldedo = sb("foldedo", [P, B, D])

        scan_at = aligned()
        xs = sb("xs", [P, SUB, ROW])
        xn = sb("xn", [P, SUB, D])
        soft_e = xn[:].rearrange("p s (a l) -> p (s a) l", l=LC)
        u = sb("u", [P, 2, KT, LC])
        dlt = sb("dlt", [P, 2, KT, LC])
        soft_l = sb("soft_l", [P, KT, LC])
        Bs = sb("Bs", [P, 2, BG, LC])
        dBu = sb("dBu", [P, 3, KT, LC])
        h = sb("h", [P, H_RING, KT, LC])
        W_FLOATS = KT * FF + FT * D
        assert nc.sbuf_base - scan_at >= 4 * W_FLOATS
        half = sb("half", [P, SUB + 1])
        st = sb("st", [P, 3, SUB, 6])
        mv = sb("mv", [P, 3, SUB, 2])
        rstd = sb("rstd", [P, 3, SUB])
        shift = sb("shift", [P, 3, SUB])
        acc_at = aligned()
        acc = sb("acc", [P, 4, SUB, D])
        onehot = sb("onehot", [NB, LC])
        proj = sb("proj", [XW, LC])
        Cl = sb("Cl", [P, 2, SUB, NS])
        carry = sb("carry", [P, NS, KT])
        ids = sb("ids", [P, NC * SUB], U32)
        ids_now = sb("ids_now", [P, SUB], U32)

        xn23_at = aligned()
        xn23 = sb("xn23", [P, SUB, D])
        xnT = sb("xnT", [P, KT, LC])
        prob = sb("prob", [P, SUB, KEYS])
        pstat = sb("pstat", [P, 4, SUB])
        probT = sb("probT", [P, SUB * P])
        msum = sb("msum", [P, NC, KT])

        x3 = sb("x3", [P, 2, KT, LC])
        x2 = sb("x2", [P, SUB, D])
        hid = sb("hid", [P, 3, LC])
        b1 = sb("b1", [P, FT])
        b2 = sb("b2", [P, D])
        mean = sb("mean", [P, KT])
        vote = sb("vote", [1, 4, NE])
        expert = sb("expert", [1, 4], I32)

        SPAN = KT * (LC + 1)
        dA_long, dBu_long, h_long = [big[:, i * 4 * SPAN:(i + 1) * 4 * SPAN].rearrange("p (n s) -> p n s", n=4)
                                     for i in range(3)]

        def tiles_of(a, n):
            return a[:, n % 4, :].rearrange("p (k l) -> p k l", k=KT)

        def h_of(kind, n):
            return tiles_of(h_long, n)[:, :, 1:] if kind.fast else h[:, n % H_RING]

        free = big[:, 0:TB * ROW]
        wq, wk, wv = [free[:, i * KT * D:(i + 1) * KT * D].rearrange("p (k d) -> p k d", k=KT) for i in range(3)]
        keysT, valuesT = [free[:, 3 * KT * D + i * B * KT * KEYS:3 * KT * D + (i + 1) * B * KT * KEYS]
                          .rearrange("p (b k n) -> p b k n", b=B, k=KT) for i in range(2)]
        x3flat = x3[:].rearrange("p a k l -> p (a k l)")
        ctxT = x3flat[:, 0:B * KT * KEYS].rearrange("p (b k n) -> p b k n", b=B, k=KT)
        rawT = x3flat[:, B * KT * KEYS:].rearrange("p (a k n) -> p a k n", a=2, k=KT)
        rt = [x2[:].rearrange("p s d -> p (s d)")[:, i * P:(i + 1) * P] for i in range(7)]
        pos = sb("pos", [P, B, TB], U32)

        def over(name, shape, at, dt=F32R):
            return nc.alloc_sbuf_tensor_at(name, shape, dt, offset=at)

        def two_weights(w):
            return (w[:, 0:KT * FF].rearrange("p (k f) -> p k f", k=KT), w[:, KT * FF:].rearrange("p (f d) -> p f d", f=FT))

        w1_raw, w2_raw = two_weights(over("w_raw", [P, W_FLOATS], scan_at, F32))
        w1_high, w2_high = two_weights(over("w_high", [P, W_FLOATS], big_at))
        w1_low, w2_low = two_weights(over("w_low", [P, W_FLOATS], scan_at))
        x3_high = over("x3_high", [P, 2, KT, LC], acc_at)
        x3_low = over("x3_low", [P, 2, KT, LC], acc_at + 4 * 2 * KT * LC)
        hid_raw = over("hid_raw", [P, 4, LC], foldedo_at, F32)
        hid_high = over("hid_high", [P, 4, LC], xn23_at)
        hid_low = over("hid_low", [P, 4, LC], wo_at)

        dA = ps("dA", [P, 2, 2 * LC])
        hT = ps("hT", [P, 2, D])
        work = ps("work", [P, 2, 512])
        fo = ps("fo", [P, 2, D])

        def turned_h(kind, n, j):
            return (dA if kind.fast and n % 2 else hT)[:, j]

        means_in, prep_in, fold_in = sem("means_in"), sem("prep_in"), sem("fold_in")
        x_in = [[sem(f"x_in{b}_{i}") for i in range(4)] for b in range(B)]
        consts_ready = sem("consts_ready")
        root_ready = sem("root_ready")
        var_ready = [sem(f"var{i}_ready") for i in (1, 2, 3)]
        rstd_ready = [sem(f"rstd{i}_ready") for i in (1, 2, 3)]
        mhat_link, mhat_ready = sem("mhat_link"), sem("mhat_ready")
        filled, evacuated = sem("filled"), sem("evacuated")
        a_link = sem("a_link")
        scored = sem("scored")
        route_link, onehot_ready, counted = sem("route_link"), sem("onehot_ready"), sem("counted")
        pos_ready, tagged, sorted_out = sem("pos_ready"), sem("tagged"), sem("sorted_out")
        xs_in = sem("xs_in")
        shift_link = [sem(f"shift{i}_link") for i in (1, 2, 3)]
        norm_link = [sem(f"norm{i}_link") for i in (1, 2, 3)]
        xn_ready, xn2_ready, xn3_ready = sem("xn_ready"), sem("xn2_ready"), sem("xn3_ready")
        acc_link, acc_ready = sem("acc_link"), sem("acc_ready")
        abs_ready, e_ready, ln_ready = sem("abs_ready"), sem("e_ready"), sem("ln_ready")
        soft_link, dlt_ready, du_ready = sem("soft_link"), sem("dlt_ready"), sem("du_ready")
        b_stored, b_in = sem("b_stored"), [sem(f"b_in{i}") for i in range(2)]
        dA_ready, dBu_ready, scanned = sem("dA_ready"), sem("dBu_ready"), sem("scanned")
        hT_ready, hT_used, carried = sem("hT_ready"), sem("hT_used"), sem("carried")
        carry_zeroed = sem("carry_zeroed")
        long_ready = sem("long_ready")
        smax_ready, expo_ready = sem("smax_ready"), sem("expo_ready")
        soft_sum, probs_ready = sem("soft_sum"), sem("probs_ready")
        smax_link = sem("smax_link")
        x2_ready, x2_stored, x3_stored = sem("x2_ready"), sem("x2_stored"), sem("x3_stored")
        mean_link, mean_ready, voted = sem("mean_link"), sem("mean_ready"), sem("voted")
        vote_link, expert_ready = sem("vote_link"), sem("expert_ready")
        w_in, b12_in = [sem(f"w_in{i}") for i in range(FT // 2)], sem("b12_in")
        w_high_ready, w_low_ready = sem("w_high_ready"), sem("w_low_ready")
        x3_high_ready, x3_low_ready, hid_low_ready = sem("x3_high_ready"), sem("x3_low_ready"), sem("hid_low_ready")
        x3_in, x2_in, x2_biased = sem("x3_in"), sem("x2_in"), sem("x2_biased")
        ffn_ready, res_ready = sem("ffn_ready"), sem("res_ready")
        ids_link, ids_ready, out_stored = sem("ids_link"), sem("ids_ready"), sem("out_stored")

        def wait(eng, s, value):
            if not isinstance(value, int) or value > 0:
                eng.wait_ge(s, value)

        def settle(eng, value):
            if not isinstance(value, int):
                eng.nop(nofuse=True)

        at_prep0 = len(SETUP_USES)
        at_it0 = at_prep0 + len(PREP_USES)
        assert all(n % 2 == 0 for n in (at_prep0, at_it0, FT, *(len(k.uses()) for _, k in STRETCH)))

        class Uses:
            def __init__(self, base, names):
                self.base, self.names = base, names

            def bank(self, name):
                return work[:, self.names.index(name) % 2]

            def fill(self, pe, name):
                wait(pe, evacuated, self.base + (self.names.index(name) - 1))
                return self.bank(name)

            def read(self, act, name):
                act.wait_ge(filled, self.base + (self.names.index(name) + 1))
                settle(act, self.base)
                return self.bank(name)

            def done(self, eng, name):
                eng.wait_ge(evacuated, self.base + (self.names.index(name) + 1))

        setup_uses = Uses(0, SETUP_USES)
        prep0_uses = Uses(at_prep0, PREP_USES)
        def base_of(c, k):
            at = at_it0
            for (lo, hi), kind in STRETCH[:k]:
                at += (hi - lo) * len(kind.uses())
            (lo, _), kind = STRETCH[k]
            return at + (c - lo) * len(kind.uses())

        def stretches(eng, body):
            for k, ((lo, hi), kind) in enumerate(STRETCH):
                batch = 0 if lo <= CB else 1
                if hi - lo == 1:
                    body(lo, Uses(base_of(lo, k), kind.uses()), kind, batch)
                else:
                    with eng.Fori(lo, hi) as c:
                        body(c, Uses(base_of(c, k), kind.uses()), kind, batch)

        at_tail = base_of(NC, len(STRETCH) - 1)
        tail_kind = Kind(prep=False, ffn=True, tail=True)
        tail_uses = Uses(at_tail, tail_kind.uses())
        at_ffn = at_tail + len(tail_uses.names)

        block = ctx.enter_context(nc.Block())

        @block.sync
        def _(sp):
            def load(dst, src, s):
                sp.dma_start(dst, src).then_inc(s, 16)

            def row(v):
                return v.rearrange("(o d) -> o d", o=1)

            def by_tile(m):
                return m.rearrange("(k p) n -> p k n", p=P)

            def load_rows(b):
                n = TB // 4
                for i in range(4):
                    load(rows[:, b, i * n:(i + 1) * n, 0:D],
                         t["x"][b, i * n * P:(i + 1) * n * P, :].rearrange("(t p) d -> p t d", p=P), x_in[b][i])

            load(means[:], t["means"], means_in)
            load(meansT[:], by_tile(t["meansT"]), means_in)
            load(promptT[:], by_tile(t["promptT"]), means_in)
            load_rows(0)
            load(wx[:], by_tile(t["wx"]), prep_in)
            load(wdt[:], t["wdt"], prep_in)
            load(bdt[:], t["bdt"], prep_in)
            load(A[:], by_tile(t["A_logs"]), prep_in)
            load(Dbc[:], row(t["Ds"]).to_broadcast([P, D]), prep_in)
            load_rows(1)
            load(wo[:], by_tile(t["WoT"]), fold_in)
            for i, n in enumerate(("bq", "bk", "bv")):
                load(bqkv[:, i, :], t[n], fold_in)
            load(bo[:], row(t["bo"]), fold_in)
            load(wr[:], by_tile(t["Wr"]), fold_in)
            load(br[:], row(t["br"]), fold_in)
            for b in range(B):
                load(ctxT[:, b], by_tile(t["ctxT"][b]), fold_in)

            def load_xs(c):
                if not isinstance(c, int) or c > 0:
                    sp.wait_ge(dlt_ready, c)
                    sp.wait_ge(acc_ready, c)
                sp.dma_start(xs[:], xsorted.rearrange("(c s p) r -> c p s r", s=SUB, p=P)[c]).then_inc(xs_in, 16)

            def store_b(c, us):
                us.done(sp, "proj")
                sp.dma_start(b_rows[c], proj[XB0:XB0 + NS, :]).then_inc(b_stored, 16)
                sp.wait_ge(b_stored, 16 * (c + 1))

            def load_b(c, g):
                wait(sp, dBu_ready, NS * c + BG * (g - 1))
                sp.dma_start(Bs[:, g % 2],
                             b_rows[c, g * BG:(g + 1) * BG, :].rearrange("(o n) l -> o n l", o=1).to_broadcast([P, BG, LC])
                             ).then_inc(b_in[g % 2], 16)

            def load_x3(q):
                wait(sp, ffn_ready, q - 1)
                wait(sp, x3_in, 16 * q)
                sp.wait_ge(x3_stored, 16 * (q + 1))
                sp.dma_start(x3[:, q % 2], x3_dram[q].rearrange("p (k l) -> p k l", k=KT)).then_inc(x3_in, 16)

            chosen = []

            def load_w(b, lo, hi):
                if lo == 0:
                    sp.wait_ge(expert_ready, b + 1)
                    chosen.append(sp.value_load(expert[0:1, 0:1], min_val=0, max_val=NE - 1))
                    load_x3(b * CB)
                    if b == 0:
                        load_b12(b)
                e = chosen[b]
                to1, to2 = (w1, w2) if b == 0 else (w1_raw, w2_raw)
                for i in range(lo, hi):
                    f = slice(2 * i * P, 2 * (i + 1) * P)
                    sp.dma_start(to1[:, :, f], t["W1"][e].rearrange("(k p) f -> p k f", p=P)[:, :, f]).then_inc(w_in[i], 16)
                    f = slice(2 * i, 2 * (i + 1))
                    sp.dma_start(to2[:, f, :], t["W2"][e].rearrange("(n p) d -> p n d", p=P)[:, f, :]).then_inc(w_in[i], 16)

            def load_b12(b):
                if b > 0:
                    sp.wait_ge(ffn_ready, b * CB)
                    sp.wait_ge(x2_biased, b * CB)
                e = chosen[b]
                sp.dma_start(b1[:], t["b1"][e]).then_inc(b12_in, 16)
                sp.dma_start(b2[:], t["b2"][e].rearrange("(o d) -> o d", o=1).to_broadcast([P, D])).then_inc(b12_in, 16)

            def load_x2(q):
                wait(sp, out_stored, 16 * SUB * q)
                sp.wait_ge(x2_stored, 16 * (q + 1))
                sp.dma_start(x2[:], x2_dram[q].rearrange("p (s d) -> p s d", s=SUB)).then_inc(x2_in, 16)

            def store_post(c):
                sp.wait_ge(x2_ready, c + 1)
                wait(sp, x2_stored, 16 * c)
                sp.dma_start(x2_dram[c].rearrange("p (s d) -> p s d", s=SUB), acc[:, c % 4]).then_inc(x2_stored, 16)

            def store_x3(c, uses):
                sp.wait_ge(evacuated, uses)
                wait(sp, x3_stored, 16 * c)
                sp.dma_start(x3_dram[c].rearrange("p (k l) -> p k l", k=KT), xnT[:]).then_inc(x3_stored, 16)

            sp.wait_ge(sorted_out, 16 * TB)
            load_xs(0)
            for w, n in ((wq, "Wq"), (wk, "WkT"), (wv, "WvT")):
                load(w, by_tile(t[n]), fold_in)
            store_b(0, prep0_uses)
            load_b(0, 0)
            load_b(0, 1)

            def body(c, us, kind, batch):
                if kind.prep and (kind.finish or not kind.ffn):
                    load_xs(c + 1)
                if kind.post and not kind.second:
                    store_x3(c - 2, us.base)
                load_b(c, 2)
                if kind.ffn and not kind.finish:
                    load_w(0, 4, 6)
                if kind.ffn:
                    load_x2(c - (CB + 1))
                    load_x3(c - CB)
                load_b(c, 3)
                if kind.ffn and not kind.finish:
                    load_w(0, 6, 8)
                if kind.prep:
                    store_b(c + 1, us)
                if kind.post:
                    store_post(c - 1)
                if kind.prep:
                    load_b(c + 1, 0)
                if kind.prep:
                    load_b(c + 1, 1)
                if kind.second:
                    sp.wait_ge(sorted_out, 16 * TB * B)
                if kind.choose:
                    load_xs(c + 2)
                    load_w(0, 0, 4)
            stretches(sp, body)

            store_x3(NC - 2, at_tail)
            load_x2(CB - 1)
            store_post(NC - 1)
            store_x3(NC - 1, at_tail + tail_uses.names.index("xn3T1") + 1)
            load_w(1, 0, FT // 2)
            load_b12(1)
            with sp.Fori(CB, NC - 1) as q:
                load_x2(q)
                load_x3(q + 1)
            load_x2(NC - 1)
            sp.wait_ge(out_stored, 16 * SUB * NC)

        @block.gpsimd
        def _(pool):
            pool.memset(ident[:], 0.0).then_inc(consts_ready, 1)
            pool.memset(ones[:], 1.0).then_inc(consts_ready, 1)
            pool.memset(before[:], 1.0).then_inc(consts_ready, 1)
            pool.memset(prompt[:], 0.0).then_inc(consts_ready, 1)
            pool.memset(carry[:], 0.0).then_inc(consts_ready, 1)
            pool.memset(half[:, 0:SUB], -0.5).then_inc(consts_ready, 1)
            pool.memset(half[:, SUB:SUB + 1], 0.5).then_inc(consts_ready, 1)
            pool.wait_ge(consts_ready, 7)
            pool.affine_select(out=ident[:], in_=ident[:], compare_op=ALU.not_equal, fill=1.0, base=0,
                               pattern=[[-1, P]], channel_multiplier=1).then_inc(consts_ready, 1)
            pool.affine_select(out=before[:], in_=before[:], compare_op=ALU.is_gt, fill=0.0, base=0,
                               pattern=[[1, P]], channel_multiplier=-1).then_inc(consts_ready, 1)
            pool.iota(rank8[:], pattern=[[0, TB], [-1, NB]], base=NB, channel_multiplier=0,
                      allow_small_or_imprecise_dtypes=True).then_inc(consts_ready, 1)
            for b in range(B):
                tags = rows[:, b, :, D:D + 1].bitcast(I32)
                pool.iota(tags, pattern=[[P, TB], [0, 1]], base=b * S, channel_multiplier=1).then_inc(tagged, 1)
            pool.wait_ge(mhat_link, 2)
            pool.tensor_tensor(msq[:, 1:2], msq[:, 0:1], half[0:NB, SUB:SUB + 1], ALU.pow).then_inc(root_ready, 1)

            def sort_tiles(b, lo, hi):
                if lo == 0:
                    pool.wait_ge(pos_ready, b + 1)
                    pool.wait_ge(tagged, B)
                    for i in range(4):
                        pool.wait_ge(x_in[b][i], 16)
                for i in range(lo, hi):
                    pool.indirect_dma_start(xsorted, bass.IndirectOffsetOnAxis(pos[:, b, i:i + 1], 0),
                                            rows[:, b, i, :], None).then_inc(sorted_out, 16)

            sort_tiles(0, 0, TB)

            def acc_init(c):
                pool.wait_ge(xn_ready, c + 1)
                pool.wait_ge(xs_in, 16 * (c + 1))
                if not isinstance(c, int) or c > 2:
                    pool.wait_ge(x2_stored, 16 * (c - 2))
                    pool.wait_ge(xn3_ready, c - 2)
                settle(pool, c)
                a = acc[:, c % 4]
                pool.tensor_tensor(a, xn[:], Dbc[:].rearrange("p (o d) -> p o d", o=1).to_broadcast([P, SUB, D]),
                                   ALU.mult).then_inc(acc_link, 1)
                pool.wait_ge(acc_link, c + 1)
                settle(pool, c)
                pool.tensor_copy(ids[:, bass.ds(c * SUB, SUB)], xs[:, :, D:D + 1].bitcast(U32)
                                 .rearrange("p s o -> p (s o)")).then_inc(ids_link, 1)
                pool.tensor_tensor(a, a, xs[:, :, 0:D], ALU.add).then_inc(acc_ready, 1)

            def du(c):
                pool.wait_ge(dlt_ready, c + 1)
                settle(pool, c)
                pool.tensor_tensor(u[:, c % 2], u[:, c % 2], dlt[:, c % 2], ALU.mult).then_inc(du_ready, 1)

            def invert_root(i, c):
                pool.wait_ge(var_ready[i], c + 1)
                pool.tensor_tensor(rstd[:, i, :], rstd[:, i, :], half[:, 0:SUB], ALU.pow).then_inc(shift_link[i], 1)
                pool.wait_ge(shift_link[i], c + 1)
                pool.tensor_tensor(shift[:, i, :], shift[:, i, :], rstd[:, i, :], ALU.mult).then_inc(rstd_ready[i], 1)

            invert_root(0, 0)
            pool.wait_ge(prep_in, 16 * 5)
            acc_init(0)
            du(0)

            def bias_x2(q, b):
                pool.wait_ge(b12_in, 32 * (b + 1))
                pool.wait_ge(x2_in, 16 * (q + 1))
                pool.tensor_tensor(x2[:], x2[:], b2[:].rearrange("p (o d) -> p o d", o=1).to_broadcast([P, SUB, D]),
                                   ALU.add).then_inc(x2_biased, 1)

            def scatter(q):
                wait(pool, out_stored, 16 * SUB * q)
                pool.wait_ge(ids_link, NC if isinstance(q, int) and q >= CB else q + 1)
                pool.tensor_copy(ids_now[:], ids[:, bass.ds(q * SUB, SUB)]).then_inc(ids_ready, 1)
                pool.wait_ge(ids_ready, q + 1)
                pool.wait_ge(res_ready, q + 1)
                settle(pool, q)
                for s in range(SUB):
                    pool.indirect_dma_start(t["out"].rearrange("b s d -> (b s) d"),
                                            bass.IndirectOffsetOnAxis(ids_now[:, s:s + 1], 0),
                                            x2[:, s, :], None).then_inc(out_stored, 16)

            def add_out(c, us):
                us.done(pool, "out1")
                pool.wait_ge(xn2_ready, c + 1)
                settle(pool, c)
                pool.tensor_tensor(acc[:, c % 4], acc[:, c % 4], xn23[:], ALU.add).then_inc(x2_ready, 1)

            def body(c, us, kind, batch):
                for n in range(NS):
                    if n % BG == 0:
                        g = n // BG
                        pool.wait_ge(b_in[g % 2], 32 * c + 16 * (g // 2 + 1))
                    if n == 0:
                        pool.wait_ge(du_ready, c + 1)
                    wait(pool, scanned, 2 * NS * c + 2 * (n - (4 if kind.fast else DBU_BACK[n]) + 1))
                    settle(pool, c)
                    to = tiles_of(dBu_long, n)[:, :, 1:] if kind.fast else dBu[:, DBU_SLOT[n]]
                    pool.tensor_tensor(to, u[:, c % 2],
                                       Bs[:, (n // BG) % 2, n % BG, :].rearrange("p (o l) -> p o l", o=1)
                                       .to_broadcast([P, KT, LC]), ALU.mult).then_inc(dBu_ready, 1)
                    if kind.prep and n == kind.pool["root12"]:
                        invert_root(0, c + 1)
                    if kind.post and n == kind.pool["root12"]:
                        invert_root(1, c - 1)
                    if kind.post and n == kind.pool["root3"]:
                        invert_root(2, c - 1)
                    if kind.finish and n == kind.pool["scatter"]:
                        scatter(c - (CB + 2))
                    if kind.ffn and n == kind.pool["bias"]:
                        bias_x2(c - (CB + 1), 0)
                    if kind.post and n == kind.pool["x2"]:
                        add_out(c - 1, us)
                    if kind.prep and n == kind.pool["acc"]:
                        acc_init(c + 1)
                    if kind.second and 7 <= n < 7 + TB // 2:
                        sort_tiles(1, 2 * (n - 7), 2 * (n - 7) + 2)
                    if kind.prep and n == kind.pool["du"]:
                        du(c + 1)
                if kind.second:
                    pool.wait_ge(sorted_out, 16 * TB * B)
                    pool.wait_ge(evacuated, us.base)
                    for n in range(4):
                        i = pool.memset(tiles_of(dA_long, n)[:, :, 0:1], 0.0)
                    i.then_inc(long_ready, 1)
            stretches(pool, body)
            invert_root(1, NC - 1)
            scatter(CB - 2)
            bias_x2(CB - 1, 0)
            add_out(NC - 1, tail_uses)
            invert_root(2, NC - 1)

            def split_x3(q):
                pool.wait_ge(ffn_ready, q - 1)
                pool.wait_ge(x3_in, 16 * (q + 1))
                settle(pool, q)
                pool.tensor_copy(x3_high[:, q % 2], x3[:, q % 2]).then_inc(x3_high_ready, 1)
                pool.wait_ge(x3_high_ready, q - CB + 1)
                settle(pool, q)
                pool.tensor_tensor(x3_low[:, q % 2], x3[:, q % 2], x3_high[:, q % 2].bitcast(F32), ALU.subtract
                                   ).then_inc(x3_low_ready, 1)

            pool.wait_ge(expert_ready, B)
            pool.wait_ge(x2_stored, 16 * NC)
            split_x3(CB)
            scatter(CB - 1)
            with pool.Fori(CB, NC - 1) as q:
                bias_x2(q, 1)
                split_x3(q + 1)
                scatter(q)
            bias_x2(NC - 1, 1)
            scatter(NC - 1)

        @block.scalar
        def _(act):
            def out_of(us, name, dst, view=lambda a: a, func=ACT.Copy, **kw):
                act.activation(dst, view(us.read(act, name)), func, **kw).then_inc(evacuated, 1)

            act.preload_act_table_set("natural_log_exp_and_others")
            us = setup_uses
            out_of(us, "mhat", mhatT[:], lambda a: a[:, 0:KT * NB].rearrange("p (k n) -> p k n", k=KT))
            out_of(us, "prompt", prompt[:, XC0:XC0 + NS], lambda a: a[0:NB, 0:NS])

            def fours(a):
                return a.rearrange("p (k n) -> p k n", k=KT)

            def biased(us, name, dst, which):
                a = fours(us.read(act, name))
                for k in range(KT):
                    i = act.activation(dst[:, k, :], a[:, k, :], ACT.Identity, bias=bqkv[:, which, k:k + 1])
                i.then_inc(evacuated, 1)

            def fold(name, us):
                what, b = name[:-1], int(name[-1])
                if name == FOLD_USES[0]:
                    act.wait_ge(fold_in, 16 * 12)
                if what == "keysT":
                    biased(us, name, keysT[:, b], 1)
                elif what == "foldedq":
                    out_of(us, name, foldedq[:, b], fours)
                elif what == "biasq":
                    out_of(us, name, biasq[:, b, :], lambda a: a[0:1, 0:KEYS])
                elif what == "valuesT":
                    biased(us, name, valuesT[:, b], 2)
                else:
                    out_of(us, name, foldedo[:, b, :])

            def raw(b, i, us):
                out_of(us, RAW_USES[b][i], rawT[:, i % 2], fours)

            for i in range(TB):
                raw(0, i, us)
            act.wait_ge(prep_in, 16 * 5)
            act.activation(A[:], A[:], ACT.Exp).then_inc(a_link, 1)
            act.wait_ge(a_link, 1)
            act.activation(A[:], A[:], ACT.Copy, scale=-1.0).then_inc(a_link, 1)
            act.wait_ge(a_link, 2)

            def normalise(dst, src, i, c, ready):
                act.wait_ge(rstd_ready[i], c + 1)
                settle(act, c)
                for s in range(SUB):
                    j = act.activation(dst[:, s, :], src[:, s, :], ACT.Identity, scale=rstd[:, i, s:s + 1],
                                       bias=shift[:, i, s:s + 1])
                j.then_inc(ready, 1)

            def norm1(c):
                wait(act, acc_ready, c)
                normalise(xn, xs[:, :, 0:D], 0, c, xn_ready)

            def norm2(c):
                normalise(xn23, acc[:, c % 4], 1, c, xn2_ready)

            def norm3(c):
                normalise(xn23, acc[:, c % 4], 2, c, xn3_ready)

            def read_prep(name, c, us):
                i = int(name[-1]) if name[-1].isdigit() else 0
                if name == "onehot":
                    out_of(us, name, onehot[:], lambda a: a[0:NB, 0:LC])
                elif name in ("uT0", "uT1"):
                    if i == 0:
                        wait(act, dBu_ready, NS * (c - 1))
                    out_of(us, name, u[:, c % 2, 2 * i:2 * i + 2, :], twos)
                elif name == "proj":
                    wait(act, b_stored, 16 * c)
                    out_of(us, name, proj[:], lambda a: a[0:XW, 0:LC])
                elif name in ("delta0", "delta1"):
                    a = twos(us.read(act, name))
                    for k in range(2):
                        j = act.activation(dlt[:, c % 2, 2 * i + k, :], a[:, k, :], ACT.Identity,
                                           bias=bdt[:, 2 * i + k:2 * i + k + 1])
                    j.then_inc(evacuated, 1)
                elif name in ("C0", "C1"):
                    if i == 0:
                        wait(act, hT_used, 2 * NS * (c - 1))
                    out_of(us, name, Cl[:, c % 2, i, :], lambda a: a[:, XC0:XC0 + NS])

            def twos(a):
                return a.rearrange("p (k l) -> p k l", k=2)

            def prep_soft_e(c):
                act.wait_ge(abs_ready, c + 1)
                act.wait_ge(acc_ready, c + 1)
                act.activation(soft_e, soft_l[:], ACT.Exp).then_inc(e_ready, 1)

            def prep_soft_l(c):
                act.wait_ge(e_ready, c + 1)
                act.activation(soft_l[:], soft_e, ACT.Ln, bias=1.0).then_inc(ln_ready, 1)

            def read_post(name, c, us):
                i = int(name[-1]) if name[-1].isdigit() else 0
                if name in ("xn2T0", "xn2T1"):
                    if i == 0:
                        wait(act, x3_stored, 16 * c)
                    out_of(us, name, xnT[:, 2 * i:2 * i + 2, :], twos)
                elif name == "scores":
                    out_of(us, name, prob[:], lambda a: a[:, 0:SUB * KEYS].rearrange("p (s n) -> p s n", s=SUB))
                elif name == "probsT":
                    out_of(us, name, probT[:], lambda a: a[:, 0:LC])
                elif name in ("out0", "out1"):
                    out_of(us, name, xn23[:, i, :])
                elif name in ("xn3T0", "xn3T1"):
                    a = twos(us.read(act, name))
                    for k in range(2):
                        m = 2 * i + k
                        j = act.activation(xnT[:, m, :], a[:, k, :], ACT.Copy, accum_out=msum[:, c, m:m + 1])
                    j.then_inc(evacuated, 1)

            def post_expo(c):
                act.wait_ge(smax_ready, c + 1)
                for s in range(SUB):
                    act.activation(prob[:, s, :], prob[:, s, :], ACT.Exp, bias=pstat[:, 1, s:s + 1], scale=SCALE,
                                   accum_out=pstat[:, 2, s:s + 1]).then_inc(expo_ready, 1)

            def hidden(q, f, us):
                act.activation(hid[:, f % 3, :], us.read(act, f"hidden{f}")[:, 0:LC], ACT.Relu,
                               bias=b1[:, f:f + 1]).then_inc(evacuated, 1)

            norm1(0)
            for name in PREP_USES:
                read_prep(name, 0, prep0_uses)
            prep_soft_e(0)
            prep_soft_l(0)

            def read_at(n, c, us, kind):
                for name in kind.uses_at(n):
                    if name.startswith("hidden"):
                        if n == 0:
                            act.wait_ge(b12_in, 32)
                        hidden(c - (CB + 1), n, us)
                    elif name.startswith("raw"):
                        raw(1, n, us)
                    elif name in FOLD_USES:
                        fold(name, us)
                    elif name in PREP_USES:
                        read_prep(name, c + 1, us)
                    else:
                        read_post(name, c - 1, us)

            def body(c, us, kind, batch):
                act.wait_ge(dlt_ready, c + 1)
                if kind.fast:
                    exponentials(c, 0, kind)
                    exponentials(c, 1, kind)
                for n in range(NS):
                    if not kind.fast:
                        exponentials(c, n, kind)
                    elif n + 2 < NS:
                        exponentials(c, n + 2, kind)
                    if n > 0:
                        save_carry(c, n - 1, kind)
                    if kind.prep and n == kind.act["soft_e"]:
                        prep_soft_e(c + 1)
                    if kind.prep and n == kind.act["soft_l"]:
                        prep_soft_l(c + 1)
                    if kind.act_norms and n == kind.act["norm1"]:
                        norm1(c + 1)
                    if kind.act_norms and kind.post and n == kind.act["norm2"]:
                        norm2(c - 1)
                    if kind.act_norms and kind.post and n == kind.act["norm3"]:
                        norm3(c - 1)
                    if n > 0 and not kind.fast:
                        read_at(n - 1, c, us, kind)
                    if kind.post and n == kind.act["expo"]:
                        post_expo(c - 1)
                    if kind.fast:
                        read_at(n, c, us, kind)
                save_carry(c, NS - 1, kind)
                if not kind.fast:
                    read_at(NS - 1, c, us, kind)

            def exponentials(c, n, kind):
                if kind.fast:
                    act.wait_ge(scanned, 2 * NS * c + 2 * (n - 3))
                    act.wait_ge(long_ready, 1)
                    settle(act, c)
                    act.activation(tiles_of(dBu_long, n)[:, 1:, 0], carry[:, n, 1:], ACT.Copy)
                for k in range(KT):
                    if kind.fast:
                        to = tiles_of(dA_long, n)[:, k, 1:]
                    else:
                        to = dA[:, k // 2, (k % 2) * LC:(k % 2 + 1) * LC]
                        if kind.choose and n == 0 and k == 0:
                            act.wait_ge(hT_used, 2 * NS * c)
                        if k % 2 == 0:
                            wait(act, scanned, 2 * NS * c + 2 * n + k // 2 - 1)
                            settle(act, c)
                    i = act.activation(to, dlt[:, c % 2, k, :], ACT.Exp, scale=A[:, k, n:n + 1])
                    if k % 2 == 1:
                        i.then_inc(dA_ready, 1)

            def save_carry(c, n, kind):
                act.wait_ge(scanned, 2 * NS * c + 2 * n + 2)
                settle(act, c)
                act.activation(carry[:, n, :], h_of(kind, n)[:, :, LC - 1], ACT.Copy).then_inc(carried, 1)
            stretches(act, body)

            us = tail_uses
            for n in range(NS):
                read_at(n, NC, us, tail_kind)
                if n == TAIL_EXPO:
                    post_expo(NC - 1)

            def round_weights(i):
                act.wait_ge(ffn_ready, CB)
                act.wait_ge(w_in[i], 32 * B)
                f = slice(2 * i * P, 2 * (i + 1) * P)
                act.activation(w1_high[:, :, f], w1_raw[:, :, f], ACT.Copy).then_inc(w_high_ready, 1)
                f = slice(2 * i, 2 * (i + 1))
                act.activation(w2_high[:, f, :], w2_raw[:, f, :], ACT.Copy).then_inc(w_high_ready, 1)

            def hidden_parts(q, f):
                act.wait_ge(filled, at_ffn + (q - CB) * FT + f + 1)
                settle(act, q)
                bank = work[:, f % 2, 0:LC]
                act.activation(hid_raw[:, f % 4, :], bank, ACT.Relu, bias=b1[:, f:f + 1])
                act.activation(hid_high[:, f % 4, :], bank, ACT.Relu, bias=b1[:, f:f + 1]).then_inc(evacuated, 1)

            round_weights(0)
            round_weights(1)
            act.wait_ge(b12_in, 32 * B)
            for f in range(FT):
                if f % 2 == 0 and f // 2 + 2 < FT // 2:
                    round_weights(f // 2 + 2)
                hidden_parts(CB, f)
            with act.Fori(CB + 1, NC) as q:
                for f in range(FT):
                    hidden_parts(q, f)

        @block.vector
        def _(dve):
            V = dve

            def chain(s, base):
                at = [base]

                def link(ins):
                    at[0] = at[0] + 1
                    ins.then_inc(s, 1)
                    dve.wait_ge(s, at[0])
                return link

            dve.wait_ge(means_in, 16 * 3)
            link = chain(mhat_link, 0)
            link(V.tensor_tensor(mhat[:], means[:], means[:], ALU.mult))
            link(V.tensor_reduce(msq[:, 0:1], mhat[:], AX.X, ALU.add))
            dve.wait_ge(root_ready, 1)
            link(V.tensor_scalar(msq[:, 1:2], msq[:, 1:2], 1e-12, None, ALU.max))
            link(V.reciprocal(msq[:, 2:3], msq[:, 1:2]))
            link(V.tensor_scalar(mhat[:], means[:], msq[:, 2:3], None, ALU.mult))
            link(V.tensor_reduce(msq[:, 0:1], mhat[:], AX.X, ALU.add))
            link(V.tensor_scalar(msq[:, 3:4], msq[:, 0:1], 1.0 / D, None, ALU.mult))
            V.tensor_scalar(mhat[:], mhat[:], msq[:, 3:4], None, ALU.subtract).then_inc(mhat_ready, 1)

            dve.wait_ge(consts_ready, 10)
            sc, eq, oh, tot, inc, tmp = [rt[i].rearrange("p (t k) -> p t k", k=NB) for i in range(6)]
            m1, m2 = rt[6][:, 0:TB], rt[6][:, TB:2 * TB]
            ROUTE_LINKS, PLACE_LINKS = 6, 6

            def spread(m):
                return m.rearrange("p (t o) -> p t o", o=1).to_broadcast([P, TB, NB])

            def route(b):
                link = chain(route_link, b * (ROUTE_LINKS + PLACE_LINKS))
                dve.wait_ge(scored, b + 1)
                link(V.tensor_copy(sc, fo[:, 1, 0:TB * NB].rearrange("p (t k) -> p t k", k=NB)))
                link(V.tensor_reduce(m1, sc, AX.X, ALU.max))
                link(V.tensor_tensor(eq, sc, spread(m1), ALU.is_equal))
                link(V.tensor_tensor(eq, eq, rank8[:], ALU.mult))
                link(V.tensor_reduce(m2, eq, AX.X, ALU.max))
                link(V.tensor_tensor(oh, rank8[:], spread(m2), ALU.is_equal))
                V.tensor_copy(rows[:, b, :, D + 1:ROW], oh).then_inc(onehot_ready, 1)

            def place(b):
                link = chain(route_link, b * (ROUTE_LINKS + PLACE_LINKS) + ROUTE_LINKS)
                dve.wait_ge(counted, b + 1)
                link(V.tensor_copy(rt[3].rearrange("p (k t) -> p k t", k=NB),
                                   fo[:, 0, P:2 * P].rearrange("p (t k) -> p k t", k=NB)))
                link(V.tensor_tensor_scan(rt[4], ones[:], rt[3], 0.0, ALU.mult, ALU.add))
                link(V.tensor_tensor(rt[4], rt[4], rt[3], ALU.subtract))
                link(V.tensor_tensor(tmp, fo[:, 0, 0:P].rearrange("p (t k) -> p t k", k=NB),
                                     rt[4].rearrange("p (k t) -> p t k", k=NB), ALU.add))
                link(V.tensor_tensor(tmp, tmp, oh, ALU.mult))
                link(V.tensor_reduce(m1, tmp, AX.X, ALU.add))
                V.tensor_scalar(pos[:, b, :], m1, float(b * S), None, ALU.add).then_inc(pos_ready, 1)

            route(0)
            place(0)

            def stats(src, i, c):
                link = chain(norm_link[i], 2 * c)
                settle(dve, c)
                for s in range(SUB):
                    j = V.bn_stats(st[:, i, s, :], src[:, s, :])
                link(j)
                settle(dve, c)
                for s in range(SUB):
                    j = V.bn_aggr(mv[:, i, s, :], st[:, i, s, :])
                link(j)
                V.tensor_scalar(shift[:, i, :], mv[:, i, :, 0], -1.0, None, ALU.mult)
                V.tensor_scalar(rstd[:, i, :], mv[:, i, :, 1], EPS, None, ALU.add).then_inc(var_ready[i], 1)

            def normalise(dst, src, i, c, ready):
                dve.wait_ge(rstd_ready[i], c + 1)
                for s in range(SUB):
                    j = V.tensor_scalar(dst[:, s, :], src[:, s, :], mv[:, i, s, 0:1], rstd[:, i, s:s + 1],
                                        ALU.subtract, ALU.mult)
                j.then_inc(ready, 1)

            def norm1(c):
                wait(dve, acc_ready, c)
                normalise(xn, xs[:, :, 0:D], 0, c, xn_ready)

            def norm2(c):
                normalise(xn23, acc[:, c % 4], 1, c, xn2_ready)

            def norm3(c):
                normalise(xn23, acc[:, c % 4], 2, c, xn3_ready)

            def norm1_stats(c):
                dve.wait_ge(xs_in, 16 * (c + 1))
                stats(xs[:, :, 0:D], 0, c)

            def absz(c, us):
                us.done(dve, "delta1")
                wait(dve, dlt_ready, c)
                z = dlt[:, c % 2].rearrange("p k l -> p (k l)")
                V.scalar_tensor_tensor(out=soft_l[:].rearrange("p k l -> p (k l)"), in0=z, scalar=-1.0, in1=z,
                                       op0=ALU.mult, op1=ALU.min).then_inc(abs_ready, 1)

            def softplus(c):
                link = chain(soft_link, 3 * c)
                dve.wait_ge(ln_ready, c + 1)
                z = dlt[:, c % 2].rearrange("p k l -> p (k l)")
                e_, l_ = [v.rearrange("p k l -> p (k l)") for v in (soft_e, soft_l[:])]
                link(V.scalar_tensor_tensor(out=z, in0=z, scalar=0.0, in1=l_, op0=ALU.max, op1=ALU.add))
                link(V.tensor_scalar(l_, e_, 1.0, 1.0, ALU.add, ALU.subtract))
                link(V.tensor_tensor(e_, e_, l_, ALU.subtract))
                V.tensor_tensor(z, z, e_, ALU.add).then_inc(dlt_ready, 1)

            def norm2_stats(c):
                dve.wait_ge(hT_used, 2 * NS * (c + 1))
                stats(acc[:, c % 4], 1, c)

            def smax(c, us):
                us.done(dve, "scores")
                V.tensor_reduce(pstat[:, 0, :], prob[:], AX.X, ALU.max).then_inc(smax_link, 1)
                dve.wait_ge(smax_link, c + 1)
                V.tensor_scalar(pstat[:, 1, :], pstat[:, 0, :], -SCALE, None, ALU.mult).then_inc(smax_ready, 1)

            def snorm(c):
                dve.wait_ge(expo_ready, SUB * (c + 1))
                V.reciprocal(pstat[:, 3, :], pstat[:, 2, :]).then_inc(soft_sum, 1)
                dve.wait_ge(soft_sum, c + 1)
                V.tensor_tensor(prob[:], prob[:], pstat[:, 3, :].rearrange("p (s o) -> p s o", o=1)
                                .to_broadcast([P, SUB, KEYS]), ALU.mult).then_inc(probs_ready, 1)

            def norm3_stats(c):
                dve.wait_ge(x2_ready, c + 1)
                stats(acc[:, c % 4], 2, c)

            def finish(q):
                dve.wait_ge(ffn_ready, q + 1)
                dve.wait_ge(x2_biased, q + 1)
                for s in range(SUB):
                    j = V.tensor_tensor(x2[:, s, :], fo[:, s, :], x2[:, s, :], ALU.add)
                j.then_inc(res_ready, 1)

            def token_mean(b, us):
                us.done(dve, "xn3T1")
                V.tensor_reduce(mean[:], msum[:, b * CB:(b + 1) * CB, :].rearrange("p c k -> p k c"), AX.X,
                                ALU.add).then_inc(mean_link, 1)
                dve.wait_ge(mean_link, b + 1)
                V.tensor_scalar(mean[:], mean[:], 1.0 / S, None, ALU.mult).then_inc(mean_ready, 1)

            def choose(b):
                dve.wait_ge(voted, b + 1)
                link = chain(vote_link, 5 * b)
                link(V.tensor_tensor(vote[:, 0, :], (fo, hT)[b][0:1, 0, 0:NE], br[:], ALU.add))
                link(V.tensor_reduce(vote[:, 1, 0:1], vote[:, 0, :], AX.X, ALU.max))
                link(V.tensor_scalar(vote[:, 2, :], vote[:, 0, :], vote[:, 1, 0:1], None, ALU.is_equal))
                link(V.tensor_tensor(vote[:, 2, :], vote[:, 2, :], rank8[0:1, 0, :], ALU.mult))
                link(V.tensor_reduce(vote[:, 3, 0:1], vote[:, 2, :], AX.X, ALU.max))
                V.tensor_scalar(expert[:, 0:1], vote[:, 3, 0:1], -1.0, float(NE), ALU.mult, ALU.add
                                ).then_inc(expert_ready, 1)

            norm1_stats(0)
            absz(0, prep0_uses)
            softplus(0)

            def body(c, us, kind, batch):
                def rows_of(n, j):
                    use = 2 * NS * c + 2 * n + j
                    dve.wait_ge(hT_ready, use + 1)
                    if n == 0:
                        dve.wait_ge(acc_ready, c + 1)
                    else:
                        dve.wait_ge(hT_used, use - 1)
                    a = acc[:, c % 4, j, :]
                    V.scalar_tensor_tensor(out=a, in0=turned_h(kind, n, j), scalar=Cl[:, c % 2, j, n:n + 1], in1=a,
                                           op0=ALU.mult, op1=ALU.add).then_inc(hT_used, 1)

                def h_free(c, n):
                    dve.wait_ge(dBu_ready, NS * c + n + 1)
                    wait(dve, hT_ready, 2 * NS * c + 2 * (n - H_RING + 1))
                    wait(dve, carried, NS * c + n - H_RING + 1)

                if kind.choose:
                    dve.wait_ge(carried, NS * c)
                    V.memset(carry[:], 0.0).then_inc(carry_zeroed, 1)
                    dve.wait_ge(carry_zeroed, 1)
                if kind.prep:
                    norm1_stats(c + 1)
                if kind.post:
                    norm2_stats(c - 1)
                for n in range(NS):
                    if kind.fast:
                        dve.wait_ge(dA_ready, 2 * NS * c + 2 * (n + 1))
                        h_free(c, n)
                        V.tensor_tensor_scan(h_long[:, n % 4, 1:], dA_long[:, n % 4, 1:], dBu_long[:, n % 4, 1:],
                                             carry[:, n, 0:1], ALU.mult, ALU.add).then_inc(scanned, 2)
                        if n > 1:
                            rows_of(n - 2, 0)
                            rows_of(n - 2, 1)
                    for k in range(0 if kind.fast else KT):
                        if k % 2 == 0:
                            dve.wait_ge(dA_ready, 2 * NS * c + 2 * n + k // 2 + 1)
                        if k == 0:
                            h_free(c, n)
                        j = V.tensor_tensor_scan(h[:, n % H_RING, k, :], dA[:, k // 2, (k % 2) * LC:(k % 2 + 1) * LC],
                                                 dBu[:, DBU_SLOT[n], k, :], carry[:, n, k:k + 1], ALU.mult, ALU.add)
                        if k % 2 == 1:
                            j.then_inc(scanned, 1)
                            if n > 1:
                                rows_of(n - 2, k // 2)
                    if kind.finish and n == kind.dve["finish"]:
                        finish(c - (CB + 2))
                    if kind.prep and not kind.act_norms and n == kind.dve["norm1"]:
                        norm1(c + 1)
                    if kind.post and not kind.act_norms and n == kind.dve["norm2"]:
                        norm2(c - 1)
                    if kind.second and n == kind.dve["route"]:
                        route(1)
                    if kind.second and n == kind.dve["place"]:
                        place(1)
                    if kind.post and n == kind.dve["max"]:
                        smax(c - 1, us)
                    if kind.post and n == kind.dve["normal"]:
                        snorm(c - 1)
                    if kind.prep and n == kind.dve["abs"]:
                        absz(c + 1, us)
                    if kind.prep and n == kind.dve["softplus"]:
                        softplus(c + 1)
                    if kind.post and n == kind.dve["stats3"]:
                        norm3_stats(c - 1)
                    if kind.post and not kind.act_norms and n == kind.dve["norm3"]:
                        norm3(c - 1)
                    if kind.choose and n == kind.dve["mean"]:
                        token_mean(0, us)
                    if kind.choose and n == kind.dve["choose"]:
                        choose(0)
                for n in range(NS - 2, NS):
                    for j in range(SUB):
                        rows_of(n, j)
            stretches(dve, body)

            us = tail_uses
            finish(CB - 2)
            norm2_stats(NC - 1)
            norm2(NC - 1)
            smax(NC - 1, us)
            snorm(NC - 1)
            norm3_stats(NC - 1)
            norm3(NC - 1)
            token_mean(1, us)
            choose(1)
            finish(CB - 1)

            def rest_of_weights(i):
                f = slice(2 * i * P, 2 * (i + 1) * P)
                dve.wait_ge(w_high_ready, 2 * i + 1)
                V.tensor_tensor(w1_low[:, :, f], w1_raw[:, :, f], w1_high[:, :, f].bitcast(F32), ALU.subtract
                                ).then_inc(w_low_ready, 1)
                f = slice(2 * i, 2 * (i + 1))
                dve.wait_ge(w_high_ready, 2 * i + 2)
                V.tensor_tensor(w2_low[:, f, :], w2_raw[:, f, :], w2_high[:, f, :].bitcast(F32), ALU.subtract
                                ).then_inc(w_low_ready, 1)

            def hidden_low(q, f):
                dve.wait_ge(evacuated, at_ffn + (q - CB) * FT + f + 1)
                settle(dve, q)
                V.tensor_tensor(hid_low[:, f % 4, :], hid_raw[:, f % 4, :], hid_high[:, f % 4, :].bitcast(F32),
                                ALU.subtract).then_inc(hid_low_ready, 1)

            rest_of_weights(0)
            rest_of_weights(1)
            for f in range(FT):
                if f % 2 == 0 and f // 2 + 2 < FT // 2:
                    rest_of_weights(f // 2 + 2)
                hidden_low(CB, f)
            with dve.Fori(CB + 1, NC) as q:
                for f in range(FT):
                    hidden_low(q, f)
                    if f == 1:
                        finish(q - 1)
            finish(NC - 1)

        @block.tensor
        def _(pe):
            us = setup_uses
            pe.wait_ge(means_in, 16 * 3)
            pe.wait_ge(consts_ready, 10)
            pe.wait_ge(mhat_ready, 1)
            w = us.fill(pe, "mhat")
            for k in range(KT):
                i = pe.transpose(w[:, k * NB:(k + 1) * NB], mhat[:, k * P:(k + 1) * P], ident[0:NB, 0:NB])
            i.then_inc(filled, 1)

            def product(out, lhs, rhs, lo=0, hi=None):
                n = len(lhs)
                for i in range(lo, n if hi is None else hi):
                    j = pe.matmul(out, lhs[i], rhs[i], start=(i == 0), stop=(i == n - 1))
                return j

            w = us.fill(pe, "prompt")
            product(w[0:NB, 0:NS], [meansT[:, k, :] for k in range(KT)], [promptT[:, k, :] for k in range(KT)]
                    ).then_inc(filled, 1)

            def fold(name, us):
                what, b = name[:-1], int(name[-1])
                if name == FOLD_USES[0]:
                    pe.wait_ge(fold_in, 16 * 12)
                ctx_k = [ctxT[:, b, k, :] for k in range(KT)]
                keys_k = [keysT[:, b, k, :] for k in range(KT)]
                w = us.fill(pe, name)
                if what in ("keysT", "foldedq", "valuesT"):
                    weight, moving = {"keysT": (wk, ctx_k), "foldedq": (wq, keys_k), "valuesT": (wv, ctx_k)}[what]
                    if what == "foldedq":
                        us.done(pe, f"keysT{b}")
                    for m in range(KT):
                        i = product(w[:, m * P:(m + 1) * P], [weight[:, k, m * P:(m + 1) * P] for k in range(KT)], moving)
                elif what == "biasq":
                    i = product(w[0:1, 0:KEYS], [bqkv[:, 0, k:k + 1] for k in range(KT)], keys_k)
                else:
                    us.done(pe, f"valuesT{b}")
                    i = product(w, [valuesT[:, b, k, :] for k in range(KT)] + [ones[0:1, :]],
                                [wo[:, k, :] for k in range(KT)] + [bo[:]])
                i.then_inc(filled, 1)

            def raw(b, i, us):
                if i % (TB // 4) == 0:
                    pe.wait_ge(x_in[b][i // (TB // 4)], 16)
                w = us.fill(pe, RAW_USES[b][i])
                for k in range(KT):
                    j = pe.transpose(w[:, k * P:(k + 1) * P], rows[:, b, i, k * P:(k + 1) * P], ident[:])
                j.then_inc(filled, 1)

            def score(b, i, number):
                pe.wait_ge(evacuated, number + 1)
                j = product(fo[:, 1, i * NB:(i + 1) * NB], [rawT[:, i % 2, k, :] for k in range(KT)],
                            [mhatT[:, k, :] for k in range(KT)])
                if i == TB - 1:
                    j.then_inc(scored, 1)

            def count(b):
                pe.wait_ge(onehot_ready, b + 1)
                pe.matmul(fo[:, 0, 0:P], before[:], rt[2], start=True, stop=True)
                pe.matmul(fo[:, 0, P:2 * P], ones[:], rt[2], start=True, stop=True).then_inc(counted, 1)

            for i in range(TB):
                raw(0, i, us)
                if i > 0:
                    score(0, i - 1, SETUP_USES.index(RAW_USES[0][i - 1]))
            score(0, TB - 1, SETUP_USES.index(RAW_USES[0][TB - 1]))
            count(0)

            def turn(us, name, src):
                w = us.fill(pe, name)
                i = int(name[-1])
                for k in range(2):
                    for s in range(SUB):
                        m = 2 * i + k
                        j = pe.transpose(w[:, k * LC + s * P:k * LC + (s + 1) * P], src[:, s, m * P:(m + 1) * P], ident[:])
                j.then_inc(filled, 1)

            def fill_prep(name, c, us):
                i = int(name[-1]) if name[-1].isdigit() else 0
                if name == "onehot":
                    pe.wait_ge(xs_in, 16 * (c + 1))
                    w = us.fill(pe, name)
                    settle(pe, us.base)
                    for s in range(SUB):
                        j = pe.matmul(w[0:NB, s * P:(s + 1) * P], xs[:, s, D + 1:ROW], ident[:], start=True, stop=True)
                    j.then_inc(filled, 1)
                elif name in ("uT0", "uT1"):
                    pe.wait_ge(xn_ready, c + 1)
                    turn(us, name, xn)
                elif name == "proj":
                    us.done(pe, "uT1")
                    w = us.fill(pe, name)
                    product(w[0:XW, 0:LC], [wx[:, k, :] for k in range(KT)] + [prompt[:]],
                            [u[:, c % 2, k, :] for k in range(KT)] + [onehot[:]]).then_inc(filled, 1)
                elif name in ("delta0", "delta1"):
                    us.done(pe, "proj")
                    w = us.fill(pe, name)
                    for k in range(2):
                        m = 2 * i + k
                        j = pe.matmul(w[:, k * LC:(k + 1) * LC], wdt[:, m * P:(m + 1) * P], proj[0:R, :], start=True, stop=True)
                    j.then_inc(filled, 1)
                elif name in ("C0", "C1"):
                    w = us.fill(pe, name)
                    settle(pe, us.base)
                    pe.transpose(w[:, 0:XB0], proj[0:XB0, i * P:(i + 1) * P], ident[0:XB0, 0:XB0]).then_inc(filled, 1)

            def fill_post(name, c, us, b):
                if name in ("xn2T0", "xn2T1"):
                    pe.wait_ge(xn2_ready, c + 1)
                    turn(us, name, xn23)
                elif name in ("xn3T0", "xn3T1"):
                    pe.wait_ge(xn3_ready, c + 1)
                    turn(us, name, xn23)
                elif name == "scores":
                    us.done(pe, "xn2T1")
                    w = us.fill(pe, name)
                    for s in range(SUB):
                        j = product(w[:, s * KEYS:(s + 1) * KEYS],
                                    [xnT[:, k, s * P:(s + 1) * P] for k in range(KT)] + [ones[0:1, :]],
                                    [foldedq[:, b, k, :] for k in range(KT)] + [biasq[:, b, :]])
                    j.then_inc(filled, 1)
                elif name == "probsT":
                    pe.wait_ge(probs_ready, c + 1)
                    w = us.fill(pe, name)
                    for s in range(SUB):
                        j = pe.transpose(w[:, s * P:(s + 1) * P], prob[:, s, :], ident[:])
                    j.then_inc(filled, 1)
            def out_terms(us, name, b, lo, hi):
                t, n = int(name[-1]), KT + 1
                if lo == 0:
                    us.done(pe, "probsT")
                    us.fill(pe, name)
                j = product(us.bank(name), [xnT[:, k, t * P:(t + 1) * P] for k in range(KT)] + [probT[:, t * P:(t + 1) * P]],
                            [wo[:, k, :] for k in range(KT)] + [foldedo[:, b, :]], lo, hi)
                if hi == n:
                    j.then_inc(filled, 1)

            def first_product(q, f, us):
                w = us.fill(pe, f"hidden{f}")
                product(w[:, 0:LC], [w1[:, k, f * P:(f + 1) * P] for k in range(KT)],
                        [x3[:, q % 2, k, :] for k in range(KT)]).then_inc(filled, 1)

            def second_product(q, f, us):
                us.done(pe, f"hidden{f}")
                if f == 0:
                    wait(pe, res_ready, q)
                for s in range(SUB):
                    j = pe.matmul(fo[:, s, :], hid[:, f % 3, s * P:(s + 1) * P], w2[:, f, :],
                                  start=(f == 0), stop=(f == FT - 1))
                if f == FT - 1:
                    j.then_inc(ffn_ready, 1)

            def vote_for(b):
                pe.wait_ge(mean_ready, b + 1)
                product((fo, hT)[b][0:1, 0, 0:NE], [mean[:, k:k + 1] for k in range(KT)], [wr[:, k, :] for k in range(KT)]
                        ).then_inc(voted, 1)

            pe.wait_ge(prep_in, 16 * 5)
            for name in PREP_USES:
                fill_prep(name, 0, prep0_uses)

            def fill_at(n, half, c, us, b, kind):
                names = [name for name in kind.slots(n) if name not in ("out0", "out1")]
                for name in names[0:1] if half == 0 else names[1:]:
                    if name in PREP_USES:
                        fill_prep(name, c + 1, us)
                    else:
                        fill_post(name, c - 1, us, b)
                part = kind.out.get((n, half))
                if part and kind.post:
                    name, lo, hi = part
                    out_terms(us, name, b, lo, hi)

            def body(c, us, kind, batch):
                def turn_h(n, j):
                    use = 2 * NS * c + 2 * n + j
                    if j == 0:
                        pe.wait_ge(scanned, 2 * NS * c + 2 * n + 2)
                    wait(pe, hT_used, use - (3 if kind.fast and n > 0 else 1))
                    for k in range(KT):
                        i = pe.transpose(turned_h(kind, n, j)[:, k * P:(k + 1) * P], h_of(kind, n)[:, k, j * P:(j + 1) * P], ident[:])
                    i.then_inc(hT_ready, 1)

                q = c - (CB + 1)
                for n in range(NS):
                    if n > 0:
                        turn_h(n - 1, 0)
                    if kind.ffn:
                        if not kind.finish and n % 2 == 0:
                            pe.wait_ge(w_in[n // 2], 32)
                        if n == 0:
                            pe.wait_ge(x3_in, 16 * (q + 1))
                        first_product(q, n, us)
                    if kind.first:
                        raw(1, n, us)
                    fill_at(n, 0, c, us, batch, kind)
                    if n > 0:
                        turn_h(n - 1, 1)
                        if kind.ffn:
                            second_product(q, n - 1, us)
                    if kind.first and n > 0:
                        score(1, n - 1, us.base + us.names.index(RAW_USES[1][n - 1]))
                    if kind.second and n == 0:
                        score(1, TB - 1, last_raw)
                    if kind.second and n == kind.dve["route"] + 1:
                        count(1)
                    fill_at(n, 1, c, us, batch, kind)
                    if kind.first and 1 <= n <= len(FOLD_USES):
                        fold(FOLD_USES[n - 1], us)
                    if kind.choose and n == kind.dve["choose"]:
                        vote_for(0)
                for j in range(SUB):
                    turn_h(NS - 1, j)
                if kind.ffn:
                    second_product(q, FT - 1, us)

            last_raw = at_it0 + STRETCH[0][1].uses().index(RAW_USES[1][TB - 1])
            stretches(pe, body)

            us = tail_uses
            q = CB - 1
            pe.wait_ge(x3_in, 16 * (q + 1))
            for n in range(NS):
                first_product(q, n, us)
                if n > 0:
                    second_product(q, n - 1, us)
                for half in range(2):
                    fill_at(n, half, NC, us, 1, tail_kind)
                if n == TAIL_VOTE:
                    vote_for(1)
            second_product(q, FT - 1, us)

            def parts(high_l, low_l, high_r, low_r):
                return [(high_l, low_r), (low_l, high_r), (high_l, high_r)]

            def first_parts(q, f):
                base = at_ffn + (q - CB) * FT
                pe.wait_ge(evacuated, base + f - 1)
                if f == 0:
                    pe.wait_ge(x3_low_ready, q - CB + 1)
                if f % 2 == 0:
                    pe.wait_ge(w_low_ready, f + 2)
                tile = slice(f * P, (f + 1) * P)
                terms = [p for k in range(KT) for p in parts(w1_high[:, k, tile], w1_low[:, k, tile],
                                                             x3_high[:, q % 2, k, :], x3_low[:, q % 2, k, :])]
                product(work[:, f % 2, 0:LC], *zip(*terms)).then_inc(filled, 1)

            def second_parts(q, f):
                pe.wait_ge(hid_low_ready, (q - CB) * FT + f + 1)
                if f == 0:
                    pe.wait_ge(res_ready, q)
                for s in range(SUB):
                    tile = slice(s * P, (s + 1) * P)
                    for i, (l, r) in enumerate(parts(hid_high[:, f % 4, tile], hid_low[:, f % 4, tile],
                                                     w2_high[:, f, :], w2_low[:, f, :])):
                        j = pe.matmul(fo[:, s, :], l, r, start=(f == 0 and i == 0), stop=(f == FT - 1 and i == 2))
                if f == FT - 1:
                    j.then_inc(ffn_ready, 1)

            for f in range(FT):
                first_parts(CB, f)
                if f >= 2:
                    second_parts(CB, f - 2)
            with pe.Fori(CB + 1, NC) as q:
                for f in range(FT):
                    first_parts(q, f)
                    if f >= 2:
                        second_parts(q, f - 2)
                    else:
                        second_parts(q - 1, FT - 2 + f)
            for f in range(FT - 2, FT):
                second_parts(NC - 1, f)


def kernel(x, ctx_1024, L0_attn_means, L0_attn_prompt_weight, L0_attn_x_proj_weight, L0_attn_dt_projs_weight,
           L0_attn_dt_projs_bias, L0_attn_A_logs, L0_attn_Ds, L0_xattn_Wq, L0_xattn_bq, L0_xattn_Wk, L0_xattn_bk,
           L0_xattn_Wv, L0_xattn_bv, L0_xattn_Wo, L0_xattn_bo, L0_ffn_Wr, L0_ffn_br, L0_ffn_W1, L0_ffn_b1,
           L0_ffn_W2, L0_ffn_b2):
    import concourse.bacc as bacc
    from concourse.bass_utils import run_bass_kernel_spmd

    def tiles(v):
        return np.ascontiguousarray(np.asarray(v).reshape(-1, P).T)

    def turned(m):
        return np.ascontiguousarray(np.asarray(m).T)

    xp = np.asarray(L0_attn_x_proj_weight)
    wx = np.zeros((D, XW), xp.dtype)
    wx[:, 0:R] = xp[0:R].T
    wx[:, XC0:XC0 + NS] = xp[R + NS:].T
    wx[:, XB0:XB0 + NS] = xp[R:R + NS].T
    arrays = {
        "x": np.ascontiguousarray(x), "ctxT": np.ascontiguousarray(np.asarray(ctx_1024).transpose(0, 2, 1)),
        "means": np.ascontiguousarray(L0_attn_means), "meansT": turned(L0_attn_means),
        "promptT": turned(L0_attn_prompt_weight), "wx": wx, "wdt": turned(L0_attn_dt_projs_weight),
        "bdt": tiles(L0_attn_dt_projs_bias), "A_logs": np.ascontiguousarray(L0_attn_A_logs),
        "Ds": np.ascontiguousarray(L0_attn_Ds),
        "Wq": np.ascontiguousarray(L0_xattn_Wq), "WkT": turned(L0_xattn_Wk), "WvT": turned(L0_xattn_Wv),
        "WoT": turned(L0_xattn_Wo), "bq": tiles(L0_xattn_bq), "bk": tiles(L0_xattn_bk), "bv": tiles(L0_xattn_bv),
        "bo": np.ascontiguousarray(L0_xattn_bo), "Wr": np.ascontiguousarray(L0_ffn_Wr),
        "br": np.ascontiguousarray(L0_ffn_br), "W1": np.ascontiguousarray(L0_ffn_W1),
        "b1": np.ascontiguousarray(np.asarray(L0_ffn_b1).reshape(NE, FT, P).transpose(0, 2, 1)),
        "W2": np.ascontiguousarray(L0_ffn_W2), "b2": np.ascontiguousarray(L0_ffn_b2),
    }
    nc = bacc.Bacc("TRN2", target_bir_lowering=False, num_devices=1)
    t = {n: nc.dram_tensor(f"in_{n}", a.shape, mybir.dt.from_np(a.dtype), kind="ExternalInput").ap()
         for n, a in arrays.items()}
    t["out"] = nc.dram_tensor("out_x", (B, S, D), F32, kind="ExternalOutput").ap()
    build(nc, t)
    r = run_bass_kernel_spmd(nc, [{f"in_{n}": a for n, a in arrays.items()}], core_ids=[0])
    return r.results[0]["out_x"]
```
